# Optimizing a Trainium2 kernel written in Bass

```python
import numpy as np
import jax
import jax.numpy as jnp

def _softmax(x, axis=-1):
    return jax.nn.softmax(x, axis=axis)

def _gelu(x):
    return jax.nn.gelu(x, approximate=True)

def _silu(x):
    return jax.nn.silu(x)

def _sigmoid(x):
    return jax.nn.sigmoid(x)

def _layernorm(x, axis=-1, eps=1e-05):
    m = jnp.mean(x, axis=axis, keepdims=True)
    v = jnp.var(x, axis=axis, keepdims=True)
    return (x - m) / jnp.sqrt(v + eps)

def _scatter_add(tgt, idx, src, axis=0):
    return tgt.at[idx].add(src)

def _segment_sum(src, seg, n):
    return jax.ops.segment_sum(src, seg, n)
kernel_name = 'mk_perceiver_d1_seqx_r2_d2e69c'

def setup_inputs(seed: int=0):
    np.random.seed(seed)
    _w = jnp.asarray

    def _rec_inputs():
        import jax
        import jax.numpy as jnp
        _rk = jax.random.key(seed)
        x = -0.0005207 + 1.001 * jax.random.normal(jax.random.fold_in(_rk, 1), (128, 32, 512), jnp.float32)
        _lenS = 32 - jax.random.randint(jax.random.fold_in(_rk, 7), (128,), 0, max(1, 32 // 4) + 1, jnp.int32)
        _lenS2 = 257 - jax.random.randint(jax.random.fold_in(_rk, 8), (128,), 0, max(1, 257 // 4) + 1, jnp.int32)
        _ctx_1024P = jax.random.normal(jax.random.fold_in(_rk, 11), (128, 16, 512), jnp.float32)
        _ctx_1024c = jax.random.dirichlet(jax.random.fold_in(_rk, 511), 0.3 * jnp.ones((16,), jnp.float32), (128, 257))
        _ctx_1024t = jnp.einsum('bsk,bkd->bsd', _ctx_1024c, _ctx_1024P)
        _ctx_1024t = _ctx_1024t * jax.lax.rsqrt(jnp.mean(jnp.square(_ctx_1024t)) + 1e-12) * 0.953939
        ctx_1024 = -1.39393e-06 + 0.999914 * (_ctx_1024t + 0.3 * jax.random.normal(jax.random.fold_in(_rk, 611), (128, 257, 512), jnp.float32))
        return (x, ctx_1024)
    x, ctx_1024 = _rec_inputs()

    def _L0_xattn_setup():
        import jax, jax.numpy as jnp
        import numpy as np
        DIM = 512
        NUM_HEADS = 16
        HEAD_DIM = DIM // NUM_HEADS
        SCALE = HEAD_DIM ** (-0.5)
        key0 = jax.random.key(seed)
        ks = jax.random.split(key0, 8)
        B, L, S = (2, 512, 1024)
        inp = {'query': jax.random.normal(ks[0], (B, L, DIM), dtype=jnp.float32), 'key': jax.random.normal(ks[1], (B, S, DIM), dtype=jnp.float32), 'value': jax.random.normal(ks[2], (B, S, DIM), dtype=jnp.float32), 'Wq': jax.random.normal(ks[3], (DIM, DIM), dtype=jnp.float32) * DIM ** (-0.5), 'Wk': jax.random.normal(ks[4], (DIM, DIM), dtype=jnp.float32) * DIM ** (-0.5), 'Wv': jax.random.normal(ks[5], (DIM, DIM), dtype=jnp.float32) * DIM ** (-0.5), 'Wo': jax.random.normal(ks[6], (DIM, DIM), dtype=jnp.float32) * DIM ** (-0.5), 'bo': jax.random.normal(ks[7], (DIM,), dtype=jnp.float32) * 0.02}
        return inp
    _L0_xattn_all = _L0_xattn_setup()
    _L0_xattn_in = {k: v for k, v in _L0_xattn_all.items() if k in ('Wq', 'Wk', 'Wv', 'Wo', 'bo')}
    del _L0_xattn_all

    def _L0_attn_setup():
        import jax, jax.numpy as jnp
        import numpy as np
        B, T, IN_DIM, EMB = (8, 1024, 512, 512)
        NEG_INF = -1e+30
        key = jax.random.key(seed)
        ks = jax.random.split(key, 7)
        s = 1.0 / np.sqrt(IN_DIM)
        return {'x': jax.random.normal(ks[0], (B, T, IN_DIM), dtype=jnp.float32), 'Wq': jax.random.normal(ks[1], (IN_DIM, EMB), dtype=jnp.float32) * s, 'bq': jax.random.normal(ks[2], (EMB,), dtype=jnp.float32) * 0.01, 'Wk': jax.random.normal(ks[3], (IN_DIM, EMB), dtype=jnp.float32) * s, 'bk': jax.random.normal(ks[4], (EMB,), dtype=jnp.float32) * 0.01, 'Wv': jax.random.normal(ks[5], (IN_DIM, EMB), dtype=jnp.float32) * s, 'bv': jax.random.normal(ks[6], (EMB,), dtype=jnp.float32) * 0.01}
    _L0_attn_all = _L0_attn_setup()
    _L0_attn_in = {k: v for k, v in _L0_attn_all.items() if k in ('Wq', 'bq', 'Wk', 'bk', 'Wv', 'bv')}
    del _L0_attn_all

    def _L0_ffn_setup():
        import jax, jax.numpy as jnp
        import numpy as np

        def _binarize(w):
            alpha = jax.lax.stop_gradient(jnp.mean(jnp.abs(w), axis=1, keepdims=True))
            bw = alpha * jnp.sign(w)
            return w + jax.lax.stop_gradient(bw - w)
        key = jax.random.key(seed)
        k1, k2, k3, k4, k5 = jax.random.split(key, 5)
        D, H = (512, 2048)
        x = jax.random.normal(k1, (64, 196, D), dtype=jnp.float32)
        w1 = jax.random.normal(k2, (H, D), dtype=jnp.float32) * 0.02
        b1 = jax.random.normal(k3, (H,), dtype=jnp.float32) * 0.02
        w2 = jax.random.normal(k4, (D, H), dtype=jnp.float32) * 0.02
        b2 = jax.random.normal(k5, (D,), dtype=jnp.float32) * 0.02
        return {'x': x, 'w1': w1, 'b1': b1, 'w2': w2, 'b2': b2}
    _L0_ffn_all = _L0_ffn_setup()
    _L0_ffn_in = {k: v for k, v in _L0_ffn_all.items() if k in ('w1', 'b1', 'w2', 'b2')}
    del _L0_ffn_all
    return {'x': x, 'ctx_1024': ctx_1024, 'L0_xattn_Wq': _L0_xattn_in['Wq'], 'L0_xattn_Wk': _L0_xattn_in['Wk'], 'L0_xattn_Wv': _L0_xattn_in['Wv'], 'L0_xattn_Wo': _L0_xattn_in['Wo'], 'L0_xattn_bo': _L0_xattn_in['bo'], 'L0_attn_Wq': _L0_attn_in['Wq'], 'L0_attn_bq': _L0_attn_in['bq'], 'L0_attn_Wk': _L0_attn_in['Wk'], 'L0_attn_bk': _L0_attn_in['bk'], 'L0_attn_Wv': _L0_attn_in['Wv'], 'L0_attn_bv': _L0_attn_in['bv'], 'L0_ffn_w1': _L0_ffn_in['w1'], 'L0_ffn_b1': _L0_ffn_in['b1'], 'L0_ffn_w2': _L0_ffn_in['w2'], 'L0_ffn_b2': _L0_ffn_in['b2']}

def reference(x, ctx_1024, L0_xattn_Wq, L0_xattn_Wk, L0_xattn_Wv, L0_xattn_Wo, L0_xattn_bo, L0_attn_Wq, L0_attn_bq, L0_attn_Wk, L0_attn_bk, L0_attn_Wv, L0_attn_bv, L0_ffn_w1, L0_ffn_b1, L0_ffn_w2, L0_ffn_b2):
    import jax
    import jax.numpy as jnp

    def _L0_xattn_ref(query, key, value, Wq, Wk, Wv, Wo, bo):
        import jax, jax.numpy as jnp
        import numpy as np
        DIM = 512
        NUM_HEADS = 16
        HEAD_DIM = DIM // NUM_HEADS
        SCALE = HEAD_DIM ** (-0.5)
        B, L, C = query.shape
        S = key.shape[1]
        H, D = (NUM_HEADS, HEAD_DIM)
        q = (query @ Wq).reshape(B, L, H, D).transpose(0, 2, 1, 3)
        k = (key @ Wk).reshape(B, S, H, D).transpose(0, 2, 1, 3)
        v = (value @ Wv).reshape(B, S, H, D).transpose(0, 2, 1, 3)
        attn = jnp.einsum('bhld,bhsd->bhls', q * SCALE, k)
        attn = jax.nn.softmax(attn, axis=-1)
        x = jnp.einsum('bhls,bhsd->bhld', attn, v)
        x = x.transpose(0, 2, 1, 3).reshape(B, L, C)
        return x @ Wo + bo

    def _L0_attn_ref(x, Wq, bq, Wk, bk, Wv, bv):
        import jax, jax.numpy as jnp
        import numpy as np
        B, T, IN_DIM, EMB = (8, 1024, 512, 512)
        NEG_INF = -1e+30
        q = x @ Wq + bq
        k = x @ Wk + bk
        v = x @ Wv + bv
        scale = jnp.asarray(EMB, x.dtype) ** 0.5
        scores = jnp.einsum('btd,bsd->bts', q, k) / scale
        Tq = scores.shape[-2]
        causal = jnp.tril(jnp.ones((Tq, Tq), dtype=bool))
        scores = jnp.where(causal, scores, jnp.asarray(NEG_INF, scores.dtype))
        m = jnp.max(scores, axis=(-2, -1), keepdims=True)
        e = jnp.exp(scores - m)
        w = e / jnp.sum(e, axis=(-2, -1), keepdims=True)
        return jnp.einsum('bts,bsd->btd', w, v)

    def _L0_ffn_ref(x, w1, b1, w2, b2):
        import jax, jax.numpy as jnp
        import numpy as np

        def _binarize(w):
            alpha = jax.lax.stop_gradient(jnp.mean(jnp.abs(w), axis=1, keepdims=True))
            bw = alpha * jnp.sign(w)
            return w + jax.lax.stop_gradient(bw - w)
        bw1 = _binarize(w1)
        h = jnp.einsum('bsd,hd->bsh', x, bw1) + b1
        h = jax.nn.gelu(h, approximate=False)
        bw2 = _binarize(w2)
        out = jnp.einsum('bsh,dh->bsd', h, bw2) + b2
        return out
    x = x + _L0_xattn_ref(_layernorm(x, axis=-1), ctx_1024, ctx_1024, L0_xattn_Wq, L0_xattn_Wk, L0_xattn_Wv, L0_xattn_Wo, L0_xattn_bo)
    x = x + _L0_attn_ref(_layernorm(x, axis=-1), L0_attn_Wq, L0_attn_bq, L0_attn_Wk, L0_attn_bk, L0_attn_Wv, L0_attn_bv)
    x = x + _L0_ffn_ref(_layernorm(x, axis=-1), L0_ffn_w1, L0_ffn_b1, L0_ffn_w2, L0_ffn_b2)
    return x

_drawn_inputs = setup_inputs


def setup_inputs(seed=0):
    import zlib

    import numpy as np

    out = dict(_drawn_inputs(seed))
    spreads = {}
    factors = {'L0_xattn_bo': 3.203,
     'L0_attn_Wq': 5.733,
     'L0_attn_bq': 8.0,
     'L0_attn_Wk': 5.657,
     'L0_attn_bk': 8.0,
     'L0_attn_Wv': 3.137,
     'L0_attn_bv': 41.255,
     'L0_ffn_b1': 7.811,
     'L0_ffn_b2': 3.314}
    for name, (base, spread) in spreads.items():
        noise = np.random.default_rng([zlib.crc32(name.encode()), seed]).standard_normal(out[name].shape)
        drawn = base * np.exp(spread * noise) if base else spread * noise
        out[name] = jnp.asarray(drawn.astype(out[name].dtype))
    for name, factor in factors.items():
        out[name] = (out[name] * factor).astype(out[name].dtype)
    return out
```

```python
from contextlib import ExitStack

import concourse.bass as bass
from concourse import mybir

P = 128
F32 = mybir.dt.float32
F16 = mybir.dt.float16
ALU = mybir.AluOpType
ACT = mybir.ActivationFunctionType
AX = mybir.AxisListType

W_SCALE = 64.0
W_UNSCALE = 1.0 / W_SCALE
EXP_SHIFT = 6.931471805599453
EPS = 1e-5
MASKED = -1e30
FEATURES = 512


def past(engine, semaphore, count):
    if isinstance(count, int) and count <= 0:
        return
    engine.wait_ge(semaphore, count)


def passes(hi_a, lo_a, hi_b, lo_b):
    return ((hi_a, hi_b), (hi_a, lo_b), (lo_a, hi_b))


def merge_statistics(nc, dve, n, stats, both, diff, mean, var_eps, stats_done, stats_count, merged, eps_done):
    dve.wait_ge(stats_done, stats_count)
    nc.vector.tensor_tensor(both, stats[:, :, 1:3], stats[:, :, 4:6], ALU.add).then_inc(merged, 1)
    nc.vector.tensor_tensor(diff, stats[:, :, 1], stats[:, :, 4], ALU.subtract).then_inc(merged, 1)
    dve.wait_ge(merged, n * 5 + 2)
    nc.vector.tensor_scalar(mean, both[:, :, 0], 0.5, None, ALU.mult).then_inc(merged, 1)
    nc.vector.tensor_scalar(var_eps, both[:, :, 1], 1.0 / FEATURES, EPS, ALU.mult, ALU.add).then_inc(merged, 1)
    nc.vector.tensor_tensor(diff, diff, diff, ALU.mult).then_inc(merged, 1)
    dve.wait_ge(merged, n * 5 + 5)
    nc.vector.scalar_tensor_tensor(out=var_eps, in0=diff, scalar=0.25, in1=var_eps, op0=ALU.mult,
                                   op1=ALU.add).then_inc(eps_done, 1)


def perceiver_block(nc, x, ctx_main, ctx_last, xWq, xWk, xWv, xWo, bo, sWq, bq, sWk, bk, sWv, bv,
                    w1, w1_t, b1, w2, w2_t, b2, v_last_rows, out):
    TOKENS, D = x.shape
    BATCH = ctx_main.shape[0]
    S = ctx_main.shape[3]
    L = TOKENS // BATCH
    KC = D // P
    DH = 32
    HPG = P // DH
    ST = S // P
    HID = w1.shape[0]
    NJ = HID // P
    X_SCALE = float(DH) ** -0.5
    S_SCALE = float(D) ** -0.5

    with ExitStack() as whole:
        def sem_in(stack, name):
            return stack.enter_context(nc.semaphore(name))

        def sb_in(stack, name, shape, dt=F32):
            return stack.enter_context(nc.sbuf_tensor(name, shape, dt))

        psum = whole.enter_context(nc.psum_tensor("psum", [P, 8, 512], F32))

        heads_hi = sb_in(whole, "heads_hi", [P, KC, TOKENS], F16)
        heads_lo = sb_in(whole, "heads_lo", [P, KC, TOKENS], F16)
        late = {}
        for name in ("xWo", "sWq", "sWk", "sWv"):
            late[name] = (sb_in(whole, name + "_hi", [P, KC, D], F16),
                          sb_in(whole, name + "_lo", [P, KC, D], F16))
        sign1 = sb_in(whole, "sign1", [P, KC, HID], F16)
        sign2 = sb_in(whole, "sign2", [P, NJ, D], F16)
        alpha1 = sb_in(whole, "alpha1", [P, NJ])
        alpha2_row = sb_in(whole, "alpha2_row", [P, D])
        ident = sb_in(whole, "ident", [P, P])

        with ExitStack() as early:
            xWk_hi = sb_in(early, "xWk_hi", [P, KC, D], F16)
            xWk_lo = sb_in(early, "xWk_lo", [P, KC, D], F16)
            xWv_hi = sb_in(early, "xWv_hi", [P, KC, D], F16)
            xWv_lo = sb_in(early, "xWv_lo", [P, KC, D], F16)
            k_last_hi = sb_in(early, "k_last_hi", [P, KC, BATCH], F16)
            k_last_lo = sb_in(early, "k_last_lo", [P, KC, BATCH], F16)
            with ExitStack() as first:
                xWq_hi = sb_in(first, "xWq_hi", [P, KC, D], F16)
                xWq_lo = sb_in(first, "xWq_lo", [P, KC, D], F16)
                prepare(nc, sem_in, sb_in, psum, dict(
                    xWq=(xWq, xWq_hi, xWq_lo), xWk=(xWk, xWk_hi, xWk_lo), xWv=(xWv, xWv_hi, xWv_lo),
                    xWo=(xWo, *late["xWo"]), sWq=(sWq, *late["sWq"]), sWk=(sWk, *late["sWk"]),
                    sWv=(sWv, *late["sWv"])), w1, w1_t, w2, w2_t, sign1, sign2, alpha1, alpha2_row,
                    ident, ctx_last, k_last_hi, k_last_lo, v_last_rows)
                cross_queries(nc, sem_in, sb_in, psum, x, xWq_hi, xWq_lo, ident, heads_hi, heads_lo)
            cross_attention(nc, sem_in, sb_in, psum, ctx_main, v_last_rows, xWk_hi, xWk_lo, xWv_hi,
                            xWv_lo, k_last_hi, k_last_lo, ident, heads_hi, heads_lo, X_SCALE)
        token_stages(nc, sem_in, sb_in, psum, x, bo, bq, bk, bv, b1, b2, late, sign1, sign2, alpha1,
                     alpha2_row, ident, heads_hi, heads_lo, S_SCALE, out)


def prepare(nc, sem_in, sb_in, psum, split, w1, w1_t, w2, w2_t, sign1, sign2, alpha1, alpha2_row,
            ident, ctx_last, k_last_hi, k_last_lo, v_last_rows):
    KC, NJ = sign1.shape[1], sign2.shape[1]
    D, HID = sign2.shape[2], sign1.shape[2]
    BATCH = k_last_hi.shape[2]
    RING = 3
    JP = NJ // KC

    def rows(w):
        return w.rearrange("(c p) n -> p c n", p=P)

    pieces = [("split", rows(split[n][0]), n) for n in ("xWk", "xWv", "xWq", "xWo", "sWq", "sWk", "sWv")]
    pieces.insert(0, ("last", ctx_last, None))
    for c in range(KC):
        pieces.append(("sum2", w2[c * P:(c + 1) * P, :], c))
    for c in range(KC):
        pieces.append(("sign1", w1_t[c * P:(c + 1) * P, :], c))
        pieces.append(("sign2", rows(w2_t[c * JP * P:(c + 1) * JP * P, :]), c))
        pieces.append(("sum1", rows(w1[c * JP * P:(c + 1) * JP * P, :]), c))

    with ExitStack() as ctx:
        raw = [sb_in(ctx, f"raw{r}", [P, KC * D]) for r in range(RING)]
        cl_hi = sb_in(ctx, "cl_hi", [P, KC, BATCH], F16)
        cl_lo = sb_in(ctx, "cl_lo", [P, KC, BATCH], F16)
        vl = sb_in(ctx, "vl", [P, D])
        sum1 = sb_in(ctx, "sum1", [P, NJ])
        sum2 = sb_in(ctx, "sum2", [P, KC])
        alpha2 = sb_in(ctx, "alpha2", [P, KC])
        ones = sb_in(ctx, "ones", [P, P])
        diag = sb_in(ctx, "diag", [P, D])

        landed = [sem_in(ctx, f"piece_landed{r}") for r in range(RING)]
        hi_done = sem_in(ctx, "prep_hi_done")
        dve_done = sem_in(ctx, "prep_dve_done")
        ones_set = sem_in(ctx, "ones_set")
        ident_set = sem_in(ctx, "ident_set")
        alpha_done = sem_in(ctx, "alpha_done")
        diag_done = sem_in(ctx, "diag_done")
        k_last_ps = sem_in(ctx, "k_last_ps")
        v_last_ps = sem_in(ctx, "v_last_ps")
        alpha2_ps = sem_in(ctx, "alpha2_ps")
        kl_hi_done = sem_in(ctx, "kl_hi_done")
        kl_lo_done = sem_in(ctx, "kl_lo_done")
        vl_done = sem_in(ctx, "vl_done")
        row_done = sem_in(ctx, "row_done")
        stored = sem_in(ctx, "v_last_stored")

        hi_after, dve_after, a, d = [], [], 0, 0
        for kind, _, _ in pieces:
            a += kind in ("last", "split", "sign1", "sign2")
            d += kind in ("last", "split", "sum1", "sum2")
            hi_after.append(a)
            dve_after.append(d)
        sums_done = dve_after[-1]
        KL, VL, ROW = 0, 1, 2
        k_bank = psum[:, KL, :].rearrange("p (c b) -> p c b", c=KC)

        block = ctx.enter_context(nc.Block())

        @block.sync
        def _(sp):
            for n, (_, src, _) in enumerate(pieces):
                if n >= RING:
                    sp.wait_ge(hi_done, hi_after[n - RING])
                    sp.wait_ge(dve_done, dve_after[n - RING])
                dst = raw[n % RING][:, :]
                if len(src.shape) == 3:
                    dst = raw[n % RING][:, 0:src.shape[1] * src.shape[2]].rearrange(
                        "p (c n) -> p c n", c=src.shape[1])
                sp.dma_start(dst, src).then_inc(landed[n % RING], 16)
            sp.wait_ge(vl_done, 1)
            sp.dma_start(v_last_rows, vl[:, :]).then_inc(stored, 16)
            sp.wait_ge(stored, 16)

        @block.gpsimd
        def _(pool):
            nc.gpsimd.memset(ones[:, :], 1.0).then_inc(ones_set, 1)
            pool.wait_ge(ones_set, 1)
            nc.gpsimd.affine_select(out=ident[:, :], in_=ones[:, :], compare_op=ALU.is_equal, fill=0.0,
                                    base=0, pattern=[[-1, P]], channel_multiplier=1).then_inc(ident_set, 1)

        @block.scalar
        def _(act):
            for n, (kind, _, c) in enumerate(pieces):
                src = raw[n % RING]
                if kind in ("sum1", "sum2"):
                    continue
                act.wait_ge(landed[n % RING], 16 * (n // RING + 1))
                if kind == "last":
                    nc.scalar.copy(cl_hi[:, :, :], src[:, 0:KC * BATCH].rearrange(
                        "p (c b) -> p c b", c=KC)).then_inc(hi_done, 1)
                elif kind == "split":
                    nc.scalar.mul(split[c][1].rearrange("p c n -> p (c n)"), src[:, :],
                                  W_SCALE).then_inc(hi_done, 1)
                elif kind == "sign1":
                    nc.scalar.activation(sign1[:, c, :], src[:, :], ACT.Sign).then_inc(hi_done, 1)
                elif kind == "sign2":
                    nc.scalar.activation(sign2[:, c * JP:(c + 1) * JP, :].rearrange("p c n -> p (c n)"),
                                         src[:, :], ACT.Sign).then_inc(hi_done, 1)
            act.wait_ge(k_last_ps, 1)
            nc.scalar.mul(k_last_hi[:, :, :], k_bank, W_UNSCALE).then_inc(kl_hi_done, 1)
            act.wait_ge(v_last_ps, 1)
            nc.scalar.mul(vl[:, :].rearrange("p (h g d) -> p g h d", h=4, g=KC),
                          psum[:, VL, :].rearrange("p (g h d) -> p g h d", h=4, g=KC),
                          W_UNSCALE).then_inc(vl_done, 1)
            act.wait_ge(alpha2_ps, 1)
            nc.scalar.copy(alpha2_row[:, :], psum[:, ROW, :]).then_inc(row_done, 1)

        @block.vector
        def _(dve):
            for n, (kind, _, c) in enumerate(pieces):
                src = raw[n % RING]
                if kind in ("sign1", "sign2"):
                    continue
                dve.wait_ge(landed[n % RING], 16 * (n // RING + 1))
                if kind in ("last", "split"):
                    dve.wait_ge(hi_done, hi_after[n])
                if kind == "last":
                    view = src[:, 0:KC * BATCH].rearrange("p (c b) -> p c b", c=KC)
                    nc.vector.tensor_tensor(cl_lo[:, :, :], view, cl_hi[:, :, :],
                                            ALU.subtract).then_inc(dve_done, 1)
                elif kind == "split":
                    nc.vector.scalar_tensor_tensor(
                        out=split[c][2].rearrange("p c n -> p (c n)"), in0=src[:, :], scalar=W_SCALE,
                        in1=split[c][1].rearrange("p c n -> p (c n)"), op0=ALU.mult,
                        op1=ALU.subtract).then_inc(dve_done, 1)
                elif kind == "sum2":
                    nc.vector.tensor_reduce(sum2[:, c:c + 1], src[:, :], AX.X, ALU.add,
                                            apply_absolute_value=True).then_inc(dve_done, 1)
                elif kind == "sum1":
                    nc.vector.tensor_reduce(
                        sum1[:, c * JP:(c + 1) * JP], src[:, :].rearrange("p (c n) -> p c n", c=JP),
                        AX.X, ALU.add, apply_absolute_value=True).then_inc(dve_done, 1)
            dve.wait_ge(dve_done, sums_done)
            nc.vector.tensor_scalar(alpha2[:, :], sum2[:, :], 1.0 / HID, None, ALU.mult).then_inc(alpha_done, 1)
            nc.vector.tensor_scalar(alpha1[:, :], sum1[:, :], 1.0 / D, None, ALU.mult).then_inc(alpha_done, 1)
            dve.wait_ge(alpha_done, 2)
            dve.wait_ge(ident_set, 1)
            for c in range(KC):
                nc.vector.tensor_scalar(diag[:, c * P:(c + 1) * P], ident[:, :], alpha2[:, c:c + 1], None,
                                        ALU.mult).then_inc(diag_done, 1)
            dve.wait_ge(kl_hi_done, 1)
            nc.vector.scalar_tensor_tensor(out=k_last_lo[:, :, :], in0=k_bank, scalar=W_UNSCALE,
                                           in1=k_last_hi[:, :, :], op0=ALU.mult,
                                           op1=ALU.subtract).then_inc(kl_lo_done, 1)

        @block.tensor
        def _(pe):
            pe.wait_ge(hi_done, 3)
            pe.wait_ge(dve_done, 3)
            for m in range(KC):
                cols = slice(m * P, (m + 1) * P)
                steps = [(a[:, k, cols], b[:, k, :]) for k in range(KC)
                         for a, b in passes(split["xWk"][1], split["xWk"][2], cl_hi, cl_lo)]
                for n, (a, b) in enumerate(steps):
                    mm = nc.tensor.matmul(k_bank[:, m, :], a, b, start=(n == 0), stop=(n == len(steps) - 1))
            mm.then_inc(k_last_ps, 1)
            steps = [(a[:, k, :], b[:, k, :]) for k in range(KC)
                     for a, b in passes(cl_hi, cl_lo, split["xWv"][1], split["xWv"][2])]
            for n, (a, b) in enumerate(steps):
                mm = nc.tensor.matmul(psum[:, VL, :], a, b, start=(n == 0), stop=(n == len(steps) - 1))
            mm.then_inc(v_last_ps, 1)
            pe.wait_ge(ones_set, 1)
            pe.wait_ge(diag_done, KC)
            nc.tensor.matmul(psum[:, ROW, :], ones[:, :], diag[:, :], start=True, stop=True).then_inc(alpha2_ps, 1)


def cross_queries(nc, sem_in, sb_in, psum, x, wq_hi, wq_lo, ident, heads_hi, heads_lo):
    KC, TOKENS = heads_hi.shape[1], heads_hi.shape[2]
    D = wq_hi.shape[2]
    TILES = 4
    GROUP = TILES * P
    NG = TOKENS // GROUP
    x_rows = x.rearrange("(t p) d -> p t d", p=P)

    with ExitStack() as ctx:
        xs = [sb_in(ctx, f"xs{u}", [P, TILES, D]) for u in range(2)]
        xT_hi = [sb_in(ctx, f"xT_hi{u}", [P, KC, GROUP], F16) for u in range(2)]
        xT_lo = [sb_in(ctx, f"xT_lo{u}", [P, KC, GROUP], F16) for u in range(2)]
        stats = sb_in(ctx, "stats", [P, TILES, 6])
        both = sb_in(ctx, "both", [P, TILES, 2])
        diff = sb_in(ctx, "diff", [P, TILES])
        mean = sb_in(ctx, "mean", [P, TILES])
        var_eps = sb_in(ctx, "var_eps", [P, TILES])
        half = sb_in(ctx, "half", [P, TILES])
        rstd = sb_in(ctx, "rstd", [P, TILES])

        x_landed = [sem_in(ctx, f"x_landed{u}") for u in range(2)]
        half_set = sem_in(ctx, "half_set")
        stats_done = sem_in(ctx, "stats_done")
        merged = sem_in(ctx, "merged")
        eps_done = sem_in(ctx, "eps_done")
        rstd_done = sem_in(ctx, "rstd_done")
        norm_done = sem_in(ctx, "norm_done")
        t_ps = sem_in(ctx, "t_ps")
        xT_hi_done = sem_in(ctx, "xT_hi_done")
        xT_lo_done = sem_in(ctx, "xT_lo_done")
        q_ps = sem_in(ctx, "q_ps")
        q_hi_done = sem_in(ctx, "q_hi_done")
        q_lo_done = sem_in(ctx, "q_lo_done")

        def t_bank(t):
            return psum[:, t, :].rearrange("p (c n) -> p c n", c=KC)

        block = ctx.enter_context(nc.Block())

        @block.sync
        def _(sp):
            def load(g, u):
                past(sp, t_ps, TILES * (g - 1))
                sp.dma_start(xs[u][:, :, :], x_rows[:, bass.ds(g * TILES, TILES), :]).then_inc(x_landed[u], 16)
            load(0, 0)
            load(1, 1)
            with sp.Fori(1, NG // 2) as i:
                for u in range(2):
                    load(i * 2 + u, u)

        @block.gpsimd
        def _(pool):
            nc.gpsimd.memset(half[:, :], -0.5).then_inc(half_set, 1)
            pool.wait_ge(half_set, 1)

            def power(g):
                pool.wait_ge(eps_done, g + 1)
                nc.gpsimd.tensor_tensor(rstd[:, :], var_eps[:, :], half[:, :], ALU.pow).then_inc(rstd_done, 1)
            with pool.Fori(0, NG) as g:
                power(g)

        @block.vector
        def _(dve):
            def normalise(i, u):
                g = i * 2 + u
                dve.wait_ge(x_landed[u], 16 * (i + 1))
                for t in range(TILES):
                    nc.vector.bn_stats(stats[:, t, :], xs[u][:, t, :]).then_inc(stats_done, 1)
                merge_statistics(nc, dve, g, stats, both[:, :, :], diff[:, :], mean[:, :], var_eps[:, :],
                                 stats_done, (g + 1) * TILES, merged, eps_done)
                dve.wait_ge(rstd_done, g + 1)
                for t in range(TILES):
                    nc.vector.tensor_scalar(xs[u][:, t, :], xs[u][:, t, :], mean[:, t:t + 1],
                                            rstd[:, t:t + 1], ALU.subtract, ALU.mult).then_inc(norm_done, 1)

            def low_xT(g, u):
                past(dve, q_ps, KC * (g - 1))
                for t in range(TILES):
                    dve.wait_ge(xT_hi_done, g * TILES + t + 1)
                    nc.vector.tensor_tensor(xT_lo[u][:, :, t * P:(t + 1) * P], t_bank(t),
                                            xT_hi[u][:, :, t * P:(t + 1) * P],
                                            ALU.subtract).then_inc(xT_lo_done, 1)

            def low_q(g):
                for m in range(KC):
                    dve.wait_ge(q_hi_done, g * KC + m + 1)
                    nc.vector.scalar_tensor_tensor(
                        out=heads_lo[:, m, bass.ds(g * GROUP, GROUP)], in0=psum[:, KC + m, :],
                        scalar=W_UNSCALE, in1=heads_hi[:, m, bass.ds(g * GROUP, GROUP)], op0=ALU.mult,
                        op1=ALU.subtract).then_inc(q_lo_done, 1)

            normalise(0, 0)
            low_xT(0, 0)
            normalise(0, 1)
            with dve.Fori(0, NG // 2 - 1) as i:
                for u in range(2):
                    low_xT(i * 2 + u + 1, 1 - u)
                    normalise(i + 1, u)
                    low_q(i * 2 + u)
            low_xT(NG - 1, 1)
            low_q(NG - 2)
            low_q(NG - 1)

        @block.scalar
        def _(act):
            def high_xT(g, u):
                past(act, q_ps, KC * (g - 1))
                for t in range(TILES):
                    act.wait_ge(t_ps, g * TILES + t + 1)
                    nc.scalar.copy(xT_hi[u][:, :, t * P:(t + 1) * P], t_bank(t)).then_inc(xT_hi_done, 1)

            def high_q(g):
                for m in range(KC):
                    act.wait_ge(q_ps, g * KC + m + 1)
                    nc.scalar.mul(heads_hi[:, m, bass.ds(g * GROUP, GROUP)], psum[:, KC + m, :],
                                  W_UNSCALE).then_inc(q_hi_done, 1)

            high_xT(0, 0)
            with act.Fori(0, NG // 2 - 1) as i:
                for u in range(2):
                    high_xT(i * 2 + u + 1, 1 - u)
                    high_q(i * 2 + u)
            high_xT(NG - 1, 1)
            high_q(NG - 2)
            high_q(NG - 1)

        @block.tensor
        def _(pe):
            def transposes(g, u):
                for t in range(TILES):
                    pe.wait_ge(norm_done, g * TILES + t + 1)
                    past(pe, xT_lo_done, (g - 1) * TILES + t + 1)
                    for c in range(KC):
                        mm = nc.tensor.transpose(t_bank(t)[:, c, :], xs[u][:, t, c * P:(c + 1) * P],
                                                 ident[:, :])
                    mm.then_inc(t_ps, 1)

            def queries(g, u):
                pe.wait_ge(xT_lo_done, (g + 1) * TILES)
                for m in range(KC):
                    past(pe, q_lo_done, (g - 1) * KC + m + 1)
                    steps = [(a[:, k, m * P:(m + 1) * P], b[:, k, :]) for k in range(KC)
                             for a, b in passes(wq_hi, wq_lo, xT_hi[u], xT_lo[u])]
                    for n, (a, b) in enumerate(steps):
                        mm = nc.tensor.matmul(psum[:, KC + m, :], a, b, start=(n == 0),
                                              stop=(n == len(steps) - 1))
                    mm.then_inc(q_ps, 1)

            transposes(0, 0)
            transposes(1, 1)
            queries(0, 0)
            with pe.Fori(1, NG // 2) as i:
                transposes(i * 2, 0)
                queries(i * 2 - 1, 1)
                transposes(i * 2 + 1, 1)
                queries(i * 2, 0)
            queries(NG - 1, 1)


def cross_attention(nc, sem_in, sb_in, psum, ctx_main, v_last_rows, wk_hi, wk_lo, wv_hi, wv_lo,
                    k_last_hi, k_last_lo, ident, heads_hi, heads_lo, SCALE):
    BATCH, _, KC, S = ctx_main.shape
    D = wk_hi.shape[2]
    L = heads_hi.shape[2] // BATCH
    HPG = P // 32
    ST = S // P
    KW = S + 8
    HALF = BATCH // 2

    with ExitStack() as ctx:
        raw = [sb_in(ctx, f"ctx_raw{u}", [P, KC, S]) for u in range(2)]
        c_hi = [sb_in(ctx, f"c_hi{u}", [P, KC, S], F16) for u in range(2)]
        c_lo = [sb_in(ctx, f"c_lo{u}", [P, KC, S], F16) for u in range(2)]
        kT_hi = sb_in(ctx, "kT_hi", [P, KC, KW], F16)
        kT_lo = sb_in(ctx, "kT_lo", [P, KC, KW], F16)
        v_hi = [sb_in(ctx, f"v_hi{u}", [P, ST, D], F16) for u in range(2)]
        v_lo = [sb_in(ctx, f"v_lo{u}", [P, ST, D], F16) for u in range(2)]
        bd_hi = sb_in(ctx, "bd_hi", [P, KC, HPG, L], F16)
        bd_lo = sb_in(ctx, "bd_lo", [P, KC, HPG, L], F16)
        e = sb_in(ctx, "e", [P, KC, S + 1])
        pT_hi = sb_in(ctx, "pT_hi", [P, ST, D], F16)
        pT_lo = sb_in(ctx, "pT_lo", [P, ST, D], F16)
        row_max = sb_in(ctx, "row_max", [P, KC])
        neg_max = sb_in(ctx, "neg_max", [P, KC])
        sums = sb_in(ctx, "sums", [P, KC])
        inv = sb_in(ctx, "inv", [P, KC])
        v_rep = [sb_in(ctx, f"v_rep{u}", [P, KC, 32]) for u in range(2)]
        last_part = sb_in(ctx, "last_part", [P, KC, 32])
        o_sum = sb_in(ctx, "o_sum", [P, KC, 32])
        o_norm = sb_in(ctx, "o_norm", [P, KC, 32])
        o_T = sb_in(ctx, "o_T", [P, KC, 32])

        ctx_landed = [sem_in(ctx, f"ctx_landed{u}") for u in range(2)]
        rep_landed = [sem_in(ctx, f"rep_landed{u}") for u in range(2)]
        names = ["bd_clear", "bd_ready", "k_col", "c_hi_done", "c_lo_done", "last_done", "k_ps", "v_ps",
                 "s_ps", "p_ps", "pv_ps", "k_hi_done", "k_lo_done", "v_hi_done", "v_lo_done", "max_done",
                 "neg_done", "e_done", "pT_hi_done", "pT_lo_done", "inv_done", "o_sum_done",
                 "o_norm_done", "o_T_done", "o_hi_done", "o_lo_done"]
        (bd_clear, bd_ready, k_col, c_hi_done, c_lo_done, last_done, k_ps, v_ps, s_ps, p_ps, pv_ps,
         k_hi_done, k_lo_done, v_hi_done, v_lo_done, max_done, neg_done, e_done, pT_hi_done, pT_lo_done,
         inv_done, o_sum_done, o_norm_done, o_T_done, o_hi_done, o_lo_done) = [sem_in(ctx, n) for n in names]

        def k_bank(h):
            return psum[:, 4 + h, :].rearrange("p (c s) -> p c s", c=2)

        def v_bank(t):
            return psum[:, 6 + t, :]

        scores = psum[:, 0:KC, 0:S + 1]
        out_bank = psum[:, 3, :].rearrange("p (g n) -> p g n", g=KC)

        block = ctx.enter_context(nc.Block())

        @block.sync
        def _(sp):
            def load(i, u):
                b = i * 2 + u
                past(sp, c_hi_done, b - 1)
                past(sp, c_lo_done, b - 1)
                sp.dma_start(raw[u][:, :, :], ctx_main[bass.ds(b, 1)].rearrange("o p c s -> (o p) c s")
                             ).then_inc(ctx_landed[u], 16)
                past(sp, last_done, b - 1)
                for h in range(HPG):
                    sp.dma_start(v_rep[u][h * L:(h + 1) * L, :, :].rearrange("p g d -> p (g d)"),
                                 v_last_rows[bass.ds(b, 1), h * P:(h + 1) * P].to_broadcast([L, P])
                                 ).then_inc(rep_landed[u], 16)
            load(0, 0)
            load(0, 1)
            with sp.Fori(1, HALF) as i:
                for u in range(2):
                    load(i, u)

        @block.gpsimd
        def _(pool):
            nc.gpsimd.memset(bd_hi[:, :, :, :], 0.0).then_inc(bd_clear, 1)
            nc.gpsimd.memset(bd_lo[:, :, :, :], 0.0).then_inc(bd_clear, 1)
            pool.wait_ge(bd_clear, 2)

            def spread(b):
                past(pool, s_ps, b)
                if not (isinstance(b, int) and b == 0):
                    pool.wait_ge(c_lo_done, b + 1)
                for h in range(HPG):
                    rows = slice(32 * h, 32 * h + 32)
                    nc.gpsimd.tensor_copy(bd_hi[rows, :, h, :],
                                          heads_hi[rows, :, bass.ds(b * L, L)]).then_inc(bd_ready, 1)
                    nc.gpsimd.tensor_copy(bd_lo[rows, :, h, :],
                                          heads_lo[rows, :, bass.ds(b * L, L)]).then_inc(bd_ready, 1)
                pool.wait_ge(bd_ready, 2 * HPG * (b + 1))
                nc.gpsimd.tensor_copy(kT_hi[:, :, S:S + 1], k_last_hi[:, :, bass.ds(b, 1)]).then_inc(k_col, 1)
                nc.gpsimd.tensor_copy(kT_lo[:, :, S:S + 1], k_last_lo[:, :, bass.ds(b, 1)]).then_inc(k_col, 1)

            def low_context(i, u):
                b = i * 2 + u
                pool.wait_ge(c_hi_done, b + 1)
                nc.gpsimd.tensor_tensor(c_lo[u][:, :, :], raw[u][:, :, :], c_hi[u][:, :, :],
                                        ALU.subtract).then_inc(c_lo_done, 1)

            def last_token(i, u):
                b = i * 2 + u
                pool.wait_ge(e_done, KC * (b + 1))
                pool.wait_ge(rep_landed[u], 16 * HPG * (i + 1))
                past(pool, o_sum_done, HPG * b)
                nc.gpsimd.tensor_tensor(last_part[:, :, :], v_rep[u][:, :, :],
                                        e[:, :, S:S + 1].to_broadcast([P, KC, 32]),
                                        ALU.mult).then_inc(last_done, 1)

            spread(0)
            low_context(0, 0)
            low_context(0, 1)
            with pool.Fori(0, HALF - 1) as i:
                for u in range(2):
                    b = i * 2 + u
                    spread(b + 1)
                    last_token(i, u)
                    low_context(i + 1, u)
            spread(BATCH - 1)
            last_token(HALF - 1, 0)
            last_token(HALF - 1, 1)

        @block.scalar
        def _(act):
            def high_context(i, u):
                b = i * 2 + u
                act.wait_ge(ctx_landed[u], 16 * (i + 1))
                past(act, v_ps, ST * (b - 1))
                nc.scalar.copy(c_hi[u][:, :, :], raw[u][:, :, :]).then_inc(c_hi_done, 1)

            def high_keys(b):
                for h in range(2):
                    act.wait_ge(k_ps, 2 * b + h + 1)
                    nc.scalar.mul(kT_hi[:, 2 * h:2 * h + 2, 0:S], k_bank(h), W_UNSCALE).then_inc(k_hi_done, 1)

            def high_values(b, u, t):
                act.wait_ge(v_ps, ST * b + t + 1)
                nc.scalar.mul(v_hi[u][:, t, :], v_bank(t), W_UNSCALE).then_inc(v_hi_done, 1)

            def exponentials(b):
                act.wait_ge(neg_done, b + 1)
                past(act, last_done, b)
                for g in range(KC):
                    nc.scalar.activation(e[:, g, :], psum[:, g, 0:S + 1], ACT.Exp, bias=neg_max[:, g:g + 1],
                                         scale=SCALE, accum_out=sums[:, g:g + 1]).then_inc(e_done, 1)

            def high_probs(b):
                for t in range(ST):
                    act.wait_ge(p_ps, ST * b + t + 1)
                    nc.scalar.copy(pT_hi[:, t, :], psum[:, t, :]).then_inc(pT_hi_done, 1)

            def high_output(b):
                act.wait_ge(o_T_done, b + 1)
                nc.scalar.copy(heads_hi[:, :, bass.ds(b * L, L)], o_T[:, :, :]).then_inc(o_hi_done, 1)

            def step(i, u, more=True, ahead=True):
                b = i * 2 + u
                exponentials(b)
                if ahead:
                    high_context(i + 1, u)
                if more:
                    high_keys(b + 1)
                high_probs(b)
                if more:
                    high_values(b + 1, 1 - u, 0)
                    high_values(b + 1, 1 - u, 1)
                high_output(b)

            high_context(0, 0)
            high_context(0, 1)
            high_keys(0)
            high_values(0, 0, 0)
            high_values(0, 0, 1)
            with act.Fori(0, HALF - 1) as i:
                for u in range(2):
                    step(i, u)
            step(HALF - 1, 0, ahead=False)
            step(HALF - 1, 1, more=False, ahead=False)

        @block.vector
        def _(dve):
            def maxima(b):
                dve.wait_ge(s_ps, b + 1)
                nc.vector.reduce_max(row_max[:, :], scores, AX.X).then_inc(max_done, 1)
                dve.wait_ge(max_done, b + 1)
                nc.vector.tensor_scalar(neg_max[:, :], row_max[:, :], -SCALE, EXP_SHIFT, ALU.mult,
                                        ALU.add).then_inc(neg_done, 1)

            def low_keys(b):
                for h in range(2):
                    dve.wait_ge(k_hi_done, 2 * b + h + 1)
                    nc.vector.scalar_tensor_tensor(
                        out=kT_lo[:, 2 * h:2 * h + 2, 0:S], in0=k_bank(h), scalar=W_UNSCALE,
                        in1=kT_hi[:, 2 * h:2 * h + 2, 0:S], op0=ALU.mult,
                        op1=ALU.subtract).then_inc(k_lo_done, 1)

            def low_values(b, u, t):
                dve.wait_ge(v_hi_done, ST * b + t + 1)
                nc.vector.scalar_tensor_tensor(
                    out=v_lo[u][:, t, :], in0=v_bank(t), scalar=W_UNSCALE, in1=v_hi[u][:, t, :],
                    op0=ALU.mult, op1=ALU.subtract).then_inc(v_lo_done, 1)

            def low_probs(b):
                for t in range(ST):
                    dve.wait_ge(pT_hi_done, ST * b + t + 1)
                    nc.vector.tensor_tensor(pT_lo[:, t, :], psum[:, t, :], pT_hi[:, t, :],
                                            ALU.subtract).then_inc(pT_lo_done, 1)

            def inverse(b):
                dve.wait_ge(e_done, KC * (b + 1))
                nc.vector.reciprocal(inv[:, :], sums[:, :]).then_inc(inv_done, 1)

            def gather_output(b):
                dve.wait_ge(pv_ps, b + 1)
                dve.wait_ge(last_done, b + 1)
                for h in range(HPG):
                    rows = slice(32 * h, 32 * h + 32)
                    nc.vector.tensor_tensor(o_sum[rows, :, :], out_bank[rows, :, 32 * h:32 * h + 32],
                                            last_part[rows, :, :], ALU.add).then_inc(o_sum_done, 1)

            def finish_output(b):
                dve.wait_ge(o_sum_done, HPG * (b + 1))
                dve.wait_ge(inv_done, b + 1)
                nc.vector.tensor_tensor(o_norm[:, :, :], o_sum[:, :, :],
                                        inv[:, :].unsqueeze(2).to_broadcast([P, KC, 32]),
                                        ALU.mult).then_inc(o_norm_done, 1)
                dve.wait_ge(o_norm_done, b + 1)
                past(dve, o_hi_done, b)
                past(dve, o_lo_done, b)
                nc.vector.transpose(o_T[:, :, :], o_norm[:, :, :]).then_inc(o_T_done, 1)

            def low_output(b):
                dve.wait_ge(o_hi_done, b + 1)
                nc.vector.tensor_tensor(heads_lo[:, :, bass.ds(b * L, L)], o_T[:, :, :],
                                        heads_hi[:, :, bass.ds(b * L, L)], ALU.subtract).then_inc(o_lo_done, 1)

            def step(b, u, more=True):
                maxima(b)
                if more:
                    low_keys(b + 1)
                inverse(b)
                low_probs(b)
                if more:
                    low_values(b + 1, 1 - u, 0)
                gather_output(b)
                if more:
                    low_values(b + 1, 1 - u, 1)
                finish_output(b)
                low_output(b)

            low_keys(0)
            low_values(0, 0, 0)
            low_values(0, 0, 1)
            with dve.Fori(0, HALF - 1) as i:
                for u in range(2):
                    step(i * 2 + u, u)
            step(BATCH - 2, 0)
            step(BATCH - 1, 1, more=False)

        @block.tensor
        def _(pe):
            def run(bank, steps, skip=False):
                for n, (a, b) in enumerate(steps):
                    mm = nc.tensor.matmul(bank, a, b, start=(n == 0), stop=(n == len(steps) - 1))
                return mm

            def keys(b, u):
                pe.wait_ge(c_lo_done, b + 1)
                for h in range(2):
                    past(pe, k_lo_done, 2 * (b - 1) + h + 1)
                    for m in (2 * h, 2 * h + 1):
                        mm = run(k_bank(h)[:, m % 2, :],
                                 [(w[:, k, m * P:(m + 1) * P], c[:, k, :]) for k in range(KC)
                                  for w, c in passes(wk_hi, wk_lo, c_hi[u], c_lo[u])])
                    mm.then_inc(k_ps, 1)

            def values(b, u, t):
                past(pe, v_lo_done, ST * (b - 1) + t + 1)
                run(v_bank(t), [(c[:, k, t * P:(t + 1) * P], w[:, k, :]) for k in range(KC)
                                for c, w in passes(c_hi[u], c_lo[u], wv_hi, wv_lo)]).then_inc(v_ps, 1)

            def score(b):
                pe.wait_ge(bd_ready, 2 * HPG * (b + 1))
                pe.wait_ge(k_col, 2 * (b + 1))
                pe.wait_ge(k_lo_done, 2 * (b + 1))
                past(pe, pT_lo_done, ST * b)
                past(pe, o_sum_done, HPG * b)
                for g in range(KC):
                    mm = run(psum[:, g, 0:S + 1],
                             [(q[:, g, :, :].rearrange("p h l -> p (h l)"), k[:, g, 0:S + 1])
                              for q, k in passes(bd_hi, bd_lo, kT_hi, kT_lo)])
                mm.then_inc(s_ps, 1)

            def probs(b):
                pe.wait_ge(e_done, KC * (b + 1))
                for t in range(ST):
                    for g in range(KC):
                        mm = nc.tensor.transpose(psum[:, t, g * P:(g + 1) * P], e[:, g, t * P:(t + 1) * P],
                                                 ident[:, :])
                    mm.then_inc(p_ps, 1)

            def outputs(b, u):
                pe.wait_ge(pT_lo_done, ST * (b + 1))
                pe.wait_ge(v_lo_done, ST * (b + 1))
                for g in range(KC):
                    cols = slice(g * P, (g + 1) * P)
                    mm = run(out_bank[:, g, :], [(p[:, t, cols], v[:, t, cols]) for t in range(ST)
                                                 for p, v in passes(pT_hi, pT_lo, v_hi[u], v_lo[u])])
                mm.then_inc(pv_ps, 1)

            def step(b, u, more=True):
                score(b)
                if more:
                    keys(b + 1, 1 - u)
                probs(b)
                if more:
                    values(b + 1, 1 - u, 0)
                outputs(b, u)
                if more:
                    values(b + 1, 1 - u, 1)

            keys(0, 0)
            values(0, 0, 0)
            values(0, 0, 1)
            with pe.Fori(0, HALF - 1) as i:
                for u in range(2):
                    step(i * 2 + u, u)
            step(BATCH - 2, 0)
            step(BATCH - 1, 1, more=False)


def token_stages(nc, sem_in, sb_in, psum, x, bo, bq, bk, bv, b1, b2, late, sign1, sign2, alpha1,
                 alpha2_row, ident, heads_hi, heads_lo, SCALE, out):
    TOKENS, D = x.shape
    KC, NJ = sign1.shape[1], sign2.shape[1]
    T = 2
    GROUP = T * P
    NG = TOKENS // GROUP
    BT = 32
    BPT = P // BT
    x_rows = x.rearrange("(t p) d -> p t d", p=P)
    out_rows = out.rearrange("(t p) d -> p t d", p=P)

    with ExitStack() as ctx:
        xb = sb_in(ctx, "xb", [P, T, D])
        res = [sb_in(ctx, f"res{u}", [P, T, D]) for u in range(2)]
        xn = sb_in(ctx, "xn", [P, T, D])
        at_hi = sb_in(ctx, "at_hi", [P, KC, GROUP], F16)
        at_lo = sb_in(ctx, "at_lo", [P, KC, GROUP], F16)
        x2T_hi = sb_in(ctx, "x2T_hi", [P, KC, GROUP], F16)
        x2T_lo = sb_in(ctx, "x2T_lo", [P, KC, GROUP], F16)
        x3T_hi = sb_in(ctx, "x3T_hi", [P, KC, GROUP], F16)
        x3T_lo = sb_in(ctx, "x3T_lo", [P, KC, GROUP], F16)
        qk = [sb_in(ctx, f"qk{r}", [P, 2, GROUP]) for r in range(2)]
        qk_hi = sb_in(ctx, "qk_hi", [P, 2 * KC, GROUP], F16)
        qk_lo = sb_in(ctx, "qk_lo", [P, 2 * KC, GROUP], F16)
        val = sb_in(ctx, "val", [P, D])
        val_hi = sb_in(ctx, "val_hi", [P, T, D], F16)
        val_lo = sb_in(ctx, "val_lo", [P, T, D], F16)
        act = [sb_in(ctx, f"gelu{r}", [P, GROUP]) for r in range(2)]
        act_hi = [sb_in(ctx, f"gelu_hi{r}", [P, GROUP], F16) for r in range(2)]
        act_lo = [sb_in(ctx, f"gelu_lo{r}", [P, GROUP], F16) for r in range(2)]
        res_out = [sb_in(ctx, f"res_out{t}", [P, D]) for t in range(T)]
        bo_row = sb_in(ctx, "bo_row", [P, D])
        bv_row = sb_in(ctx, "bv_row", [P, D])
        b2_row = sb_in(ctx, "b2_row", [P, D])
        bqk_col = sb_in(ctx, "bqk_col", [P, 2 * KC])
        b1_col = sb_in(ctx, "b1_col", [P, NJ])
        zeros = sb_in(ctx, "zeros", [P, BT])
        mask = sb_in(ctx, "mask", [P, BT])
        half = sb_in(ctx, "neg_half", [P, T])
        stats = sb_in(ctx, "stats_c", [P, T, 6])
        both = sb_in(ctx, "both_c", [P, T, 2])
        diff = sb_in(ctx, "diff_c", [P, T])
        mean = sb_in(ctx, "mean_c", [P, T])
        var_eps = sb_in(ctx, "var_eps_c", [P, T])
        rstd = sb_in(ctx, "rstd_c", [P, T])
        sc = sb_in(ctx, "sc", [P, T, BT])
        row = sb_in(ctx, "row", [P, T])
        spread = sb_in(ctx, "spread", [P, T, BT])
        across = sb_in(ctx, "across", [P, T, BT])
        neg_max = sb_in(ctx, "neg_max_c", [P, T])
        ex = sb_in(ctx, "ex", [P, T, BT])
        ex_sum = sb_in(ctx, "ex_sum", [P, T])
        ex_T = sb_in(ctx, "ex_T", [P, T, BT])
        total = sb_in(ctx, "total", [P, T])
        inv_total = sb_in(ctx, "inv_total", [P, T])
        w_hi = sb_in(ctx, "w_hi", [P, T, P], F16)
        w_lo = sb_in(ctx, "w_lo", [P, T, P], F16)

        names = ["consts_landed", "x_landed", "pool_const", "mask_done", "xb_done", "at_done", "b2_added",
                 "rstd2_done", "rstd3_done", "wo_ps", "t2_ps", "t3_ps", "qk_ps", "val_ps", "sc_ps", "pv_ps",
                 "h_ps", "f_ps", "x2T_hi_done", "x2T_lo_done", "x3T_hi_done", "x3T_lo_done", "qk_done",
                 "qk_hi_done", "qk_lo_done", "val_done", "val_hi_done", "val_lo_done", "x1_done", "x2_done",
                 "stats2_done", "stats3_done", "merged2", "merged3", "eps2_done", "eps3_done",
                 "norm2_done", "norm3_done", "sc_done", "chain", "neg_done", "ex_done", "inv_done",
                 "ex_T_done", "w_hi_done", "w_done", "gelu_done", "gelu_hi_done", "gelu_lo_done",
                 "scaled_done", "out_done", "out_stored0", "out_stored1"]
        s = {n: sem_in(ctx, n + "_c") for n in names}
        stored = [s["out_stored0"], s["out_stored1"]]
        CHAIN = 5

        def f_bank(t):
            return psum[:, t, :]

        def h_bank(j):
            return psum[:, 2 + j % 2, 0:GROUP]

        def g_bank(n):
            return psum[:, 4 + n, :]

        def chunks(bank, c):
            return bank.rearrange("p (c n) -> p c n", c=c)

        QK_BANK = (2, 3, 0, 1)
        sc_bank = g_bank(0)[:, 0:T * P].rearrange("p (t n) -> p t n", t=T)

        def rounds(engine, one):
            one(0, 0, front=True, ffn=False)
            one(1, 1, front=True, ffn=True)
            with engine.Fori(1, NG // 2 - 1) as i:
                one(i * 2, 0, front=True, ffn=True)
                one(i * 2 + 1, 1, front=True, ffn=True)
            one(NG - 2, 0, front=True, ffn=True)
            one(NG - 1, 1, front=True, ffn=True)
            one(NG, 0, front=False, ffn=True)

        block = ctx.enter_context(nc.Block())

        @block.sync
        def _(sp):
            for dst, src in ((bo_row, bo), (bv_row, bv), (b2_row, b2)):
                sp.dma_start(dst[:, :], src.to_broadcast([P, D])).then_inc(s["consts_landed"], 16)
            for dst, src in ((bqk_col[:, 0:KC], bq), (bqk_col[:, KC:], bk), (b1_col[:, :], b1)):
                sp.dma_start(dst, src).then_inc(s["consts_landed"], 16)

            def load(n):
                past(sp, s["x1_done"], T * n)
                sp.dma_start(xb[:, :, :], x_rows[:, bass.ds(n * T, T), :]).then_inc(s["x_landed"], 16)

            def one(n, u, front, ffn):
                if not (isinstance(n, int) and n >= NG - 1):
                    load(n + 1)
                if ffn:
                    for t in range(T):
                        sp.wait_ge(s["out_done"], (n - 1) * T + t + 1)
                        sp.dma_start(out_rows[:, bass.ds((n - 1) * T + t, 1), :],
                                     res_out[t][:, :].unsqueeze(1)).then_inc(stored[t], 16)
            load(0)
            rounds(sp, one)
            for t in range(T):
                sp.wait_ge(stored[t], 16 * NG)

        @block.gpsimd
        def _(pool):
            nc.gpsimd.memset(half[:, :], -0.5).then_inc(s["pool_const"], 1)
            nc.gpsimd.memset(zeros[:, :], 0.0).then_inc(s["pool_const"], 1)
            nc.gpsimd.memset(w_hi[:, :, :], 0.0).then_inc(s["pool_const"], 1)
            nc.gpsimd.memset(w_lo[:, :, :], 0.0).then_inc(s["pool_const"], 1)
            pool.wait_ge(s["pool_const"], 4)
            for b in range(BPT):
                rows = slice(BT * b, BT * b + BT)
                nc.gpsimd.affine_select(out=mask[rows, :], in_=zeros[rows, :], compare_op=ALU.is_ge,
                                        fill=MASKED, base=0, pattern=[[-1, BT]],
                                        channel_multiplier=1).then_inc(s["mask_done"], 1)
            pool.wait_ge(s["mask_done"], BPT)
            pool.wait_ge(s["consts_landed"], 16 * 6)

            def stage(n):
                past(pool, s["wo_ps"], T * n)
                for src, dst in ((heads_hi, at_hi), (heads_lo, at_lo)):
                    nc.gpsimd.tensor_copy(dst[:, :, :], src[:, :, bass.ds(n * GROUP, GROUP)]
                                          ).then_inc(s["at_done"], 1)
                pool.wait_ge(s["x_landed"], 16 * (n + 1))
                nc.gpsimd.tensor_tensor(xb[:, :, :], xb[:, :, :],
                                        bo_row[:, :].unsqueeze(1).to_broadcast([P, T, D]),
                                        ALU.add).then_inc(s["xb_done"], 1)

            def power(n, eps_done, rstd_done):
                pool.wait_ge(eps_done, n + 1)
                nc.gpsimd.tensor_tensor(rstd[:, :], var_eps[:, :], half[:, :], ALU.pow).then_inc(rstd_done, 1)

            def one(n, u, front, ffn):
                if not front:
                    return
                power(n, s["eps2_done"], s["rstd2_done"])
                if not (isinstance(n, int) and n == NG - 1):
                    stage(n + 1)
                power(n, s["eps3_done"], s["rstd3_done"])
                pool.wait_ge(s["norm3_done"], T * (n + 1))
                nc.gpsimd.tensor_tensor(res[u][:, :, :], res[u][:, :, :],
                                        b2_row[:, :].unsqueeze(1).to_broadcast([P, T, D]),
                                        ALU.add).then_inc(s["b2_added"], 1)
            stage(0)
            rounds(pool, one)

        @block.scalar
        def _(eng):
            def high_T(bank_ready, dst, done, n):
                for t in range(T):
                    eng.wait_ge(bank_ready, T * n + t + 1)
                    nc.scalar.copy(dst[:, :, t * P:(t + 1) * P], chunks(g_bank(t), KC)).then_inc(done, 1)

            def hidden(g, j):
                eng.wait_ge(s["h_ps"], NJ * g + j + 1)
                past(eng, s["gelu_lo_done"], NJ * g + j - 1)
                nc.scalar.activation(act[j % 2][:, :], h_bank(j), ACT.Gelu, bias=b1_col[:, j:j + 1],
                                     scale=alpha1[:, j:j + 1]).then_inc(s["gelu_done"], 1)
                eng.wait_ge(s["gelu_done"], NJ * g + j + 1)
                nc.scalar.copy(act_hi[j % 2][:, :], act[j % 2][:, :]).then_inc(s["gelu_hi_done"], 1)

            def one(n, u, front, ffn):
                g = n - 1

                def F(*js):
                    if ffn:
                        for j in js:
                            hidden(g, j)
                if ffn:
                    high_T(s["t3_ps"], x3T_hi, s["x3T_hi_done"], g)
                F(0, 1, 2, 3)
                if front:
                    high_T(s["t2_ps"], x2T_hi, s["x2T_hi_done"], n)
                F(4, 5)
                if front:
                    for r in range(4):
                        eng.wait_ge(s["qk_ps"], 4 * n + r + 1)
                        past(eng, s["qk_lo_done"], 4 * n + r - 1)
                        for c in range(2):
                            last = nc.scalar.activation(
                                qk[r % 2][:, c, :], chunks(g_bank(QK_BANK[r]), 2)[:, c, :], ACT.Identity,
                                bias=bqk_col[:, 2 * r + c:2 * r + c + 1], scale=W_UNSCALE)
                        last.then_inc(s["qk_done"], 1)
                F(6, 7, 8)
                if front:
                    eng.wait_ge(s["neg_done"], n + 1)
                    for t in range(T):
                        nc.scalar.activation(ex[:, t, :], sc[:, t, :], ACT.Exp, bias=neg_max[:, t:t + 1],
                                             accum_out=ex_sum[:, t:t + 1]).then_inc(s["ex_done"], 1)
                F(*range(9, NJ))
            eng.wait_ge(s["consts_landed"], 16 * 6)
            rounds(eng, one)

        @block.vector
        def _(dve):
            def low_T(hi_done, hi, lo, done, n):
                for t in range(T):
                    dve.wait_ge(hi_done, T * n + t + 1)
                    nc.vector.tensor_tensor(lo[:, :, t * P:(t + 1) * P], chunks(g_bank(t), KC),
                                            hi[:, :, t * P:(t + 1) * P], ALU.subtract).then_inc(done, 1)

            def hidden(g, j):
                dve.wait_ge(s["gelu_hi_done"], NJ * g + j + 1)
                nc.vector.tensor_tensor(act_lo[j % 2][:, :], act[j % 2][:, :], act_hi[j % 2][:, :],
                                        ALU.subtract).then_inc(s["gelu_lo_done"], 1)

            def statistics(n, u, k):
                for t in range(T):
                    dve.wait_ge(s["x1_done" if k == 2 else "x2_done"], T * n + t + 1)
                    nc.vector.bn_stats(stats[:, t, :], res[u][:, t, :]).then_inc(s[f"stats{k}_done"], 1)
                merge_statistics(nc, dve, n, stats, both[:, :, :], diff[:, :], mean[:, :], var_eps[:, :],
                                 s[f"stats{k}_done"], T * (n + 1), s[f"merged{k}"], s[f"eps{k}_done"])

            def normalise(n, u, k):
                dve.wait_ge(s[f"rstd{k}_done"], n + 1)
                if k == 2:
                    past(dve, s["t3_ps"], T * n)
                else:
                    dve.wait_ge(s["t2_ps"], T * (n + 1))
                for t in range(T):
                    nc.vector.tensor_scalar(xn[:, t, :], res[u][:, t, :], mean[:, t:t + 1],
                                            rstd[:, t:t + 1], ALU.subtract,
                                            ALU.mult).then_inc(s[f"norm{k}_done"], 1)

            def link(ins, value):
                ins.then_inc(s["chain"], 1)
                dve.wait_ge(s["chain"], value)

            def projections(n):
                for r in range(4):
                    cols = slice(2 * r, 2 * r + 2)
                    dve.wait_ge(s["qk_done"], 4 * n + r + 1)
                    nc.vector.tensor_copy(qk_hi[:, cols, :], qk[r % 2][:, :, :]).then_inc(s["qk_hi_done"], 1)
                    dve.wait_ge(s["qk_hi_done"], 4 * n + r + 1)
                    nc.vector.tensor_tensor(qk_lo[:, cols, :], qk[r % 2][:, :, :], qk_hi[:, cols, :],
                                            ALU.subtract).then_inc(s["qk_lo_done"], 1)
                for t in range(T):
                    dve.wait_ge(s["val_ps"], T * n + t + 1)
                    past(dve, s["val_lo_done"], T * n + t)
                    nc.vector.scalar_tensor_tensor(out=val[:, :], in0=g_bank(2 + t), scalar=W_UNSCALE,
                                                   in1=bv_row[:, :], op0=ALU.mult,
                                                   op1=ALU.add).then_inc(s["val_done"], 1)
                    dve.wait_ge(s["val_done"], T * n + t + 1)
                    nc.vector.tensor_copy(val_hi[:, t, :], val[:, :]).then_inc(s["val_hi_done"], 1)
                    dve.wait_ge(s["val_hi_done"], T * n + t + 1)
                    nc.vector.tensor_tensor(val_lo[:, t, :], val[:, :], val_hi[:, t, :],
                                            ALU.subtract).then_inc(s["val_lo_done"], 1)

            def maxima(n):
                dve.wait_ge(s["sc_ps"], n + 1)
                for b in range(BPT):
                    rows = slice(BT * b, BT * b + BT)
                    nc.vector.scalar_tensor_tensor(
                        out=sc[rows, :, :], in0=sc_bank[rows, :, BT * b:BT * b + BT], scalar=SCALE,
                        in1=mask[rows, :].unsqueeze(1).to_broadcast([BT, T, BT]), op0=ALU.mult,
                        op1=ALU.add).then_inc(s["sc_done"], 1)
                dve.wait_ge(s["sc_done"], BPT * (n + 1))
                link(nc.vector.reduce_max(row[:, :], sc[:, :, :], AX.X), CHAIN * n + 1)
                link(nc.vector.tensor_copy(spread[:, :, :], row[:, :].unsqueeze(2).to_broadcast([P, T, BT])),
                     CHAIN * n + 2)
                link(nc.vector.transpose(across[:, :, :], spread[:, :, :]), CHAIN * n + 3)
                link(nc.vector.reduce_max(row[:, :], across[:, :, :], AX.X), CHAIN * n + 4)
                nc.vector.tensor_scalar(neg_max[:, :], row[:, :], -1.0, EXP_SHIFT, ALU.mult,
                                        ALU.add).then_inc(s["neg_done"], 1)

            def weights(n):
                dve.wait_ge(s["ex_done"], T * (n + 1))
                nc.vector.transpose(ex_T[:, :, :], ex[:, :, :]).then_inc(s["ex_T_done"], 1)
                dve.wait_ge(s["ex_T_done"], n + 1)
                for b in range(BPT):
                    rows = slice(BT * b, BT * b + BT)
                    nc.vector.tensor_copy(w_hi[rows, :, rows], ex_T[rows, :, :]).then_inc(s["w_hi_done"], 1)
                for b in range(BPT):
                    rows = slice(BT * b, BT * b + BT)
                    dve.wait_ge(s["w_hi_done"], BPT * n + b + 1)
                    nc.vector.tensor_tensor(w_lo[rows, :, rows], ex_T[rows, :, :], w_hi[rows, :, rows],
                                            ALU.subtract).then_inc(s["w_done"], 1)

            def totals(n):
                link(nc.vector.tensor_copy(spread[:, :, :], ex_sum[:, :].unsqueeze(2).to_broadcast([P, T, BT])),
                     CHAIN * n + 5)
                nc.vector.transpose(across[:, :, :], spread[:, :, :]).then_inc(s["inv_done"], 1)
                dve.wait_ge(s["inv_done"], 3 * n + 1)
                nc.vector.reduce_sum(total[:, :], across[:, :, :], AX.X).then_inc(s["inv_done"], 1)
                dve.wait_ge(s["inv_done"], 3 * n + 2)
                nc.vector.reciprocal(inv_total[:, :], total[:, :]).then_inc(s["inv_done"], 1)

            def finish(g, u):
                dve.wait_ge(s["f_ps"], g + 1)
                for t in range(T):
                    past(dve, stored[t], 16 * g)
                    nc.vector.tensor_tensor(res_out[t][:, :], f_bank(t), alpha2_row[:, :],
                                            ALU.mult).then_inc(s["scaled_done"], 1)
                dve.wait_ge(s["b2_added"], g + 1)
                for t in range(T):
                    dve.wait_ge(s["scaled_done"], T * g + t + 1)
                    nc.vector.tensor_tensor(res_out[t][:, :], res_out[t][:, :], res[u][:, t, :],
                                            ALU.add).then_inc(s["out_done"], 1)

            def one(n, u, front, ffn):
                g = n - 1

                def F(*js):
                    if ffn:
                        for j in js:
                            hidden(g, j)
                if ffn:
                    low_T(s["x3T_hi_done"], x3T_hi, x3T_lo, s["x3T_lo_done"], g)
                if front:
                    dve.wait_ge(s["xb_done"], n + 1)
                    past(dve, s["out_done"], T * (n - 1))
                    for t in range(T):
                        dve.wait_ge(s["wo_ps"], T * n + t + 1)
                        nc.vector.scalar_tensor_tensor(out=res[u][:, t, :], in0=g_bank(2 + t),
                                                       scalar=W_UNSCALE, in1=xb[:, t, :], op0=ALU.mult,
                                                       op1=ALU.add).then_inc(s["x1_done"], 1)
                    statistics(n, u, 2)
                F(0, 1)
                if front:
                    normalise(n, u, 2)
                F(2, 3)
                if front:
                    low_T(s["x2T_hi_done"], x2T_hi, x2T_lo, s["x2T_lo_done"], n)
                F(4, 5)
                if front:
                    projections(n)
                F(6, 7)
                if front:
                    maxima(n)
                F(8, 9)
                if front:
                    weights(n)
                    totals(n)
                F(10, 11)
                if front:
                    dve.wait_ge(s["inv_done"], 3 * n + 3)
                    for t in range(T):
                        dve.wait_ge(s["pv_ps"], T * n + t + 1)
                        nc.vector.scalar_tensor_tensor(out=res[u][:, t, :], in0=g_bank(2 + t),
                                                       scalar=inv_total[:, t:t + 1], in1=res[u][:, t, :],
                                                       op0=ALU.mult, op1=ALU.add).then_inc(s["x2_done"], 1)
                    statistics(n, u, 3)
                F(12, 13)
                if front:
                    normalise(n, u, 3)
                F(14, 15)
                if ffn:
                    finish(g, 1 - u)
            dve.wait_ge(s["consts_landed"], 16 * 6)
            dve.wait_ge(s["mask_done"], BPT)
            rounds(dve, one)

        @block.tensor
        def _(pe):
            def run(bank, steps):
                for n, (a, b) in enumerate(steps):
                    mm = nc.tensor.matmul(bank, a, b, start=(n == 0), stop=(n == len(steps) - 1))
                return mm

            def transposes(n, norm_done, done):
                for t in range(T):
                    pe.wait_ge(norm_done, T * n + t + 1)
                    for c in range(KC):
                        mm = nc.tensor.transpose(chunks(g_bank(t), KC)[:, c, :], xn[:, t, c * P:(c + 1) * P],
                                                 ident[:, :])
                    mm.then_inc(done, 1)

            def layer1(g, j):
                past(pe, s["gelu_done"], NJ * g + j - 1)
                cols = slice(j * P, (j + 1) * P)
                run(h_bank(j), [(sign1[:, k, cols], x3[:, k, :]) for k in range(KC)
                                for x3 in (x3T_hi, x3T_lo)]).then_inc(s["h_ps"], 1)

            def layer2(g, j):
                pe.wait_ge(s["gelu_lo_done"], NJ * g + j + 1)
                if j == 0:
                    past(pe, s["scaled_done"], T * g)
                for t in range(T):
                    for n, a in enumerate((act_hi[j % 2], act_lo[j % 2])):
                        mm = nc.tensor.matmul(f_bank(t), a[:, t * P:(t + 1) * P], sign2[:, j, :],
                                              start=(j == 0 and n == 0), stop=(j == NJ - 1 and n == 1))
                if j == NJ - 1:
                    mm.then_inc(s["f_ps"], 1)

            def one(n, u, front, ffn):
                g = n - 1

                def F(*js):
                    if ffn:
                        for j in js:
                            layer1(g, j)
                            if j > 0:
                                layer2(g, j - 1)
                if ffn:
                    transposes(g, s["norm3_done"], s["t3_ps"])
                if front:
                    pe.wait_ge(s["at_done"], 2 * (n + 1))
                    for t in range(T):
                        rows = slice(t * P, (t + 1) * P)
                        run(g_bank(2 + t), [(a[:, k, rows], w[:, k, :]) for k in range(KC)
                                            for a, w in passes(at_hi, at_lo, *late["xWo"])]
                            ).then_inc(s["wo_ps"], 1)
                if ffn:
                    pe.wait_ge(s["x3T_lo_done"], T * (g + 1))
                F(0, 1, 2, 3)
                if front:
                    transposes(n, s["norm2_done"], s["t2_ps"])
                F(4, 5)
                if front:
                    pe.wait_ge(s["x2T_lo_done"], T * (n + 1))
                    for r in range(4):
                        hi, lo = late["sWq" if r < 2 else "sWk"]
                        for c in range(2):
                            m = 2 * (r % 2) + c
                            mm = run(chunks(g_bank(QK_BANK[r]), 2)[:, c, :],
                                     [(w[:, k, m * P:(m + 1) * P], xt[:, k, :]) for k in range(KC)
                                      for w, xt in passes(hi, lo, x2T_hi, x2T_lo)])
                        mm.then_inc(s["qk_ps"], 1)
                    for t in range(T):
                        pe.wait_ge(s["qk_done"], 4 * n + t + 1)
                        rows = slice(t * P, (t + 1) * P)
                        run(g_bank(2 + t), [(xt[:, k, rows], w[:, k, :]) for k in range(KC)
                                            for xt, w in passes(x2T_hi, x2T_lo, *late["sWv"])]
                            ).then_inc(s["val_ps"], 1)
                F(6, 7)
                if front:
                    pe.wait_ge(s["qk_lo_done"], 4 * (n + 1))
                    for t in range(T):
                        rows = slice(t * P, (t + 1) * P)
                        mm = run(sc_bank[:, t, :], [(q[:, m, rows], k[:, KC + m, rows]) for m in range(KC)
                                                    for q, k in passes(qk_hi, qk_lo, qk_hi, qk_lo)])
                    mm.then_inc(s["sc_ps"], 1)
                F(8, 9, 10, 11)
                if front:
                    pe.wait_ge(s["w_done"], BPT * (n + 1))
                    pe.wait_ge(s["val_lo_done"], T * (n + 1))
                    for t in range(T):
                        run(g_bank(2 + t), [(w[:, t, :], v[:, t, :]) for w, v in
                                            passes(w_hi, w_lo, val_hi, val_lo)]).then_inc(s["pv_ps"], 1)
                F(12, 13, 14, 15)
                if ffn:
                    layer2(g, NJ - 1)
            pe.wait_ge(s["pool_const"], 4)
            rounds(pe, one)


def kernel(x, ctx_1024, L0_xattn_Wq, L0_xattn_Wk, L0_xattn_Wv, L0_xattn_Wo, L0_xattn_bo, L0_attn_Wq,
           L0_attn_bq, L0_attn_Wk, L0_attn_bk, L0_attn_Wv, L0_attn_bv, L0_ffn_w1, L0_ffn_b1, L0_ffn_w2,
           L0_ffn_b2):
    import numpy as np
    import concourse.bacc as bacc
    from concourse.bass_utils import run_bass_kernel_spmd

    B, L, D = x.shape
    S = ctx_1024.shape[1] - 1
    ctx_t = np.asarray(ctx_1024).transpose(0, 2, 1).reshape(B, D // P, P, S + 1).transpose(0, 2, 1, 3)

    def columns(b):
        return np.asarray(b).reshape(-1, P).T

    arrays = dict(
        x=np.asarray(x).reshape(B * L, D), ctx_main=ctx_t[..., :S],
        ctx_last=ctx_t[..., S].transpose(1, 2, 0), xWq=L0_xattn_Wq, xWk=L0_xattn_Wk, xWv=L0_xattn_Wv,
        xWo=L0_xattn_Wo, bo=np.asarray(L0_xattn_bo)[None], sWq=L0_attn_Wq, bq=columns(L0_attn_bq),
        sWk=L0_attn_Wk, bk=columns(L0_attn_bk), sWv=L0_attn_Wv, bv=np.asarray(L0_attn_bv)[None],
        w1=L0_ffn_w1, w1_t=np.asarray(L0_ffn_w1).T, b1=columns(L0_ffn_b1), w2=L0_ffn_w2,
        w2_t=np.asarray(L0_ffn_w2).T, b2=np.asarray(L0_ffn_b2)[None])
    arrays = {name: np.ascontiguousarray(a) for name, a in arrays.items()}

    nc = bacc.Bacc("TRN2", target_bir_lowering=False, num_devices=1)
    args = {name: nc.dram_tensor(f"in_{name}", a.shape, mybir.dt.from_np(a.dtype), kind="ExternalInput").ap()
            for name, a in arrays.items()}
    v_last_rows = nc.dram_tensor("v_last_rows", (B, D), F32, kind="Internal").ap()
    out = nc.dram_tensor("out", (B * L, D), F32, kind="ExternalOutput").ap()
    perceiver_block(nc, v_last_rows=v_last_rows, out=out, **args)
    got = run_bass_kernel_spmd(nc, [{f"in_{name}": a for name, a in arrays.items()}], core_ids=[0])
    return got.results[0]["out"].reshape(B, L, D)
```

```python
from contextlib import ExitStack

import concourse.bass as bass
from concourse import mybir

P = 128
F32 = mybir.dt.float32
F16 = mybir.dt.float16
ALU = mybir.AluOpType
ACT = mybir.ActivationFunctionType
AX = mybir.AxisListType

W_SCALE = 64.0
W_UNSCALE = 1.0 / W_SCALE
EXP_SHIFT = 6.931471805599453
EPS = 1e-5
MASKED = -1e30
FEATURES = 512


def past(engine, semaphore, count):
    if isinstance(count, int) and count <= 0:
        return
    engine.wait_ge(semaphore, count)


def passes(hi_a, lo_a, hi_b, lo_b):
    return ((hi_a, hi_b), (hi_a, lo_b), (lo_a, hi_b))


def merge_statistics(nc, dve, n, stats, both, diff, mean, var_eps, stats_done, stats_count, merged, eps_done):
    dve.wait_ge(stats_done, stats_count)
    nc.vector.tensor_tensor(both, stats[:, :, 1:3], stats[:, :, 4:6], ALU.add).then_inc(merged, 1)
    nc.vector.tensor_tensor(diff, stats[:, :, 1], stats[:, :, 4], ALU.subtract).then_inc(merged, 1)
    dve.wait_ge(merged, n * 5 + 2)
    nc.vector.tensor_scalar(mean, both[:, :, 0], 0.5, None, ALU.mult).then_inc(merged, 1)
    nc.vector.tensor_scalar(var_eps, both[:, :, 1], 1.0 / FEATURES, EPS, ALU.mult, ALU.add).then_inc(merged, 1)
    nc.vector.tensor_tensor(diff, diff, diff, ALU.mult).then_inc(merged, 1)
    dve.wait_ge(merged, n * 5 + 5)
    nc.vector.scalar_tensor_tensor(out=var_eps, in0=diff, scalar=0.25, in1=var_eps, op0=ALU.mult,
                                   op1=ALU.add).then_inc(eps_done, 1)


def perceiver_block(nc, x, ctx_main, ctx_last, xWq, xWk, xWv, late_w, bo, bq, bk, bv, w1, w1_t, b1, w2_t, b2,
                    v_last_rows, out):
    TOKENS, D = x.shape
    BATCH = ctx_main.shape[0]
    DH = 32
    KC = D // P
    LATE = late_w.shape[0]

    with ExitStack() as whole:
        def sem_in(stack, name):
            return stack.enter_context(nc.semaphore(name))

        def sb_in(stack, name, shape, dt=F32):
            return stack.enter_context(nc.sbuf_tensor(name, shape, dt))

        psum = whole.enter_context(nc.psum_tensor("psum", [P, 8, 512], F32))

        heads_hi = sb_in(whole, "heads_hi", [P, KC, TOKENS], F16)
        heads_lo = sb_in(whole, "heads_lo", [P, KC, TOKENS], F16)
        late_hi = sb_in(whole, "late_hi", [P, LATE, KC, D], F16)
        late_lo = sb_in(whole, "late_lo", [P, LATE, KC, D], F16)
        ident = sb_in(whole, "ident", [P, P])
        ones = sb_in(whole, "ones", [P, P])

        with ExitStack() as early:
            xWk_hi = sb_in(early, "xWk_hi", [P, KC, D], F16)
            xWk_lo = sb_in(early, "xWk_lo", [P, KC, D], F16)
            xWv_hi = sb_in(early, "xWv_hi", [P, KC, D], F16)
            xWv_lo = sb_in(early, "xWv_lo", [P, KC, D], F16)
            k_last_hi = sb_in(early, "k_last_hi", [P, KC, BATCH], F16)
            k_last_lo = sb_in(early, "k_last_lo", [P, KC, BATCH], F16)
            cross_queries(nc, sem_in, sb_in, psum, x, xWq, xWk, xWv, ctx_last, ident, ones, heads_hi,
                          heads_lo, xWk_hi, xWk_lo, xWv_hi, xWv_lo, k_last_hi, k_last_lo, v_last_rows)
            cross_attention(nc, sem_in, sb_in, psum, ctx_main, v_last_rows, xWk_hi, xWk_lo, xWv_hi,
                            xWv_lo, k_last_hi, k_last_lo, ident, heads_hi, heads_lo, late_w, late_hi,
                            late_lo, float(DH) ** -0.5)
        token_stages(nc, sem_in, sb_in, psum, x, bo, bq, bk, bv, b1, b2, w1, w1_t, w2_t, late_hi, late_lo,
                     ident, ones, heads_hi, heads_lo, float(D) ** -0.5, out)


def cross_queries(nc, sem_in, sb_in, psum, x, xWq, xWk, xWv, ctx_last, ident, ones, heads_hi, heads_lo,
                  wk_hi, wk_lo, wv_hi, wv_lo, k_last_hi, k_last_lo, v_last_rows):
    KC, TOKENS = heads_hi.shape[1], heads_hi.shape[2]
    D = wk_hi.shape[2]
    BATCH = k_last_hi.shape[2]
    TILES = 4
    GROUP = TILES * P
    NG = TOKENS // GROUP
    x_rows = x.rearrange("(t p) d -> p t d", p=P)

    with ExitStack() as ctx:
        wq_hi = sb_in(ctx, "xWq_hi", [P, KC, D], F16)
        wq_lo = sb_in(ctx, "xWq_lo", [P, KC, D], F16)
        raw = [sb_in(ctx, f"raw_weight{r}", [P, KC, D]) for r in range(2)]
        raw_last = sb_in(ctx, "raw_last", [P, KC, BATCH])
        cl_hi = sb_in(ctx, "cl_hi", [P, KC, BATCH], F16)
        cl_lo = sb_in(ctx, "cl_lo", [P, KC, BATCH], F16)
        vl = sb_in(ctx, "vl", [P, D])
        xs = [sb_in(ctx, f"xs{u}", [P, TILES, D]) for u in range(2)]
        xT_hi = [sb_in(ctx, f"xT_hi{u}", [P, KC, GROUP], F16) for u in range(2)]
        xT_lo = [sb_in(ctx, f"xT_lo{u}", [P, KC, GROUP], F16) for u in range(2)]
        stats = sb_in(ctx, "stats", [P, TILES, 6])
        both = sb_in(ctx, "both", [P, TILES, 2])
        diff = sb_in(ctx, "diff", [P, TILES])
        mean = sb_in(ctx, "mean", [P, TILES])
        var_eps = sb_in(ctx, "var_eps", [P, TILES])
        half = sb_in(ctx, "half", [P, TILES])
        rstd = sb_in(ctx, "rstd", [P, TILES])

        x_landed = [sem_in(ctx, f"x_landed{u}") for u in range(2)]
        half_set = sem_in(ctx, "half_set")
        stats_done = sem_in(ctx, "stats_done")
        merged = sem_in(ctx, "merged")
        eps_done = sem_in(ctx, "eps_done")
        rstd_done = sem_in(ctx, "rstd_done")
        norm_done = sem_in(ctx, "norm_done")
        t_ps = sem_in(ctx, "t_ps")
        xT_hi_done = sem_in(ctx, "xT_hi_done")
        xT_lo_done = sem_in(ctx, "xT_lo_done")
        q_ps = sem_in(ctx, "q_ps")
        q_hi_done = sem_in(ctx, "q_hi_done")
        q_lo_done = sem_in(ctx, "q_lo_done")
        raw_landed = [sem_in(ctx, f"raw_landed{r}") for r in range(2)]
        last_landed = sem_in(ctx, "last_landed")
        w_hi_done = sem_in(ctx, "w_hi_done")
        w_lo_done = sem_in(ctx, "w_lo_done")
        cl_hi_done = sem_in(ctx, "cl_hi_done")
        cl_lo_done = sem_in(ctx, "cl_lo_done")
        ones_set = sem_in(ctx, "ones_set")
        ident_set = sem_in(ctx, "ident_set")
        k_last_ps = sem_in(ctx, "k_last_ps")
        v_last_ps = sem_in(ctx, "v_last_ps")
        kl_hi_done = sem_in(ctx, "kl_hi_done")
        kl_lo_done = sem_in(ctx, "kl_lo_done")
        vl_done = sem_in(ctx, "vl_done")
        v_stored = sem_in(ctx, "v_last_stored")
        WEIGHTS = ((xWq, wq_hi, wq_lo), (xWk, wk_hi, wk_lo), (xWv, wv_hi, wv_lo))
        k_last_bank = psum[:, 0, :].rearrange("p (c b) -> p c b", c=KC)
        v_last_bank = psum[:, 1, :]

        def t_bank(t):
            return psum[:, t, :].rearrange("p (c n) -> p c n", c=KC)

        block = ctx.enter_context(nc.Block())

        @block.sync
        def _(sp):
            def load(g, u):
                past(sp, t_ps, TILES * (g - 1))
                sp.dma_start(xs[u][:, :, :], x_rows[:, bass.ds(g * TILES, TILES), :]).then_inc(x_landed[u], 16)
            def load_weight(n):
                past(sp, w_lo_done, n - 1)
                sp.dma_start(raw[n % 2][:, :, :], WEIGHTS[n][0].rearrange("(c p) n -> p c n", p=P)
                             ).then_inc(raw_landed[n % 2], 16)
            load(0, 0)
            load_weight(0)
            load(1, 1)
            load_weight(1)
            sp.dma_start(raw_last[:, :, :], ctx_last).then_inc(last_landed, 16)
            load_weight(2)
            with sp.Fori(1, NG // 2) as i:
                for u in range(2):
                    load(i * 2 + u, u)
            sp.wait_ge(vl_done, 1)
            sp.dma_start(v_last_rows, vl[:, :]).then_inc(v_stored, 16)
            sp.wait_ge(v_stored, 16)

        @block.gpsimd
        def _(pool):
            nc.gpsimd.memset(ones[:, :], 1.0).then_inc(ones_set, 1)
            nc.gpsimd.memset(half[:, :], -0.5).then_inc(half_set, 1)
            pool.wait_ge(ones_set, 1)
            nc.gpsimd.affine_select(out=ident[:, :], in_=ones[:, :], compare_op=ALU.is_equal, fill=0.0,
                                    base=0, pattern=[[-1, P]], channel_multiplier=1).then_inc(ident_set, 1)
            pool.wait_ge(half_set, 1)

            def power(g):
                pool.wait_ge(eps_done, g + 1)
                nc.gpsimd.tensor_tensor(rstd[:, :], var_eps[:, :], half[:, :], ALU.pow).then_inc(rstd_done, 1)
            with pool.Fori(0, NG) as g:
                power(g)

        @block.vector
        def _(dve):
            def normalise(i, u):
                g = i * 2 + u
                dve.wait_ge(x_landed[u], 16 * (i + 1))
                for t in range(TILES):
                    nc.vector.bn_stats(stats[:, t, :], xs[u][:, t, :]).then_inc(stats_done, 1)
                merge_statistics(nc, dve, g, stats, both[:, :, :], diff[:, :], mean[:, :], var_eps[:, :],
                                 stats_done, (g + 1) * TILES, merged, eps_done)
                dve.wait_ge(rstd_done, g + 1)
                for t in range(TILES):
                    nc.vector.tensor_scalar(xs[u][:, t, :], xs[u][:, t, :], mean[:, t:t + 1],
                                            rstd[:, t:t + 1], ALU.subtract, ALU.mult).then_inc(norm_done, 1)

            def low_xT(g, u):
                past(dve, q_ps, KC * (g - 1))
                for t in range(TILES):
                    dve.wait_ge(xT_hi_done, g * TILES + t + 1)
                    nc.vector.tensor_tensor(xT_lo[u][:, :, t * P:(t + 1) * P], t_bank(t),
                                            xT_hi[u][:, :, t * P:(t + 1) * P],
                                            ALU.subtract).then_inc(xT_lo_done, 1)

            def low_q(g):
                for m in range(KC):
                    dve.wait_ge(q_hi_done, g * KC + m + 1)
                    nc.vector.scalar_tensor_tensor(
                        out=heads_lo[:, m, bass.ds(g * GROUP, GROUP)], in0=psum[:, KC + m, :],
                        scalar=W_UNSCALE, in1=heads_hi[:, m, bass.ds(g * GROUP, GROUP)], op0=ALU.mult,
                        op1=ALU.subtract).then_inc(q_lo_done, 1)

            def low_weight(n):
                dve.wait_ge(w_hi_done, n + 1)
                nc.vector.scalar_tensor_tensor(out=WEIGHTS[n][2][:, :, :], in0=raw[n % 2][:, :, :],
                                               scalar=W_SCALE, in1=WEIGHTS[n][1][:, :, :], op0=ALU.mult,
                                               op1=ALU.subtract).then_inc(w_lo_done, 1)
            normalise(0, 0)
            low_weight(0)
            low_xT(0, 0)
            normalise(0, 1)
            low_weight(1)
            dve.wait_ge(cl_hi_done, 1)
            nc.vector.tensor_tensor(cl_lo[:, :, :], raw_last[:, :, :], cl_hi[:, :, :],
                                    ALU.subtract).then_inc(cl_lo_done, 1)
            low_weight(2)
            with dve.Fori(0, NG // 2 - 1) as i:
                for u in range(2):
                    low_xT(i * 2 + u + 1, 1 - u)
                    normalise(i + 1, u)
                    low_q(i * 2 + u)
            low_xT(NG - 1, 1)
            low_q(NG - 2)
            low_q(NG - 1)
            dve.wait_ge(kl_hi_done, 1)
            nc.vector.scalar_tensor_tensor(out=k_last_lo[:, :, :], in0=k_last_bank, scalar=W_UNSCALE,
                                           in1=k_last_hi[:, :, :], op0=ALU.mult,
                                           op1=ALU.subtract).then_inc(kl_lo_done, 1)

        @block.scalar
        def _(act):
            def high_xT(g, u):
                past(act, q_ps, KC * (g - 1))
                for t in range(TILES):
                    act.wait_ge(t_ps, g * TILES + t + 1)
                    nc.scalar.copy(xT_hi[u][:, :, t * P:(t + 1) * P], t_bank(t)).then_inc(xT_hi_done, 1)

            def high_q(g):
                for m in range(KC):
                    act.wait_ge(q_ps, g * KC + m + 1)
                    nc.scalar.mul(heads_hi[:, m, bass.ds(g * GROUP, GROUP)], psum[:, KC + m, :],
                                  W_UNSCALE).then_inc(q_hi_done, 1)

            def high_weight(n):
                act.wait_ge(raw_landed[n % 2], 16 * (n // 2 + 1))
                nc.scalar.mul(WEIGHTS[n][1][:, :, :], raw[n % 2][:, :, :], W_SCALE).then_inc(w_hi_done, 1)
            high_weight(0)
            high_xT(0, 0)
            high_weight(1)
            act.wait_ge(last_landed, 16)
            nc.scalar.copy(cl_hi[:, :, :], raw_last[:, :, :]).then_inc(cl_hi_done, 1)
            high_weight(2)
            with act.Fori(0, NG // 2 - 1) as i:
                for u in range(2):
                    high_xT(i * 2 + u + 1, 1 - u)
                    high_q(i * 2 + u)
            high_xT(NG - 1, 1)
            high_q(NG - 2)
            act.wait_ge(k_last_ps, 1)
            nc.scalar.mul(k_last_hi[:, :, :], k_last_bank, W_UNSCALE).then_inc(kl_hi_done, 1)
            act.wait_ge(v_last_ps, 1)
            nc.scalar.mul(vl[:, :].rearrange("p (h g d) -> p g h d", h=4, g=KC),
                          v_last_bank.rearrange("p (g h d) -> p g h d", h=4, g=KC),
                          W_UNSCALE).then_inc(vl_done, 1)
            high_q(NG - 1)

        @block.tensor
        def _(pe):
            def transposes(g, u):
                for t in range(TILES):
                    pe.wait_ge(norm_done, g * TILES + t + 1)
                    past(pe, xT_lo_done, (g - 1) * TILES + t + 1)
                    for c in range(KC):
                        mm = nc.tensor.transpose(t_bank(t)[:, c, :], xs[u][:, t, c * P:(c + 1) * P],
                                                 ident[:, :])
                    mm.then_inc(t_ps, 1)

            def queries(g, u):
                pe.wait_ge(xT_lo_done, (g + 1) * TILES)
                for m in range(KC):
                    past(pe, q_lo_done, (g - 1) * KC + m + 1)
                    steps = [(a[:, k, m * P:(m + 1) * P], b[:, k, :]) for k in range(KC)
                             for a, b in passes(wq_hi, wq_lo, xT_hi[u], xT_lo[u])]
                    for n, (a, b) in enumerate(steps):
                        mm = nc.tensor.matmul(psum[:, KC + m, :], a, b, start=(n == 0),
                                              stop=(n == len(steps) - 1))
                    mm.then_inc(q_ps, 1)

            def last_tokens():
                pe.wait_ge(xT_lo_done, NG * TILES)
                pe.wait_ge(w_lo_done, 3)
                pe.wait_ge(cl_lo_done, 1)
                for m in range(KC):
                    cols = slice(m * P, (m + 1) * P)
                    steps = [(a[:, k, cols], b[:, k, :]) for k in range(KC)
                             for a, b in passes(wk_hi, wk_lo, cl_hi, cl_lo)]
                    for n, (a, b) in enumerate(steps):
                        mm = nc.tensor.matmul(k_last_bank[:, m, :], a, b, start=(n == 0),
                                              stop=(n == len(steps) - 1))
                mm.then_inc(k_last_ps, 1)
                steps = [(a[:, k, :], b[:, k, :]) for k in range(KC)
                         for a, b in passes(cl_hi, cl_lo, wv_hi, wv_lo)]
                for n, (a, b) in enumerate(steps):
                    mm = nc.tensor.matmul(v_last_bank, a, b, start=(n == 0), stop=(n == len(steps) - 1))
                mm.then_inc(v_last_ps, 1)

            pe.wait_ge(ident_set, 1)
            transposes(0, 0)
            transposes(1, 1)
            pe.wait_ge(w_lo_done, 1)
            queries(0, 0)
            with pe.Fori(1, NG // 2) as i:
                transposes(i * 2, 0)
                queries(i * 2 - 1, 1)
                transposes(i * 2 + 1, 1)
                queries(i * 2, 0)
            last_tokens()
            queries(NG - 1, 1)


def cross_attention(nc, sem_in, sb_in, psum, ctx_main, v_last_rows, wk_hi, wk_lo, wv_hi, wv_lo,
                    k_last_hi, k_last_lo, ident, heads_hi, heads_lo, late_w, late_hi, late_lo, SCALE):
    BATCH, _, KC, S = ctx_main.shape
    D = wk_hi.shape[2]
    L = heads_hi.shape[2] // BATCH
    HPG = P // 32
    ST = S // P
    KW = S + 8
    QUADS = BATCH // 4
    LATE = late_w.shape[0]

    with ExitStack() as ctx:
        raw = [sb_in(ctx, f"ctx_raw{u}", [P, KC, S]) for u in range(2)]
        c_hi = [sb_in(ctx, f"c_hi{r}", [P, KC, 2, S], F16) for r in range(2)]
        c_lo = [sb_in(ctx, f"c_lo{r}", [P, KC, 2, S], F16) for r in range(2)]
        kT_hi = [sb_in(ctx, f"kT_hi{r}", [P, KC, 2, KW], F16) for r in range(2)]
        kT_lo = [sb_in(ctx, f"kT_lo{r}", [P, KC, 2, KW], F16) for r in range(2)]
        late_raw = sb_in(ctx, "late_raw", [P, 1, KC * D])
        v_hi = [sb_in(ctx, f"v_hi{u}", [P, ST, D], F16) for u in range(2)]
        v_lo = [sb_in(ctx, f"v_lo{u}", [P, ST, D], F16) for u in range(2)]
        bd_hi = sb_in(ctx, "bd_hi", [P, KC, HPG, L], F16)
        bd_lo = sb_in(ctx, "bd_lo", [P, KC, HPG, L], F16)
        e = sb_in(ctx, "e", [P, KC, S + 1])
        pT_hi = sb_in(ctx, "pT_hi", [P, ST, D], F16)
        pT_lo = sb_in(ctx, "pT_lo", [P, ST, D], F16)
        row_max = sb_in(ctx, "row_max", [P, KC])
        neg_max = sb_in(ctx, "neg_max", [P, KC])
        sums = sb_in(ctx, "sums", [P, KC])
        inv = sb_in(ctx, "inv", [P, KC])
        v_rep = [sb_in(ctx, f"v_rep{u}", [P, KC, 32]) for u in range(2)]
        last_part = sb_in(ctx, "last_part", [P, KC, 32])
        o_sum = sb_in(ctx, "o_sum", [P, KC, 32])
        o_norm = sb_in(ctx, "o_norm", [P, KC, 32])
        o_T = sb_in(ctx, "o_T", [P, KC, 32])

        ctx_landed = [sem_in(ctx, f"ctx_landed{u}") for u in range(2)]
        rep_landed = [sem_in(ctx, f"rep_landed{u}") for u in range(2)]
        late_landed = sem_in(ctx, "late_landed")
        late_hi_done = sem_in(ctx, "late_hi_done")
        late_lo_done = sem_in(ctx, "late_lo_done")
        names = ["bd_clear", "bd_ready", "k_col", "c_hi_done", "c_lo_done", "last_done", "k_ps", "v_ps",
                 "s_ps", "p_ps", "pv_ps", "k_hi_done", "k_lo_done", "v_hi_done", "v_lo_done", "max_done",
                 "neg_done", "e_done", "pT_hi_done", "pT_lo_done", "inv_done", "o_sum_done",
                 "o_norm_done", "o_T_done", "o_hi_done", "o_lo_done"]
        (bd_clear, bd_ready, k_col, c_hi_done, c_lo_done, last_done, k_ps, v_ps, s_ps, p_ps, pv_ps,
         k_hi_done, k_lo_done, v_hi_done, v_lo_done, max_done, neg_done, e_done, pT_hi_done, pT_lo_done,
         inv_done, o_sum_done, o_norm_done, o_T_done, o_hi_done, o_lo_done) = [sem_in(ctx, n) for n in names]

        def k_bank(m):
            return psum[:, 4 + m % 2, :].rearrange("p (e s) -> p e s", e=2)

        def v_bank(t):
            return psum[:, 6 + t, :]

        scores = psum[:, 0:KC, 0:S + 1]
        out_bank = psum[:, 3, :].rearrange("p (g n) -> p g n", g=KC)

        block = ctx.enter_context(nc.Block())

        late_hi_w = late_hi.rearrange("p w c n -> p w (c n)")
        late_lo_w = late_lo.rearrange("p w c n -> p w (c n)")

        @block.sync
        def _(sp):
            def load_context(b, u):
                past(sp, c_hi_done, b - 1)
                past(sp, c_lo_done, b - 1)
                sp.dma_start(raw[u % 2][:, :, :], ctx_main[bass.ds(b, 1)].rearrange("o p c s -> (o p) c s")
                             ).then_inc(ctx_landed[u % 2], 16)

            def load_last(b, u):
                past(sp, last_done, b - 1)
                for h in range(HPG):
                    sp.dma_start(v_rep[u % 2][h * L:(h + 1) * L, :, :].rearrange("p g d -> p (g d)"),
                                 v_last_rows[bass.ds(b, 1), h * P:(h + 1) * P].to_broadcast([L, P])
                                 ).then_inc(rep_landed[u % 2], 16)

            def load_late(n):
                past(sp, late_lo_done, n)
                sp.dma_start(late_raw[:, :, :], late_w[bass.ds(n, 1)].rearrange("o p n -> p o n")
                             ).then_inc(late_landed, 16)

            def quad(i, late=False, end=False):
                if late:
                    load_late(i)
                for u in range(4):
                    b = i * 4 + u
                    if not end or b + 6 < BATCH:
                        load_context(b + 6, u)
                    if not end or b + 2 < BATCH:
                        load_last(b + 2, u)
            for b in range(6):
                load_context(b, b)
                if b < 2:
                    load_last(b, b)
            with sp.Fori(0, LATE) as i:
                quad(i, late=True)
            with sp.Fori(LATE, QUADS - 2) as i:
                quad(i)
            quad(QUADS - 2, end=True)
            quad(QUADS - 1, end=True)

        @block.gpsimd
        def _(pool):
            nc.gpsimd.memset(bd_hi[:, :, :, :], 0.0).then_inc(bd_clear, 1)
            nc.gpsimd.memset(bd_lo[:, :, :, :], 0.0).then_inc(bd_clear, 1)
            pool.wait_ge(bd_clear, 2)

            def spread(b, contexts):
                past(pool, s_ps, b)
                past(pool, c_lo_done, contexts)
                if isinstance(b, int) and b > 0:
                    pool.wait_ge(last_done, b - 1)
                    pool.wait_ge(k_col, 2 * (b // 2 + 1))
                for h in range(HPG):
                    rows = slice(32 * h, 32 * h + 32)
                    nc.gpsimd.tensor_copy(bd_hi[rows, :, h, :],
                                          heads_hi[rows, :, bass.ds(b * L, L)]).then_inc(bd_ready, 1)
                    nc.gpsimd.tensor_copy(bd_lo[rows, :, h, :],
                                          heads_lo[rows, :, bass.ds(b * L, L)]).then_inc(bd_ready, 1)

            def last_keys(b, r):
                past(pool, s_ps, b - 2)
                for k_last, kT in ((k_last_hi, kT_hi), (k_last_lo, kT_lo)):
                    nc.gpsimd.tensor_copy(kT[r][:, :, :, S], k_last[:, :, bass.ds(b, 2)]).then_inc(k_col, 1)

            def low_context(b, u):
                pool.wait_ge(c_hi_done, b + 1)
                nc.gpsimd.tensor_tensor(c_lo[u // 2][:, :, u % 2, :], raw[u % 2][:, :, :],
                                        c_hi[u // 2][:, :, u % 2, :], ALU.subtract).then_inc(c_lo_done, 1)

            def last_token(i, u, more=True):
                b = i * 4 + u
                pool.wait_ge(bd_ready, 2 * HPG * (b + 2 if more else b + 1))
                pool.wait_ge(e_done, KC * (b + 1))
                pool.wait_ge(rep_landed[u % 2], 16 * HPG * (i * 2 + u // 2 + 1))
                past(pool, o_sum_done, HPG * b)
                nc.gpsimd.tensor_tensor(last_part[:, :, :], v_rep[u % 2][:, :, :],
                                        e[:, :, S:S + 1].to_broadcast([P, KC, 32]),
                                        ALU.mult).then_inc(last_done, 1)

            def step(i, u, more=True, keys=True, ahead=True):
                b = i * 4 + u
                if more:
                    spread(b + 1, b + 4 if ahead else BATCH)
                last_token(i, u, more)
                if keys and u % 2 == 0:
                    last_keys(b + 2, 1 - u // 2)
                if ahead:
                    low_context(b + 4, u)

            spread(0, 0)
            pool.wait_ge(bd_ready, 2 * HPG)
            last_keys(0, 0)
            for b in range(4):
                low_context(b, b)
            with pool.Fori(0, QUADS - 1) as i:
                for u in range(4):
                    step(i, u)
            for u in range(4):
                step(QUADS - 1, u, more=u < 3, keys=u < 2, ahead=False)

        @block.scalar
        def _(act):
            def high_context(b, u, count):
                act.wait_ge(ctx_landed[u % 2], 16 * count)
                past(act, v_ps, ST * (b - 3))
                nc.scalar.copy(c_hi[u // 2][:, :, u % 2, :], raw[u % 2][:, :, :]).then_inc(c_hi_done, 1)

            def high_keys(pair, r, m):
                act.wait_ge(k_ps, KC * pair + m + 1)
                nc.scalar.mul(kT_hi[r][:, m, :, 0:S], k_bank(m), W_UNSCALE).then_inc(k_hi_done, 1)

            def high_values(b, u, t):
                act.wait_ge(v_ps, ST * b + t + 1)
                nc.scalar.mul(v_hi[u][:, t, :], v_bank(t), W_UNSCALE).then_inc(v_hi_done, 1)

            def exponentials(b):
                act.wait_ge(neg_done, b + 1)
                past(act, last_done, b)
                for g in range(KC):
                    nc.scalar.activation(e[:, g, :], psum[:, g, 0:S + 1], ACT.Exp, bias=neg_max[:, g:g + 1],
                                         scale=SCALE, accum_out=sums[:, g:g + 1]).then_inc(e_done, 1)

            def high_probs(b):
                for t in range(ST):
                    act.wait_ge(p_ps, ST * b + t + 1)
                    nc.scalar.copy(pT_hi[:, t, :], psum[:, t, :]).then_inc(pT_hi_done, 1)

            def high_output(b):
                act.wait_ge(o_T_done, b + 1)
                nc.scalar.copy(heads_hi[:, :, bass.ds(b * L, L)], o_T[:, :, :]).then_inc(o_hi_done, 1)

            def high_late(n):
                act.wait_ge(late_landed, 16 * (n + 1))
                nc.scalar.mul(late_hi_w[:, bass.ds(n, 1), :], late_raw[:, :, :], W_SCALE).then_inc(late_hi_done, 1)

            def step(i, u, more=True, keys=True, ahead=True):
                b = i * 4 + u
                exponentials(b)
                if keys:
                    for m in (2 * (u % 2), 2 * (u % 2) + 1):
                        high_keys(i * 2 + u // 2 + 1, 1 - u // 2, m)
                high_probs(b)
                if ahead:
                    high_context(b + 4, u, (i + 1) * 2 + u // 2 + 1)
                if more:
                    high_values(b + 1, (u + 1) % 2, 0)
                    high_values(b + 1, (u + 1) % 2, 1)
                high_output(b)

            for b in range(4):
                high_context(b, b, b // 2 + 1)
                if b == 1:
                    for m in range(KC):
                        high_keys(0, 0, m)
            for t in range(ST):
                high_values(0, 0, t)
            with act.Fori(0, LATE) as i:
                for u in range(4):
                    step(i, u)
                high_late(i)
            with act.Fori(LATE, QUADS - 1) as i:
                for u in range(4):
                    step(i, u)
            for u in range(4):
                step(QUADS - 1, u, more=u < 3, keys=u < 2, ahead=False)

        @block.vector
        def _(dve):
            def maxima(b):
                dve.wait_ge(s_ps, b + 1)
                nc.vector.reduce_max(row_max[:, :], scores, AX.X).then_inc(max_done, 1)
                dve.wait_ge(max_done, b + 1)
                nc.vector.tensor_scalar(neg_max[:, :], row_max[:, :], -SCALE, EXP_SHIFT, ALU.mult,
                                        ALU.add).then_inc(neg_done, 1)

            def low_keys(pair, r, m):
                dve.wait_ge(k_hi_done, KC * pair + m + 1)
                nc.vector.scalar_tensor_tensor(
                    out=kT_lo[r][:, m, :, 0:S], in0=k_bank(m), scalar=W_UNSCALE,
                    in1=kT_hi[r][:, m, :, 0:S], op0=ALU.mult, op1=ALU.subtract).then_inc(k_lo_done, 1)

            def low_values(b, u, t):
                dve.wait_ge(v_hi_done, ST * b + t + 1)
                nc.vector.scalar_tensor_tensor(
                    out=v_lo[u][:, t, :], in0=v_bank(t), scalar=W_UNSCALE, in1=v_hi[u][:, t, :],
                    op0=ALU.mult, op1=ALU.subtract).then_inc(v_lo_done, 1)

            def low_probs(b):
                for t in range(ST):
                    dve.wait_ge(pT_hi_done, ST * b + t + 1)
                    nc.vector.tensor_tensor(pT_lo[:, t, :], psum[:, t, :], pT_hi[:, t, :],
                                            ALU.subtract).then_inc(pT_lo_done, 1)

            def inverse(b):
                dve.wait_ge(e_done, KC * (b + 1))
                nc.vector.reciprocal(inv[:, :], sums[:, :]).then_inc(inv_done, 1)

            def gather_output(b):
                dve.wait_ge(pv_ps, b + 1)
                dve.wait_ge(last_done, b + 1)
                for h in range(HPG):
                    rows = slice(32 * h, 32 * h + 32)
                    nc.vector.tensor_tensor(o_sum[rows, :, :], out_bank[rows, :, 32 * h:32 * h + 32],
                                            last_part[rows, :, :], ALU.add).then_inc(o_sum_done, 1)

            def finish_output(b):
                dve.wait_ge(o_sum_done, HPG * (b + 1))
                dve.wait_ge(inv_done, b + 1)
                nc.vector.tensor_tensor(o_norm[:, :, :], o_sum[:, :, :],
                                        inv[:, :].unsqueeze(2).to_broadcast([P, KC, 32]),
                                        ALU.mult).then_inc(o_norm_done, 1)
                dve.wait_ge(o_norm_done, b + 1)
                past(dve, o_hi_done, b)
                past(dve, o_lo_done, b)
                nc.vector.transpose(o_T[:, :, :], o_norm[:, :, :]).then_inc(o_T_done, 1)

            def low_output(b):
                dve.wait_ge(o_hi_done, b + 1)
                nc.vector.tensor_tensor(heads_lo[:, :, bass.ds(b * L, L)], o_T[:, :, :],
                                        heads_hi[:, :, bass.ds(b * L, L)], ALU.subtract).then_inc(o_lo_done, 1)

            def low_late(n):
                dve.wait_ge(late_hi_done, n + 1)
                nc.vector.scalar_tensor_tensor(
                    out=late_lo_w[:, bass.ds(n, 1), :], in0=late_raw[:, :, :], scalar=W_SCALE,
                    in1=late_hi_w[:, bass.ds(n, 1), :], op0=ALU.mult,
                    op1=ALU.subtract).then_inc(late_lo_done, 1)

            def step(i, u, more=True, keys=True):
                b = i * 4 + u
                maxima(b)
                if keys:
                    for m in (2 * (u % 2), 2 * (u % 2) + 1):
                        low_keys(i * 2 + u // 2 + 1, 1 - u // 2, m)
                low_probs(b)
                inverse(b)
                if more:
                    low_values(b + 1, (u + 1) % 2, 0)
                gather_output(b)
                finish_output(b)
                if more:
                    low_values(b + 1, (u + 1) % 2, 1)
                low_output(b)

            for m in range(KC):
                low_keys(0, 0, m)
            for t in range(ST):
                low_values(0, 0, t)
            with dve.Fori(0, LATE) as i:
                for u in range(4):
                    step(i, u)
                low_late(i)
            with dve.Fori(LATE, QUADS - 1) as i:
                for u in range(4):
                    step(i, u)
            for u in range(4):
                step(QUADS - 1, u, more=u < 3, keys=u < 2)

        @block.tensor
        def _(pe):
            def run(bank, steps):
                for n, (a, b) in enumerate(steps):
                    mm = nc.tensor.matmul(bank, a, b, start=(n == 0), stop=(n == len(steps) - 1))
                return mm

            def keys(pair, r, m):
                pe.wait_ge(c_lo_done, 2 * pair + 2)
                past(pe, k_lo_done, KC * pair + m - 1)
                run(k_bank(m), [(w[:, k, m * P:(m + 1) * P], c[:, k, :, :]) for k in range(KC)
                                for w, c in passes(wk_hi, wk_lo, c_hi[r], c_lo[r])]).then_inc(k_ps, 1)

            def values(b, u, t):
                past(pe, v_lo_done, ST * (b - 1) + t + 1)
                rows = slice(t * P, (t + 1) * P)
                run(v_bank(t), [(c[:, k, u % 2, rows], w[:, k, :]) for k in range(KC)
                                for c, w in passes(c_hi[u // 2], c_lo[u // 2], wv_hi, wv_lo)]
                    ).then_inc(v_ps, 1)

            def score(i, u):
                b = i * 4 + u
                pe.wait_ge(bd_ready, 2 * HPG * (b + 1))
                pe.wait_ge(k_col, 2 * (i * 2 + u // 2 + 1))
                pe.wait_ge(k_lo_done, KC * (i * 2 + u // 2 + 1))
                past(pe, pT_lo_done, ST * b)
                past(pe, o_sum_done, HPG * b)
                for g in range(KC):
                    mm = run(psum[:, g, 0:S + 1],
                             [(q[:, g, :, :].rearrange("p h l -> p (h l)"), k[u // 2][:, g, u % 2, 0:S + 1])
                              for q, k in passes(bd_hi, bd_lo, kT_hi, kT_lo)])
                mm.then_inc(s_ps, 1)

            def probs(b):
                pe.wait_ge(e_done, KC * (b + 1))
                for t in range(ST):
                    for g in range(KC):
                        mm = nc.tensor.transpose(psum[:, t, g * P:(g + 1) * P], e[:, g, t * P:(t + 1) * P],
                                                 ident[:, :])
                    mm.then_inc(p_ps, 1)

            def outputs(b, u):
                pe.wait_ge(pT_lo_done, ST * (b + 1))
                pe.wait_ge(v_lo_done, ST * (b + 1))
                for g in range(KC):
                    cols = slice(g * P, (g + 1) * P)
                    mm = run(out_bank[:, g, :], [(p[:, t, cols], v[:, t, cols]) for t in range(ST)
                                                 for p, v in passes(pT_hi, pT_lo, v_hi[u % 2], v_lo[u % 2])])
                mm.then_inc(pv_ps, 1)

            def step(i, u, more=True, key=True):
                b = i * 4 + u
                score(i, u)
                if key:
                    for m in (2 * (u % 2), 2 * (u % 2) + 1):
                        keys(i * 2 + u // 2 + 1, 1 - u // 2, m)
                probs(b)
                if more:
                    values(b + 1, (u + 1) % 4, 0)
                outputs(b, u)
                if more:
                    values(b + 1, (u + 1) % 4, 1)

            for m in range(KC):
                keys(0, 0, m)
            values(0, 0, 0)
            values(0, 0, 1)
            with pe.Fori(0, QUADS - 1) as i:
                for u in range(4):
                    step(i, u)
            for u in range(4):
                step(QUADS - 1, u, more=u < 3, key=u < 2)


def token_stages(nc, sem_in, sb_in, psum, x, bo, bq, bk, bv, b1, b2, w1, w1_t, w2_t, late_hi, late_lo,
                 ident, ones, heads_hi, heads_lo, SCALE, out):
    TOKENS, D = x.shape
    HID = w1_t.shape[1]
    KC, NJ = D // P, HID // P
    T = 2
    GROUP = T * P
    NG = TOKENS // GROUP
    BT = 32
    BPT = P // BT
    RING = 2
    PIECE = 2 * D
    x_rows = x.rearrange("(t p) d -> p t d", p=P)
    out_rows = out.rearrange("(t p) d -> p t d", p=P)

    with ExitStack() as ctx:
        sign1 = sb_in(ctx, "sign1", [P, KC, HID], F16)
        sign2 = sb_in(ctx, "sign2", [P, NJ, D], F16)
        sum1 = sb_in(ctx, "sum1", [P, NJ])
        alpha1 = sb_in(ctx, "alpha1", [P, NJ])
        alpha2_row = sb_in(ctx, "alpha2_row", [P, D])
        raw = [sb_in(ctx, f"ffn_raw{r}", [P, 2 * D]) for r in range(RING)]
        xb = sb_in(ctx, "xb", [P, T, D])
        res = [sb_in(ctx, f"res{u}", [P, T, D]) for u in range(2)]
        xn = sb_in(ctx, "xn", [P, T, D])
        at_hi = sb_in(ctx, "at_hi", [P, KC, GROUP], F16)
        at_lo = sb_in(ctx, "at_lo", [P, KC, GROUP], F16)
        x2T_hi = sb_in(ctx, "x2T_hi", [P, KC, GROUP], F16)
        x2T_lo = sb_in(ctx, "x2T_lo", [P, KC, GROUP], F16)
        x3T_hi = sb_in(ctx, "x3T_hi", [P, KC, GROUP], F16)
        x3T_lo = sb_in(ctx, "x3T_lo", [P, KC, GROUP], F16)
        qk = [sb_in(ctx, f"qk{r}", [P, 2, GROUP]) for r in range(2)]
        qk_hi = sb_in(ctx, "qk_hi", [P, 2 * KC, GROUP], F16)
        qk_lo = sb_in(ctx, "qk_lo", [P, 2 * KC, GROUP], F16)
        val = sb_in(ctx, "val", [P, D])
        val_hi = sb_in(ctx, "val_hi", [P, T, D], F16)
        val_lo = sb_in(ctx, "val_lo", [P, T, D], F16)
        act = [sb_in(ctx, f"gelu{r}", [P, GROUP]) for r in range(2)]
        act_hi = [sb_in(ctx, f"gelu_hi{r}", [P, GROUP], F16) for r in range(2)]
        act_lo = [sb_in(ctx, f"gelu_lo{r}", [P, GROUP], F16) for r in range(2)]
        res_out = [sb_in(ctx, f"res_out{t}", [P, D]) for t in range(T)]
        bo_row = sb_in(ctx, "bo_row", [P, D])
        bv_row = sb_in(ctx, "bv_row", [P, D])
        b2_row = sb_in(ctx, "b2_row", [P, D])
        bqk_col = sb_in(ctx, "bqk_col", [P, 2 * KC])
        b1_col = sb_in(ctx, "b1_col", [P, NJ])
        zeros = sb_in(ctx, "zeros", [P, BT])
        mask = sb_in(ctx, "mask", [P, BT])
        half = sb_in(ctx, "neg_half", [P, T])
        stats = sb_in(ctx, "stats_c", [P, T, 6])
        both = sb_in(ctx, "both_c", [P, T, 2])
        diff = sb_in(ctx, "diff_c", [P, T])
        mean = sb_in(ctx, "mean_c", [P, T])
        var_eps = sb_in(ctx, "var_eps_c", [P, T])
        rstd = sb_in(ctx, "rstd_c", [P, T])
        sc = sb_in(ctx, "sc", [P, T, BT])
        row = sb_in(ctx, "row", [P, T])
        spread = sb_in(ctx, "spread", [P, T, BT])
        across = sb_in(ctx, "across", [P, T, BT])
        neg_max = sb_in(ctx, "neg_max_c", [P, T])
        ex = sb_in(ctx, "ex", [P, T, BT])
        ex_sum = sb_in(ctx, "ex_sum", [P, T])
        ex_T = sb_in(ctx, "ex_T", [P, T, BT])
        total = sb_in(ctx, "total", [P, T])
        inv_total = sb_in(ctx, "inv_total", [P, T])
        w_hi = sb_in(ctx, "w_hi", [P, T, P], F16)
        w_lo = sb_in(ctx, "w_lo", [P, T, P], F16)

        names = ["consts_landed", "x_landed", "pool_const", "mask_done", "xb_done", "at_done", "b2_added",
                 "rstd2_done", "rstd3_done", "wo_ps", "t2_ps", "t3_ps", "qk_ps", "val_ps", "sc_ps", "pv_ps",
                 "h_ps", "f_ps", "x2T_hi_done", "x2T_lo_done", "x3T_hi_done", "x3T_lo_done", "qk_done",
                 "qk_hi_done", "qk_lo_done", "val_done", "val_hi_done", "val_lo_done", "x1_done", "x2_done",
                 "stats2_done", "stats3_done", "merged2", "merged3", "eps2_done", "eps3_done",
                 "norm2_done", "norm3_done", "sc_done", "chain", "neg_done", "ex_done", "inv_done",
                 "ex_T_done", "w_hi_done", "w_done", "gelu_done", "gelu_hi_done", "gelu_lo_done",
                 "scaled_done", "out_done", "out_stored0", "out_stored1"]
        s = {n: sem_in(ctx, n + "_c") for n in names}
        stored = [s["out_stored0"], s["out_stored1"]]
        late = {name: (late_hi[:, w], late_lo[:, w]) for w, name in enumerate(("xWo", "sWq", "sWk", "sWv"))}
        landed = [sem_in(ctx, f"ffn_landed{r}") for r in range(RING)]
        sign_done = sem_in(ctx, "sign_done")
        sum_done = sem_in(ctx, "sum_done")
        abs_done = sem_in(ctx, "abs_done")
        added = sem_in(ctx, "added")
        alpha1_done = sem_in(ctx, "alpha1_done")
        alpha2_done = sem_in(ctx, "alpha2_done")
        NW = D * HID // (P * PIECE)
        HALVES = HID // PIECE
        staged = []
        for j in range(NW):
            c, h = j // HALVES, j % HALVES
            staged.append((w1_t[c * P:(c + 1) * P, h * PIECE:(h + 1) * PIECE], sign_done, j + 1))
            staged.append((w1.rearrange("(j p) n -> p j n", p=P)[:, 2 * j:2 * j + 2, :], sum_done, j + 1))
        for j in range(NW):
            staged.append((w2_t.rearrange("(j p) n -> p j n", p=P)[:, 2 * j:2 * j + 2, :], added, j + 1))
        def piece(n):
            return raw[n % RING], landed[n % RING], 16 * (n // RING + 1)
        sum_bank = psum[:, 0, :]
        CHAIN = 5

        def f_bank(t):
            return psum[:, t, :]

        def h_bank(j):
            return psum[:, 2 + j % 2, 0:GROUP]

        def g_bank(n):
            return psum[:, 4 + n, :]

        def chunks(bank, c):
            return bank.rearrange("p (c n) -> p c n", c=c)

        QK_BANK = (2, 3, 0, 1)
        sc_bank = g_bank(0)[:, 0:T * P].rearrange("p (t n) -> p t n", t=T)

        def rounds(engine, one):
            one(0, 0, front=True, ffn=False)
            one(1, 1, front=True, ffn=True)
            with engine.Fori(1, NG // 2 - 1) as i:
                one(i * 2, 0, front=True, ffn=True)
                one(i * 2 + 1, 1, front=True, ffn=True)
            one(NG - 2, 0, front=True, ffn=True)
            one(NG - 1, 1, front=True, ffn=True)
            one(NG, 0, front=False, ffn=True)

        block = ctx.enter_context(nc.Block())

        @block.sync
        def _(sp):
            for dst, src in ((bo_row, bo), (bv_row, bv), (b2_row, b2)):
                sp.dma_start(dst[:, :], src.to_broadcast([P, D])).then_inc(s["consts_landed"], 16)
            for dst, src in ((bqk_col[:, 0:KC], bq), (bqk_col[:, KC:], bk), (b1_col[:, :], b1)):
                sp.dma_start(dst, src).then_inc(s["consts_landed"], 16)

            def load(n):
                past(sp, s["x1_done"], T * n)
                sp.dma_start(xb[:, :, :], x_rows[:, bass.ds(n * T, T), :]).then_inc(s["x_landed"], 16)

            def one(n, u, front, ffn):
                if not (isinstance(n, int) and (n >= NG - 1 or n == 0)):
                    load(n + 1)
                if ffn:
                    for t in range(T):
                        sp.wait_ge(s["out_done"], (n - 1) * T + t + 1)
                        sp.dma_start(out_rows[:, bass.ds((n - 1) * T + t, 1), :],
                                     res_out[t][:, :].unsqueeze(1)).then_inc(stored[t], 16)
            def stage_pieces(first, last):
                for n in range(first, last):
                    if n >= RING:
                        sp.wait_ge(staged[n - RING][1], staged[n - RING][2])
                    src = staged[n][0]
                    dst = raw[n % RING][:, :]
                    if len(src.shape) == 3:
                        dst = dst.rearrange("p (j n) -> p j n", j=2)
                    sp.dma_start(dst, src).then_inc(landed[n % RING], 16)
            load(0)
            stage_pieces(0, 6)
            load(1)
            stage_pieces(6, len(staged))
            rounds(sp, one)
            for t in range(T):
                sp.wait_ge(stored[t], 16 * NG)

        @block.gpsimd
        def _(pool):
            nc.gpsimd.memset(half[:, :], -0.5).then_inc(s["pool_const"], 1)
            nc.gpsimd.memset(zeros[:, :], 0.0).then_inc(s["pool_const"], 1)
            nc.gpsimd.memset(w_hi[:, :, :], 0.0).then_inc(s["pool_const"], 1)
            nc.gpsimd.memset(w_lo[:, :, :], 0.0).then_inc(s["pool_const"], 1)
            pool.wait_ge(s["pool_const"], 4)
            for b in range(BPT):
                rows = slice(BT * b, BT * b + BT)
                nc.gpsimd.affine_select(out=mask[rows, :], in_=zeros[rows, :], compare_op=ALU.is_ge,
                                        fill=MASKED, base=0, pattern=[[-1, BT]],
                                        channel_multiplier=1).then_inc(s["mask_done"], 1)
            pool.wait_ge(s["mask_done"], BPT)
            pool.wait_ge(s["consts_landed"], 16 * 6)

            def stage(n):
                past(pool, s["wo_ps"], T * n)
                for src, dst in ((heads_hi, at_hi), (heads_lo, at_lo)):
                    nc.gpsimd.tensor_copy(dst[:, :, :], src[:, :, bass.ds(n * GROUP, GROUP)]
                                          ).then_inc(s["at_done"], 1)
                pool.wait_ge(s["x_landed"], 16 * (n + 1))
                nc.gpsimd.tensor_tensor(xb[:, :, :], xb[:, :, :],
                                        bo_row[:, :].unsqueeze(1).to_broadcast([P, T, D]),
                                        ALU.add).then_inc(s["xb_done"], 1)

            def power(n, eps_done, rstd_done):
                pool.wait_ge(eps_done, n + 1)
                nc.gpsimd.tensor_tensor(rstd[:, :], var_eps[:, :], half[:, :], ALU.pow).then_inc(rstd_done, 1)

            def one(n, u, front, ffn):
                if not front:
                    return
                power(n, s["eps2_done"], s["rstd2_done"])
                if not (isinstance(n, int) and n == NG - 1):
                    stage(n + 1)
                power(n, s["eps3_done"], s["rstd3_done"])
                pool.wait_ge(s["norm3_done"], T * (n + 1))
                nc.gpsimd.tensor_tensor(res[u][:, :, :], res[u][:, :, :],
                                        b2_row[:, :].unsqueeze(1).to_broadcast([P, T, D]),
                                        ALU.add).then_inc(s["b2_added"], 1)
            stage(0)
            rounds(pool, one)

        @block.scalar
        def _(eng):
            def high_T(bank_ready, dst, done, n):
                for t in range(T):
                    eng.wait_ge(bank_ready, T * n + t + 1)
                    nc.scalar.copy(dst[:, :, t * P:(t + 1) * P], chunks(g_bank(t), KC)).then_inc(done, 1)

            def hidden(g, j):
                eng.wait_ge(s["h_ps"], NJ * g + j + 1)
                past(eng, s["gelu_lo_done"], NJ * g + j - 1)
                nc.scalar.activation(act[j % 2][:, :], h_bank(j), ACT.Gelu, bias=b1_col[:, j:j + 1],
                                     scale=alpha1[:, j:j + 1]).then_inc(s["gelu_done"], 1)
                eng.wait_ge(s["gelu_done"], NJ * g + j + 1)
                nc.scalar.copy(act_hi[j % 2][:, :], act[j % 2][:, :]).then_inc(s["gelu_hi_done"], 1)

            def prepare(j):
                n = 2 * j if j < NW else NW + j
                src, there, count = piece(n)
                eng.wait_ge(there, count)
                if j < NW:
                    c, h = j // HALVES, j % HALVES
                    dst = sign1[:, c, h * PIECE:(h + 1) * PIECE]
                else:
                    dst = sign2[:, 2 * (j - NW):2 * (j - NW) + 2, :].rearrange("p j n -> p (j n)")
                nc.scalar.activation(dst, src[:, :], ACT.Sign).then_inc(sign_done, 1)

            def one(n, u, front, ffn):
                g = n - 1

                def F(*js):
                    for j in js:
                        if ffn:
                            hidden(g, j)
                        else:
                            prepare(j)
                F(0, 1, 2, 3)
                if front:
                    high_T(s["t2_ps"], x2T_hi, s["x2T_hi_done"], n)
                F(4, 5)
                if front:
                    for r in range(4):
                        eng.wait_ge(s["qk_ps"], 4 * n + r + 1)
                        past(eng, s["qk_lo_done"], 4 * n + r - 1)
                        for c in range(2):
                            last = nc.scalar.activation(
                                qk[r % 2][:, c, :], chunks(g_bank(QK_BANK[r]), 2)[:, c, :], ACT.Identity,
                                bias=bqk_col[:, 2 * r + c:2 * r + c + 1], scale=W_UNSCALE)
                        last.then_inc(s["qk_done"], 1)
                F(6, 7)
                if front:
                    eng.wait_ge(s["neg_done"], n + 1)
                    for t in range(T):
                        nc.scalar.activation(ex[:, t, :], sc[:, t, :], ACT.Exp, bias=neg_max[:, t:t + 1],
                                             accum_out=ex_sum[:, t:t + 1]).then_inc(s["ex_done"], 1)
                F(*range(8, NJ))
                if front:
                    past(eng, s["h_ps"], NJ * n)
                    high_T(s["t3_ps"], x3T_hi, s["x3T_hi_done"], n)
                if not ffn:
                    eng.wait_ge(added, NW)
                    nc.scalar.mul(alpha2_row[:, :], sum_bank, 1.0 / HID).then_inc(alpha2_done, 1)
                    eng.wait_ge(alpha1_done, 1)
            eng.wait_ge(s["consts_landed"], 16 * 6)
            rounds(eng, one)

        @block.vector
        def _(dve):
            def low_T(hi_done, hi, lo, done, n):
                for t in range(T):
                    dve.wait_ge(hi_done, T * n + t + 1)
                    nc.vector.tensor_tensor(lo[:, :, t * P:(t + 1) * P], chunks(g_bank(t), KC),
                                            hi[:, :, t * P:(t + 1) * P], ALU.subtract).then_inc(done, 1)

            def hidden(g, j):
                dve.wait_ge(s["gelu_hi_done"], NJ * g + j + 1)
                nc.vector.tensor_tensor(act_lo[j % 2][:, :], act[j % 2][:, :], act_hi[j % 2][:, :],
                                        ALU.subtract).then_inc(s["gelu_lo_done"], 1)

            def statistics(n, u, k):
                for t in range(T):
                    dve.wait_ge(s["x1_done" if k == 2 else "x2_done"], T * n + t + 1)
                    nc.vector.bn_stats(stats[:, t, :], res[u][:, t, :]).then_inc(s[f"stats{k}_done"], 1)
                merge_statistics(nc, dve, n, stats, both[:, :, :], diff[:, :], mean[:, :], var_eps[:, :],
                                 s[f"stats{k}_done"], T * (n + 1), s[f"merged{k}"], s[f"eps{k}_done"])

            def normalise(n, u, k):
                dve.wait_ge(s[f"rstd{k}_done"], n + 1)
                if k == 2:
                    past(dve, s["t3_ps"], T * n)
                else:
                    dve.wait_ge(s["t2_ps"], T * (n + 1))
                for t in range(T):
                    nc.vector.tensor_scalar(xn[:, t, :], res[u][:, t, :], mean[:, t:t + 1],
                                            rstd[:, t:t + 1], ALU.subtract,
                                            ALU.mult).then_inc(s[f"norm{k}_done"], 1)

            def link(ins, value):
                ins.then_inc(s["chain"], 1)
                dve.wait_ge(s["chain"], value)

            def projections(n):
                for r in range(4):
                    cols = slice(2 * r, 2 * r + 2)
                    dve.wait_ge(s["qk_done"], 4 * n + r + 1)
                    nc.vector.tensor_copy(qk_hi[:, cols, :], qk[r % 2][:, :, :]).then_inc(s["qk_hi_done"], 1)
                    dve.wait_ge(s["qk_hi_done"], 4 * n + r + 1)
                    nc.vector.tensor_tensor(qk_lo[:, cols, :], qk[r % 2][:, :, :], qk_hi[:, cols, :],
                                            ALU.subtract).then_inc(s["qk_lo_done"], 1)

            def split_values(n):
                for t in range(T):
                    dve.wait_ge(s["val_ps"], T * n + t + 1)
                    past(dve, s["val_lo_done"], T * n + t)
                    nc.vector.scalar_tensor_tensor(out=val[:, :], in0=g_bank(2 + t), scalar=W_UNSCALE,
                                                   in1=bv_row[:, :], op0=ALU.mult,
                                                   op1=ALU.add).then_inc(s["val_done"], 1)
                    dve.wait_ge(s["val_done"], T * n + t + 1)
                    nc.vector.tensor_copy(val_hi[:, t, :], val[:, :]).then_inc(s["val_hi_done"], 1)
                    dve.wait_ge(s["val_hi_done"], T * n + t + 1)
                    nc.vector.tensor_tensor(val_lo[:, t, :], val[:, :], val_hi[:, t, :],
                                            ALU.subtract).then_inc(s["val_lo_done"], 1)

            def maxima(n):
                dve.wait_ge(s["sc_ps"], n + 1)
                for b in range(BPT):
                    rows = slice(BT * b, BT * b + BT)
                    nc.vector.scalar_tensor_tensor(
                        out=sc[rows, :, :], in0=sc_bank[rows, :, BT * b:BT * b + BT], scalar=SCALE,
                        in1=mask[rows, :].unsqueeze(1).to_broadcast([BT, T, BT]), op0=ALU.mult,
                        op1=ALU.add).then_inc(s["sc_done"], 1)
                dve.wait_ge(s["sc_done"], BPT * (n + 1))
                link(nc.vector.reduce_max(row[:, :], sc[:, :, :], AX.X), CHAIN * n + 1)
                link(nc.vector.tensor_copy(spread[:, :, :], row[:, :].unsqueeze(2).to_broadcast([P, T, BT])),
                     CHAIN * n + 2)
                link(nc.vector.transpose(across[:, :, :], spread[:, :, :]), CHAIN * n + 3)
                link(nc.vector.reduce_max(row[:, :], across[:, :, :], AX.X), CHAIN * n + 4)
                nc.vector.tensor_scalar(neg_max[:, :], row[:, :], -1.0, EXP_SHIFT, ALU.mult,
                                        ALU.add).then_inc(s["neg_done"], 1)

            def weights(n):
                dve.wait_ge(s["ex_done"], T * (n + 1))
                nc.vector.transpose(ex_T[:, :, :], ex[:, :, :]).then_inc(s["ex_T_done"], 1)
                dve.wait_ge(s["ex_T_done"], n + 1)
                for b in range(BPT):
                    rows = slice(BT * b, BT * b + BT)
                    nc.vector.tensor_copy(w_hi[rows, :, rows], ex_T[rows, :, :]).then_inc(s["w_hi_done"], 1)
                for b in range(BPT):
                    rows = slice(BT * b, BT * b + BT)
                    dve.wait_ge(s["w_hi_done"], BPT * n + b + 1)
                    nc.vector.tensor_tensor(w_lo[rows, :, rows], ex_T[rows, :, :], w_hi[rows, :, rows],
                                            ALU.subtract).then_inc(s["w_done"], 1)

            def totals(n):
                link(nc.vector.tensor_copy(spread[:, :, :], ex_sum[:, :].unsqueeze(2).to_broadcast([P, T, BT])),
                     CHAIN * n + 5)
                nc.vector.transpose(across[:, :, :], spread[:, :, :]).then_inc(s["inv_done"], 1)
                dve.wait_ge(s["inv_done"], 3 * n + 1)
                nc.vector.reduce_sum(total[:, :], across[:, :, :], AX.X).then_inc(s["inv_done"], 1)
                dve.wait_ge(s["inv_done"], 3 * n + 2)
                nc.vector.reciprocal(inv_total[:, :], total[:, :]).then_inc(s["inv_done"], 1)

            def finish(g, u):
                dve.wait_ge(s["f_ps"], g + 1)
                for t in range(T):
                    past(dve, stored[t], 16 * g)
                    nc.vector.tensor_tensor(res_out[t][:, :], f_bank(t), alpha2_row[:, :],
                                            ALU.mult).then_inc(s["scaled_done"], 1)
                dve.wait_ge(s["b2_added"], g + 1)
                for t in range(T):
                    dve.wait_ge(s["scaled_done"], T * g + t + 1)
                    nc.vector.tensor_tensor(res_out[t][:, :], res_out[t][:, :], res[u][:, t, :],
                                            ALU.add).then_inc(s["out_done"], 1)

            def prepare(j):
                if j < NW:
                    src, there, count = piece(2 * j + 1)
                    dve.wait_ge(there, count)
                    nc.vector.tensor_reduce(sum1[:, 2 * j:2 * j + 2], src[:, :].rearrange(
                        "p (j n) -> p j n", j=2), AX.X, ALU.add, apply_absolute_value=True).then_inc(sum_done, 1)
                    if j == NW - 1:
                        dve.wait_ge(sum_done, NW)
                        nc.vector.tensor_scalar(alpha1[:, :], sum1[:, :], 1.0 / D, None,
                                                ALU.mult).then_inc(alpha1_done, 1)
                else:
                    src, _, _ = piece(NW + j)
                    dve.wait_ge(sign_done, j + 1)
                    sign = sign2[:, 2 * (j - NW):2 * (j - NW) + 2, :].rearrange("p j n -> p (j n)")
                    nc.vector.tensor_tensor(src[:, :], src[:, :], sign, ALU.mult).then_inc(abs_done, 1)

            def one(n, u, front, ffn):
                g = n - 1

                def F(*js):
                    for j in js:
                        if ffn:
                            hidden(g, j)
                        else:
                            prepare(j)
                if front:
                    dve.wait_ge(s["xb_done"], n + 1)
                    past(dve, s["out_done"], T * (n - 1))
                    for t in range(T):
                        dve.wait_ge(s["wo_ps"], T * n + t + 1)
                        nc.vector.scalar_tensor_tensor(out=res[u][:, t, :], in0=g_bank(2 + t),
                                                       scalar=W_UNSCALE, in1=xb[:, t, :], op0=ALU.mult,
                                                       op1=ALU.add).then_inc(s["x1_done"], 1)
                    statistics(n, u, 2)
                F(0, 1)
                if front:
                    normalise(n, u, 2)
                F(2, 3)
                if front:
                    low_T(s["x2T_hi_done"], x2T_hi, x2T_lo, s["x2T_lo_done"], n)
                F(4, 5)
                if front:
                    projections(n)
                F(6, 7)
                if front:
                    maxima(n)
                    split_values(n)
                F(8)
                if front:
                    weights(n)
                    totals(n)
                F(9, 10, 11)
                if front:
                    dve.wait_ge(s["inv_done"], 3 * n + 3)
                    for t in range(T):
                        dve.wait_ge(s["pv_ps"], T * n + t + 1)
                        nc.vector.scalar_tensor_tensor(out=res[u][:, t, :], in0=g_bank(2 + t),
                                                       scalar=inv_total[:, t:t + 1], in1=res[u][:, t, :],
                                                       op0=ALU.mult, op1=ALU.add).then_inc(s["x2_done"], 1)
                    statistics(n, u, 3)
                F(12, 13)
                if front:
                    normalise(n, u, 3)
                F(14, 15)
                if front:
                    low_T(s["x3T_hi_done"], x3T_hi, x3T_lo, s["x3T_lo_done"], n)
                if ffn:
                    finish(g, 1 - u)
                else:
                    dve.wait_ge(alpha2_done, 1)
            dve.wait_ge(s["consts_landed"], 16 * 6)
            dve.wait_ge(s["mask_done"], BPT)
            rounds(dve, one)

        @block.tensor
        def _(pe):
            def run(bank, steps):
                for n, (a, b) in enumerate(steps):
                    mm = nc.tensor.matmul(bank, a, b, start=(n == 0), stop=(n == len(steps) - 1))
                return mm

            def transposes(n, norm_done, done):
                for t in range(T):
                    pe.wait_ge(norm_done, T * n + t + 1)
                    for c in range(KC):
                        mm = nc.tensor.transpose(chunks(g_bank(t), KC)[:, c, :], xn[:, t, c * P:(c + 1) * P],
                                                 ident[:, :])
                    mm.then_inc(done, 1)

            def layer1(g, j):
                past(pe, s["gelu_done"], NJ * g + j - 1)
                cols = slice(j * P, (j + 1) * P)
                run(h_bank(j), [(sign1[:, k, cols], x3[:, k, :]) for k in range(KC)
                                for x3 in (x3T_hi, x3T_lo)]).then_inc(s["h_ps"], 1)

            def layer2(g, j):
                pe.wait_ge(s["gelu_lo_done"], NJ * g + j + 1)
                if j == 0:
                    past(pe, s["scaled_done"], T * g)
                for t in range(T):
                    for n, a in enumerate((act_hi[j % 2], act_lo[j % 2])):
                        mm = nc.tensor.matmul(f_bank(t), a[:, t * P:(t + 1) * P], sign2[:, j, :],
                                              start=(j == 0 and n == 0), stop=(j == NJ - 1 and n == 1))
                if j == NJ - 1:
                    mm.then_inc(s["f_ps"], 1)

            def prepare(j):
                if j < NW:
                    return
                pe.wait_ge(abs_done, j - NW + 1)
                for h in range(2):
                    mm = nc.tensor.matmul(sum_bank, ones[:, :], piece(NW + j)[0][:, h * D:(h + 1) * D],
                                          start=(j == NW and h == 0), stop=(j == 2 * NW - 1 and h == 1))
                mm.then_inc(added, 1)

            def one(n, u, front, ffn):
                g = n - 1

                def F(*js):
                    for j in js:
                        if not ffn:
                            prepare(j)
                            continue
                        layer1(g, j)
                        if j > 0:
                            layer2(g, j - 1)
                if front:
                    pe.wait_ge(s["at_done"], 2 * (n + 1))
                    for t in range(T):
                        rows = slice(t * P, (t + 1) * P)
                        run(g_bank(2 + t), [(a[:, k, rows], w[:, k, :]) for k in range(KC)
                                            for a, w in passes(at_hi, at_lo, *late["xWo"])]
                            ).then_inc(s["wo_ps"], 1)
                if ffn:
                    pe.wait_ge(s["x3T_lo_done"], T * (g + 1))
                F(0, 1, 2, 3)
                if front:
                    transposes(n, s["norm2_done"], s["t2_ps"])
                F(4, 5)
                if front:
                    pe.wait_ge(s["x2T_lo_done"], T * (n + 1))
                    for r in range(4):
                        hi, lo = late["sWq" if r < 2 else "sWk"]
                        for c in range(2):
                            m = 2 * (r % 2) + c
                            mm = run(chunks(g_bank(QK_BANK[r]), 2)[:, c, :],
                                     [(w[:, k, m * P:(m + 1) * P], xt[:, k, :]) for k in range(KC)
                                      for w, xt in passes(hi, lo, x2T_hi, x2T_lo)])
                        mm.then_inc(s["qk_ps"], 1)
                F(6, 7)
                if front:
                    pe.wait_ge(s["qk_lo_done"], 4 * (n + 1))
                    for t in range(T):
                        rows = slice(t * P, (t + 1) * P)
                        mm = run(sc_bank[:, t, :], [(q[:, m, rows], k[:, KC + m, rows]) for m in range(KC)
                                                    for q, k in passes(qk_hi, qk_lo, qk_hi, qk_lo)])
                    mm.then_inc(s["sc_ps"], 1)
                    for t in range(T):
                        rows = slice(t * P, (t + 1) * P)
                        run(g_bank(2 + t), [(xt[:, k, rows], w[:, k, :]) for k in range(KC)
                                            for xt, w in passes(x2T_hi, x2T_lo, *late["sWv"])]
                            ).then_inc(s["val_ps"], 1)
                F(8, 9, 10, 11)
                if front:
                    pe.wait_ge(s["w_done"], BPT * (n + 1))
                    pe.wait_ge(s["val_lo_done"], T * (n + 1))
                    for t in range(T):
                        run(g_bank(2 + t), [(w[:, t, :], v[:, t, :]) for w, v in
                                            passes(w_hi, w_lo, val_hi, val_lo)]).then_inc(s["pv_ps"], 1)
                F(12, 13, 14)
                if front:
                    transposes(n, s["norm3_done"], s["t3_ps"])
                F(15)
                if ffn:
                    layer2(g, NJ - 1)
                else:
                    pe.wait_ge(alpha2_done, 1)
            pe.wait_ge(s["pool_const"], 4)
            rounds(pe, one)


def kernel(x, ctx_1024, L0_xattn_Wq, L0_xattn_Wk, L0_xattn_Wv, L0_xattn_Wo, L0_xattn_bo, L0_attn_Wq,
           L0_attn_bq, L0_attn_Wk, L0_attn_bk, L0_attn_Wv, L0_attn_bv, L0_ffn_w1, L0_ffn_b1, L0_ffn_w2,
           L0_ffn_b2):
    import numpy as np
    import concourse.bacc as bacc
    from concourse.bass_utils import run_bass_kernel_spmd

    B, L, D = x.shape
    S = ctx_1024.shape[1] - 1
    ctx_t = np.asarray(ctx_1024).transpose(0, 2, 1).reshape(B, D // P, P, S + 1).transpose(0, 2, 1, 3)

    def columns(b):
        return np.asarray(b).reshape(-1, P).T

    def rows(w):
        return np.asarray(w).reshape(-1, P, D).transpose(1, 0, 2).reshape(P, -1)

    arrays = dict(
        x=np.asarray(x).reshape(B * L, D), ctx_main=ctx_t[..., :S],
        ctx_last=ctx_t[..., S].transpose(1, 2, 0), xWq=L0_xattn_Wq, xWk=L0_xattn_Wk, xWv=L0_xattn_Wv,
        late_w=np.stack([rows(L0_xattn_Wo), rows(L0_attn_Wq), rows(L0_attn_Wk), rows(L0_attn_Wv)]),
        bo=np.asarray(L0_xattn_bo)[None], bq=columns(L0_attn_bq), bk=columns(L0_attn_bk),
        bv=np.asarray(L0_attn_bv)[None], w1=L0_ffn_w1, w1_t=np.asarray(L0_ffn_w1).T,
        b1=columns(L0_ffn_b1), w2_t=np.asarray(L0_ffn_w2).T, b2=np.asarray(L0_ffn_b2)[None])
    arrays = {name: np.ascontiguousarray(a) for name, a in arrays.items()}

    nc = bacc.Bacc("TRN2", target_bir_lowering=False, num_devices=1)
    args = {name: nc.dram_tensor(f"in_{name}", a.shape, mybir.dt.from_np(a.dtype), kind="ExternalInput").ap()
            for name, a in arrays.items()}
    v_last_rows = nc.dram_tensor("v_last_rows", (B, D), F32, kind="Internal").ap()
    out = nc.dram_tensor("out", (B * L, D), F32, kind="ExternalOutput").ap()
    perceiver_block(nc, v_last_rows=v_last_rows, out=out, **args)
    got = run_bass_kernel_spmd(nc, [{f"in_{name}": a for name, a in arrays.items()}], core_ids=[0])
    return got.results[0]["out"].reshape(B, L, D)
```

```python
from contextlib import ExitStack

import concourse.bass as bass
from concourse import mybir

P = 128
F32 = mybir.dt.float32
F16 = mybir.dt.float16
ALU = mybir.AluOpType
ACT = mybir.ActivationFunctionType
AX = mybir.AxisListType

W_SCALE = 64.0
W_UNSCALE = 1.0 / W_SCALE
EXP_SHIFT = 6.931471805599453
EPS = 1e-5
MASKED = -1e30
FEATURES = 512


def past(engine, semaphore, count):
    if isinstance(count, int) and count <= 0:
        return
    engine.wait_ge(semaphore, count)


def passes(hi_a, lo_a, hi_b, lo_b):
    return ((hi_a, hi_b), (hi_a, lo_b), (lo_a, hi_b))


def merge_statistics(nc, dve, n, stats, both, diff, mean, var_eps, stats_done, stats_count, merged, eps_done):
    dve.wait_ge(stats_done, stats_count)
    nc.vector.tensor_tensor(both, stats[:, :, 1:3], stats[:, :, 4:6], ALU.add).then_inc(merged, 1)
    nc.vector.tensor_tensor(diff, stats[:, :, 1], stats[:, :, 4], ALU.subtract).then_inc(merged, 1)
    dve.wait_ge(merged, n * 5 + 2)
    nc.vector.tensor_scalar(mean, both[:, :, 0], 0.5, None, ALU.mult).then_inc(merged, 1)
    nc.vector.tensor_scalar(var_eps, both[:, :, 1], 1.0 / FEATURES, EPS, ALU.mult, ALU.add).then_inc(merged, 1)
    nc.vector.tensor_tensor(diff, diff, diff, ALU.mult).then_inc(merged, 1)
    dve.wait_ge(merged, n * 5 + 5)
    nc.vector.scalar_tensor_tensor(out=var_eps, in0=diff, scalar=0.25, in1=var_eps, op0=ALU.mult,
                                   op1=ALU.add).then_inc(eps_done, 1)


def perceiver_block(nc, x, ctx_main, ctx_last, xWq, xWk, xWv, late_w, bo, bq, bk, bv, w1_t, b1, w2_t, b2,
                    v_last_rows, out):
    TOKENS, D = x.shape
    BATCH = ctx_main.shape[0]
    DH = 32
    KC = D // P
    LATE = late_w.shape[0]

    with ExitStack() as whole:
        def sem_in(stack, name):
            return stack.enter_context(nc.semaphore(name))

        def sb_in(stack, name, shape, dt=F32):
            return stack.enter_context(nc.sbuf_tensor(name, shape, dt))

        psum = whole.enter_context(nc.psum_tensor("psum", [P, 8, 512], F32))

        heads_hi = sb_in(whole, "heads_hi", [P, KC, TOKENS], F16)
        heads_lo = sb_in(whole, "heads_lo", [P, KC, TOKENS], F16)
        late_hi = sb_in(whole, "late_hi", [P, LATE, KC, D], F16)
        late_lo = sb_in(whole, "late_lo", [P, LATE, KC, D], F16)
        ident = sb_in(whole, "ident", [P, P])
        ones = sb_in(whole, "ones", [P, P])

        with ExitStack() as early:
            xWk_hi = sb_in(early, "xWk_hi", [P, KC, D], F16)
            xWk_lo = sb_in(early, "xWk_lo", [P, KC, D], F16)
            xWv_hi = sb_in(early, "xWv_hi", [P, KC, D], F16)
            xWv_lo = sb_in(early, "xWv_lo", [P, KC, D], F16)
            k_last_hi = sb_in(early, "k_last_hi", [P, KC, BATCH], F16)
            k_last_lo = sb_in(early, "k_last_lo", [P, KC, BATCH], F16)
            S = ctx_main.shape[3]
            c_raw = [sb_in(early, f"ctx_raw{u}", [P, KC, S]) for u in range(2)]
            c_hi = [sb_in(early, f"c_hi{r}", [P, KC, 2, S], F16) for r in range(2)]
            c_lo = [sb_in(early, f"c_lo{r}", [P, KC, 2, S], F16) for r in range(2)]
            ctx_landed = [sem_in(early, f"ctx_landed{u}") for u in range(2)]
            c_hi_done = sem_in(early, "c_hi_done")
            c_lo_done = sem_in(early, "c_lo_done")
            contexts = (c_raw, c_hi, c_lo, ctx_landed, c_hi_done, c_lo_done)
            cross_queries(nc, sem_in, sb_in, psum, x, xWq, xWk, xWv, ctx_main, ctx_last, ident, ones,
                          heads_hi, heads_lo, xWk_hi, xWk_lo, xWv_hi, xWv_lo, k_last_hi, k_last_lo,
                          v_last_rows, contexts)
            cross_attention(nc, sem_in, sb_in, psum, ctx_main, v_last_rows, xWk_hi, xWk_lo, xWv_hi,
                            xWv_lo, k_last_hi, k_last_lo, ident, heads_hi, heads_lo, late_w, late_hi,
                            late_lo, contexts, float(DH) ** -0.5)
        token_stages(nc, sem_in, sb_in, psum, x, bo, bq, bk, bv, b1, b2, w1_t, w2_t, late_hi, late_lo,
                     ident, ones, heads_hi, heads_lo, float(D) ** -0.5, out)


def load_context(nc, sp, ctx_main, contexts, b, u):
    c_raw, _, _, ctx_landed, c_hi_done, c_lo_done = contexts
    past(sp, c_hi_done, b - 1)
    past(sp, c_lo_done, b - 1)
    sp.dma_start(c_raw[u % 2][:, :, :], ctx_main[bass.ds(b, 1)].rearrange("o p c s -> (o p) c s")
                 ).then_inc(ctx_landed[u % 2], 16)


def low_context(nc, pool, contexts, b, u):
    c_raw, c_hi, c_lo, _, c_hi_done, c_lo_done = contexts
    pool.wait_ge(c_hi_done, b + 1)
    nc.gpsimd.tensor_tensor(c_lo[u // 2][:, :, u % 2, :], c_raw[u % 2][:, :, :],
                            c_hi[u // 2][:, :, u % 2, :], ALU.subtract).then_inc(c_lo_done, 1)


def cross_queries(nc, sem_in, sb_in, psum, x, xWq, xWk, xWv, ctx_main, ctx_last, ident, ones, heads_hi,
                  heads_lo, wk_hi, wk_lo, wv_hi, wv_lo, k_last_hi, k_last_lo, v_last_rows, contexts):
    KC, TOKENS = heads_hi.shape[1], heads_hi.shape[2]
    D = wk_hi.shape[2]
    BATCH = k_last_hi.shape[2]
    TILES = 4
    GROUP = TILES * P
    NG = TOKENS // GROUP
    x_rows = x.rearrange("(t p) d -> p t d", p=P)
    c_raw, c_hi, c_lo, ctx_landed, c_hi_done, c_lo_done = contexts

    with ExitStack() as ctx:
        wq_hi = sb_in(ctx, "xWq_hi", [P, KC, D], F16)
        wq_lo = sb_in(ctx, "xWq_lo", [P, KC, D], F16)
        raw = [sb_in(ctx, f"raw_weight{r}", [P, KC, D]) for r in range(2)]
        raw_last = sb_in(ctx, "raw_last", [P, KC, BATCH])
        cl_hi = sb_in(ctx, "cl_hi", [P, KC, BATCH], F16)
        cl_lo = sb_in(ctx, "cl_lo", [P, KC, BATCH], F16)
        vl = sb_in(ctx, "vl", [P, D])
        xs = [sb_in(ctx, f"xs{u}", [P, TILES, D]) for u in range(2)]
        xT_hi = [sb_in(ctx, f"xT_hi{u}", [P, KC, GROUP], F16) for u in range(2)]
        xT_lo = [sb_in(ctx, f"xT_lo{u}", [P, KC, GROUP], F16) for u in range(2)]
        stats = sb_in(ctx, "stats", [P, TILES, 6])
        both = sb_in(ctx, "both", [P, TILES, 2])
        diff = sb_in(ctx, "diff", [P, TILES])
        mean = sb_in(ctx, "mean", [P, TILES])
        var_eps = sb_in(ctx, "var_eps", [P, TILES])
        half = sb_in(ctx, "half", [P, TILES])
        rstd = sb_in(ctx, "rstd", [P, TILES])

        x_landed = [sem_in(ctx, f"x_landed{u}") for u in range(2)]
        half_set = sem_in(ctx, "half_set")
        stats_done = sem_in(ctx, "stats_done")
        merged = sem_in(ctx, "merged")
        eps_done = sem_in(ctx, "eps_done")
        rstd_done = sem_in(ctx, "rstd_done")
        norm_done = sem_in(ctx, "norm_done")
        t_ps = sem_in(ctx, "t_ps")
        xT_hi_done = sem_in(ctx, "xT_hi_done")
        xT_lo_done = sem_in(ctx, "xT_lo_done")
        q_ps = sem_in(ctx, "q_ps")
        q_hi_done = sem_in(ctx, "q_hi_done")
        q_lo_done = sem_in(ctx, "q_lo_done")
        raw_landed = [sem_in(ctx, f"raw_landed{r}") for r in range(2)]
        last_landed = sem_in(ctx, "last_landed")
        w_hi_done = sem_in(ctx, "w_hi_done")
        w_lo_done = sem_in(ctx, "w_lo_done")
        w_scaled = sem_in(ctx, "w_scaled")
        cl_hi_done = sem_in(ctx, "cl_hi_done")
        cl_lo_done = sem_in(ctx, "cl_lo_done")
        ones_set = sem_in(ctx, "ones_set")
        ident_set = sem_in(ctx, "ident_set")
        k_last_ps = sem_in(ctx, "k_last_ps")
        v_last_ps = sem_in(ctx, "v_last_ps")
        kl_hi_done = sem_in(ctx, "kl_hi_done")
        kl_lo_done = sem_in(ctx, "kl_lo_done")
        vl_done = sem_in(ctx, "vl_done")
        v_stored = sem_in(ctx, "v_last_stored")
        WEIGHTS = ((xWq, wq_hi, wq_lo), (xWk, wk_hi, wk_lo), (xWv, wv_hi, wv_lo))
        k_last_bank = psum[:, 0, :].rearrange("p (c b) -> p c b", c=KC)
        v_last_bank = psum[:, 1, :]

        def t_bank(t):
            return psum[:, t, :].rearrange("p (c n) -> p c n", c=KC)

        FIRST, LAST = range(KC - 1), range(KC - 1, KC)

        def groups(engine, one):
            for g in range(2):
                one(g, g)
            with engine.Fori(1, NG // 2 - 1) as i:
                for u in range(2):
                    one(i * 2 + u, u)
            for g in range(NG - 2, NG):
                one(g, g % 2, g < NG - 1)

        block = ctx.enter_context(nc.Block())

        @block.sync
        def _(sp):
            def load(g, u):
                past(sp, t_ps, TILES * (g - 1))
                sp.dma_start(xs[u][:, :, :], x_rows[:, bass.ds(g * TILES, TILES), :]).then_inc(x_landed[u], 16)
            def load_weight(n):
                past(sp, w_lo_done, n - 1)
                sp.dma_start(raw[n % 2][:, :, :], WEIGHTS[n][0].rearrange("(c p) n -> p c n", p=P)
                             ).then_inc(raw_landed[n % 2], 16)
            load(0, 0)
            load_weight(0)
            load(1, 1)
            load_weight(1)
            sp.dma_start(raw_last[:, :, :], ctx_last).then_inc(last_landed, 16)
            load_weight(2)
            with sp.Fori(1, NG // 2) as i:
                for u in range(2):
                    load(i * 2 + u, u)
            for b in range(6):
                load_context(nc, sp, ctx_main, contexts, b, b % 4)
            sp.wait_ge(vl_done, 1)
            sp.dma_start(v_last_rows, vl[:, :]).then_inc(v_stored, 16)
            sp.wait_ge(v_stored, 16)

        @block.gpsimd
        def _(pool):
            nc.gpsimd.memset(ones[:, :], 1.0).then_inc(ones_set, 1)
            nc.gpsimd.memset(half[:, :], -0.5).then_inc(half_set, 1)
            pool.wait_ge(ones_set, 1)
            nc.gpsimd.affine_select(out=ident[:, :], in_=ones[:, :], compare_op=ALU.is_equal, fill=0.0,
                                    base=0, pattern=[[-1, P]], channel_multiplier=1).then_inc(ident_set, 1)
            pool.wait_ge(half_set, 1)

            def power(g):
                pool.wait_ge(eps_done, g + 1)
                nc.gpsimd.tensor_tensor(rstd[:, :], var_eps[:, :], half[:, :], ALU.pow).then_inc(rstd_done, 1)

            def low_weight(n):
                pool.wait_ge(w_scaled, n)
                pool.wait_ge(w_lo_done, n)
                nc.gpsimd.tensor_tensor(WEIGHTS[n][2][:, :, :], raw[n % 2][:, :, :], WEIGHTS[n][1][:, :, :],
                                        ALU.subtract).then_inc(w_lo_done, 1)
            power(0)
            power(1)
            low_weight(1)
            power(2)
            pool.wait_ge(cl_hi_done, 1)
            nc.gpsimd.tensor_tensor(cl_lo[:, :, :], raw_last[:, :, :], cl_hi[:, :, :],
                                    ALU.subtract).then_inc(cl_lo_done, 1)
            power(3)
            low_weight(2)
            with pool.Fori(4, NG) as g:
                power(g)
            for b in range(4):
                low_context(nc, pool, contexts, b, b)

        @block.vector
        def _(dve):
            def normalise(g, u):
                dve.wait_ge(x_landed[u], 8 * (g - u) + 16)
                for t in range(TILES):
                    nc.vector.bn_stats(stats[:, t, :], xs[u][:, t, :]).then_inc(stats_done, 1)
                merge_statistics(nc, dve, g, stats, both[:, :, :], diff[:, :], mean[:, :], var_eps[:, :],
                                 stats_done, (g + 1) * TILES, merged, eps_done)
                dve.wait_ge(rstd_done, g + 1)
                for t in range(TILES):
                    nc.vector.tensor_scalar(xs[u][:, t, :], xs[u][:, t, :], mean[:, t:t + 1],
                                            rstd[:, t:t + 1], ALU.subtract, ALU.mult).then_inc(norm_done, 1)

            def low_xT(g, u):
                past(dve, q_ps, KC * (g - 1))
                for t in range(TILES):
                    dve.wait_ge(xT_hi_done, g * TILES + t + 1)
                    nc.vector.tensor_tensor(xT_lo[u][:, :, t * P:(t + 1) * P], t_bank(t),
                                            xT_hi[u][:, :, t * P:(t + 1) * P],
                                            ALU.subtract).then_inc(xT_lo_done, 1)

            def low_q(g, chunks):
                for m in chunks:
                    dve.wait_ge(q_hi_done, g * KC + m + 1)
                    nc.vector.scalar_tensor_tensor(
                        out=heads_lo[:, m, bass.ds(g * GROUP, GROUP)], in0=psum[:, KC + m, :],
                        scalar=W_UNSCALE, in1=heads_hi[:, m, bass.ds(g * GROUP, GROUP)], op0=ALU.mult,
                        op1=ALU.subtract).then_inc(q_lo_done, 1)

            def one(g, u, more=True):
                low_q(g, FIRST)
                if more:
                    low_xT(g + 1, 1 - u)
                low_q(g, LAST)
                if not isinstance(g, int) or g + 2 < NG:
                    normalise(g + 2, u)
            normalise(0, 0)
            dve.wait_ge(w_hi_done, 1)
            nc.vector.scalar_tensor_tensor(out=wq_lo[:, :, :], in0=raw[0][:, :, :], scalar=W_SCALE,
                                           in1=wq_hi[:, :, :], op0=ALU.mult,
                                           op1=ALU.subtract).then_inc(w_lo_done, 1)
            low_xT(0, 0)
            normalise(1, 1)
            groups(dve, one)
            dve.wait_ge(kl_hi_done, 1)
            nc.vector.scalar_tensor_tensor(out=k_last_lo[:, :, :], in0=k_last_bank, scalar=W_UNSCALE,
                                           in1=k_last_hi[:, :, :], op0=ALU.mult,
                                           op1=ALU.subtract).then_inc(kl_lo_done, 1)

        @block.scalar
        def _(act):
            def high_xT(g, u):
                past(act, q_ps, KC * (g - 1))
                for t in range(TILES):
                    act.wait_ge(t_ps, g * TILES + t + 1)
                    nc.scalar.copy(xT_hi[u][:, :, t * P:(t + 1) * P], t_bank(t)).then_inc(xT_hi_done, 1)

            def high_q(g, chunks):
                for m in chunks:
                    act.wait_ge(q_ps, g * KC + m + 1)
                    nc.scalar.mul(heads_hi[:, m, bass.ds(g * GROUP, GROUP)], psum[:, KC + m, :],
                                  W_UNSCALE).then_inc(q_hi_done, 1)

            def high_weight(n):
                act.wait_ge(raw_landed[n % 2], 16 * (n // 2 + 1))
                nc.scalar.mul(WEIGHTS[n][1][:, :, :], raw[n % 2][:, :, :], W_SCALE).then_inc(w_hi_done, 1)

            def scale_weight(n):
                act.wait_ge(w_hi_done, n + 1)
                nc.scalar.mul(raw[n % 2][:, :, :], raw[n % 2][:, :, :], W_SCALE).then_inc(w_scaled, 1)

            def one(g, u, more=True):
                if not more:
                    last_tokens()
                high_q(g, FIRST)
                if more:
                    high_xT(g + 1, 1 - u)
                high_q(g, LAST)

            def last_tokens():
                for b in range(4):
                    act.wait_ge(ctx_landed[b % 2], 16 * (b // 2 + 1))
                    nc.scalar.copy(c_hi[b // 2][:, :, b % 2, :], c_raw[b % 2][:, :, :]).then_inc(c_hi_done, 1)
                act.wait_ge(k_last_ps, 1)
                nc.scalar.mul(k_last_hi[:, :, :], k_last_bank, W_UNSCALE).then_inc(kl_hi_done, 1)
                act.wait_ge(v_last_ps, 1)
                nc.scalar.mul(vl[:, :].rearrange("p (h g d) -> p g h d", h=4, g=KC),
                              v_last_bank.rearrange("p (g h d) -> p g h d", h=4, g=KC),
                              W_UNSCALE).then_inc(vl_done, 1)
            high_weight(0)
            high_xT(0, 0)
            high_weight(1)
            scale_weight(1)
            act.wait_ge(last_landed, 16)
            nc.scalar.copy(cl_hi[:, :, :], raw_last[:, :, :]).then_inc(cl_hi_done, 1)
            high_weight(2)
            scale_weight(2)
            groups(act, one)

        @block.tensor
        def _(pe):
            def transposes(g, u):
                for t in range(TILES):
                    pe.wait_ge(norm_done, g * TILES + t + 1)
                    past(pe, xT_lo_done, (g - 1) * TILES + t + 1)
                    for c in range(KC):
                        mm = nc.tensor.transpose(t_bank(t)[:, c, :], xs[u][:, t, c * P:(c + 1) * P],
                                                 ident[:, :])
                    mm.then_inc(t_ps, 1)

            def queries(g, u, chunks):
                pe.wait_ge(xT_lo_done, (g + 1) * TILES)
                for m in chunks:
                    past(pe, q_lo_done, (g - 1) * KC + m + 1)
                    steps = [(a[:, k, m * P:(m + 1) * P], b[:, k, :]) for k in range(KC)
                             for a, b in passes(wq_hi, wq_lo, xT_hi[u], xT_lo[u])]
                    for n, (a, b) in enumerate(steps):
                        mm = nc.tensor.matmul(psum[:, KC + m, :], a, b, start=(n == 0),
                                              stop=(n == len(steps) - 1))
                    mm.then_inc(q_ps, 1)

            def last_tokens():
                pe.wait_ge(xT_lo_done, NG * TILES)
                pe.wait_ge(w_lo_done, 3)
                pe.wait_ge(cl_lo_done, 1)
                for m in range(KC):
                    cols = slice(m * P, (m + 1) * P)
                    steps = [(a[:, k, cols], b[:, k, :]) for k in range(KC)
                             for a, b in passes(wk_hi, wk_lo, cl_hi, cl_lo)]
                    for n, (a, b) in enumerate(steps):
                        mm = nc.tensor.matmul(k_last_bank[:, m, :], a, b, start=(n == 0),
                                              stop=(n == len(steps) - 1))
                mm.then_inc(k_last_ps, 1)
                steps = [(a[:, k, :], b[:, k, :]) for k in range(KC)
                         for a, b in passes(cl_hi, cl_lo, wv_hi, wv_lo)]
                for n, (a, b) in enumerate(steps):
                    mm = nc.tensor.matmul(v_last_bank, a, b, start=(n == 0), stop=(n == len(steps) - 1))
                mm.then_inc(v_last_ps, 1)

            pe.wait_ge(ident_set, 1)
            transposes(0, 0)
            pe.wait_ge(w_lo_done, 1)

            def one(g, u, more=True):
                if not more:
                    last_tokens()
                queries(g, u, FIRST)
                if more:
                    transposes(g + 1, 1 - u)
                queries(g, u, LAST)
            groups(pe, one)


def cross_attention(nc, sem_in, sb_in, psum, ctx_main, v_last_rows, wk_hi, wk_lo, wv_hi, wv_lo,
                    k_last_hi, k_last_lo, ident, heads_hi, heads_lo, late_w, late_hi, late_lo, contexts,
                    SCALE):
    BATCH, _, KC, S = ctx_main.shape
    D = wk_hi.shape[2]
    L = heads_hi.shape[2] // BATCH
    HPG = P // 32
    ST = S // P
    KW = S + 8
    QUADS = BATCH // 4
    LATE = late_w.shape[0]

    c_raw, c_hi, c_lo, ctx_landed, c_hi_done, c_lo_done = contexts

    with ExitStack() as ctx:
        kT_hi = [sb_in(ctx, f"kT_hi{r}", [P, KC, 2, KW], F16) for r in range(2)]
        kT_lo = [sb_in(ctx, f"kT_lo{r}", [P, KC, 2, KW], F16) for r in range(2)]
        late_raw = sb_in(ctx, "late_raw", [P, 1, KC * D])
        v_hi = [sb_in(ctx, f"v_hi{u}", [P, ST, D], F16) for u in range(2)]
        v_lo = [sb_in(ctx, f"v_lo{u}", [P, ST, D], F16) for u in range(2)]
        bd_hi = sb_in(ctx, "bd_hi", [P, KC, HPG, L], F16)
        bd_lo = sb_in(ctx, "bd_lo", [P, KC, HPG, L], F16)
        e = sb_in(ctx, "e", [P, KC, S + 1])
        pT_hi = sb_in(ctx, "pT_hi", [P, ST, D], F16)
        pT_lo = sb_in(ctx, "pT_lo", [P, ST, D], F16)
        row_max = sb_in(ctx, "row_max", [P, KC])
        neg_max = sb_in(ctx, "neg_max", [P, KC])
        sums = sb_in(ctx, "sums", [P, KC])
        inv = sb_in(ctx, "inv", [P, KC])
        v_rep = [sb_in(ctx, f"v_rep{u}", [P, KC, 32]) for u in range(2)]
        last_part = sb_in(ctx, "last_part", [P, KC, 32])
        o_sum = sb_in(ctx, "o_sum", [P, KC, 32])
        o_norm = sb_in(ctx, "o_norm", [P, KC, 32])
        o_T = sb_in(ctx, "o_T", [P, KC, 32])

        rep_landed = [sem_in(ctx, f"rep_landed{u}") for u in range(2)]
        late_landed = sem_in(ctx, "late_landed")
        late_hi_done = sem_in(ctx, "late_hi_done")
        late_lo_done = sem_in(ctx, "late_lo_done")
        names = ["bd_clear", "bd_ready", "k_col", "last_done", "k_ps", "v_ps",
                 "s_ps", "p_ps", "pv_ps", "k_hi_done", "k_lo_done", "v_hi_done", "v_lo_done", "max_done",
                 "neg_done", "e_done", "pT_hi_done", "pT_lo_done", "inv_done", "o_sum_done",
                 "o_norm_done", "o_T_done", "o_hi_done", "o_lo_done"]
        (bd_clear, bd_ready, k_col, last_done, k_ps, v_ps, s_ps, p_ps, pv_ps,
         k_hi_done, k_lo_done, v_hi_done, v_lo_done, max_done, neg_done, e_done, pT_hi_done, pT_lo_done,
         inv_done, o_sum_done, o_norm_done, o_T_done, o_hi_done, o_lo_done) = [sem_in(ctx, n) for n in names]

        def k_bank(m):
            return psum[:, 4 + m % 2, :].rearrange("p (e s) -> p e s", e=2)

        def v_bank(t):
            return psum[:, 6 + t, :]

        scores = psum[:, 0:KC, 0:S + 1]
        out_bank = psum[:, 3, :].rearrange("p (g n) -> p g n", g=KC)

        block = ctx.enter_context(nc.Block())

        late_hi_w = late_hi.rearrange("p w c n -> p w (c n)")
        late_lo_w = late_lo.rearrange("p w c n -> p w (c n)")

        @block.sync
        def _(sp):
            def load_last(b, u):
                past(sp, last_done, b - 1)
                for h in range(HPG):
                    sp.dma_start(v_rep[u % 2][h * L:(h + 1) * L, :, :].rearrange("p g d -> p (g d)"),
                                 v_last_rows[bass.ds(b, 1), h * P:(h + 1) * P].to_broadcast([L, P])
                                 ).then_inc(rep_landed[u % 2], 16)

            def load_late(n):
                past(sp, late_lo_done, KC * n)
                sp.dma_start(late_raw[:, :, :], late_w[bass.ds(n, 1)].rearrange("o p n -> p o n")
                             ).then_inc(late_landed, 16)

            def quad(i, late=False, end=False):
                if late:
                    load_late(i)
                for u in range(4):
                    b = i * 4 + u
                    if not end or b + 6 < BATCH:
                        load_context(nc, sp, ctx_main, contexts, b + 6, u)
                    if not end or b + 2 < BATCH:
                        load_last(b + 2, u)
            for b in range(2):
                load_last(b, b)
            with sp.Fori(0, LATE) as i:
                quad(i, late=True)
            with sp.Fori(LATE, QUADS - 2) as i:
                quad(i)
            quad(QUADS - 2, end=True)
            quad(QUADS - 1, end=True)

        @block.gpsimd
        def _(pool):
            nc.gpsimd.memset(bd_hi[:, :, :, :], 0.0).then_inc(bd_clear, 1)
            nc.gpsimd.memset(bd_lo[:, :, :, :], 0.0).then_inc(bd_clear, 1)
            pool.wait_ge(bd_clear, 2)

            def spread(b, contexts):
                past(pool, s_ps, b)
                past(pool, c_lo_done, contexts)
                if isinstance(b, int) and b > 0:
                    pool.wait_ge(last_done, b - 1)
                    pool.wait_ge(k_col, 2 * (b // 2 + 1))
                for h in range(HPG):
                    rows = slice(32 * h, 32 * h + 32)
                    nc.gpsimd.tensor_copy(bd_hi[rows, :, h, :],
                                          heads_hi[rows, :, bass.ds(b * L, L)]).then_inc(bd_ready, 1)
                    nc.gpsimd.tensor_copy(bd_lo[rows, :, h, :],
                                          heads_lo[rows, :, bass.ds(b * L, L)]).then_inc(bd_ready, 1)

            def last_keys(b, r):
                past(pool, s_ps, b - 2)
                for k_last, kT in ((k_last_hi, kT_hi), (k_last_lo, kT_lo)):
                    nc.gpsimd.tensor_copy(kT[r][:, :, :, S], k_last[:, :, bass.ds(b, 2)]).then_inc(k_col, 1)

            def last_token(i, u, more=True):
                b = i * 4 + u
                pool.wait_ge(bd_ready, 2 * HPG * (b + 2 if more else b + 1))
                pool.wait_ge(e_done, KC * (b + 1))
                pool.wait_ge(rep_landed[u % 2], 16 * HPG * (i * 2 + u // 2 + 1))
                past(pool, o_sum_done, HPG * b)
                nc.gpsimd.tensor_tensor(last_part[:, :, :], v_rep[u % 2][:, :, :],
                                        e[:, :, S:S + 1].to_broadcast([P, KC, 32]),
                                        ALU.mult).then_inc(last_done, 1)

            def step(i, u, more=True, keys=True, ahead=True):
                b = i * 4 + u
                if more:
                    spread(b + 1, b + 4 if ahead else BATCH)
                last_token(i, u, more)
                if keys and u % 2 == 0:
                    last_keys(b + 2, 1 - u // 2)
                if ahead:
                    low_context(nc, pool, contexts, b + 4, u)

            spread(0, 0)
            pool.wait_ge(bd_ready, 2 * HPG)
            last_keys(0, 0)
            with pool.Fori(0, QUADS - 1) as i:
                for u in range(4):
                    step(i, u)
            for u in range(4):
                step(QUADS - 1, u, more=u < 3, keys=u < 2, ahead=False)

        @block.scalar
        def _(act):
            def high_context(b, u, count):
                act.wait_ge(ctx_landed[u % 2], 16 * count)
                past(act, v_ps, ST * (b - 3))
                nc.scalar.copy(c_hi[u // 2][:, :, u % 2, :], c_raw[u % 2][:, :, :]).then_inc(c_hi_done, 1)

            def high_keys(pair, r, m):
                act.wait_ge(k_ps, KC * pair + m + 1)
                nc.scalar.mul(kT_hi[r][:, m, :, 0:S], k_bank(m), W_UNSCALE).then_inc(k_hi_done, 1)

            def high_values(b, u, t):
                act.wait_ge(v_ps, ST * b + t + 1)
                nc.scalar.mul(v_hi[u][:, t, :], v_bank(t), W_UNSCALE).then_inc(v_hi_done, 1)

            def exponentials(b):
                act.wait_ge(neg_done, b + 1)
                past(act, last_done, b)
                for g in range(KC):
                    nc.scalar.activation(e[:, g, :], psum[:, g, 0:S + 1], ACT.Exp, bias=neg_max[:, g:g + 1],
                                         scale=SCALE, accum_out=sums[:, g:g + 1]).then_inc(e_done, 1)

            def high_probs(b):
                for t in range(ST):
                    act.wait_ge(p_ps, ST * b + t + 1)
                    nc.scalar.copy(pT_hi[:, t, :], psum[:, t, :]).then_inc(pT_hi_done, 1)

            def high_output(b):
                act.wait_ge(o_T_done, b + 1)
                nc.scalar.copy(heads_hi[:, :, bass.ds(b * L, L)], o_T[:, :, :]).then_inc(o_hi_done, 1)

            def high_late(n, c):
                act.wait_ge(late_landed, 16 * (n + 1))
                nc.scalar.mul(late_hi_w[:, bass.ds(n, 1), c * D:(c + 1) * D],
                              late_raw[:, :, c * D:(c + 1) * D], W_SCALE).then_inc(late_hi_done, 1)

            def step(i, u, more=True, keys=True, ahead=True):
                b = i * 4 + u
                exponentials(b)
                if keys:
                    for m in (2 * (u % 2), 2 * (u % 2) + 1):
                        high_keys(i * 2 + u // 2 + 1, 1 - u // 2, m)
                elif more:
                    high_values(b + 1, (u + 1) % 2, 0)
                high_probs(b)
                if ahead:
                    high_context(b + 4, u, (i + 1) * 2 + u // 2 + 1)
                if keys:
                    high_values(b + 1, (u + 1) % 2, 0)
                if more:
                    high_values(b + 1, (u + 1) % 2, 1)
                high_output(b)

            for m in range(KC):
                high_keys(0, 0, m)
            for t in range(ST):
                high_values(0, 0, t)
            with act.Fori(0, LATE) as i:
                for u in range(4):
                    step(i, u)
                    high_late(i, u)
            with act.Fori(LATE, QUADS - 1) as i:
                for u in range(4):
                    step(i, u)
            for u in range(4):
                step(QUADS - 1, u, more=u < 3, keys=u < 2, ahead=False)

        @block.vector
        def _(dve):
            def maxima(b):
                dve.wait_ge(s_ps, b + 1)
                nc.vector.reduce_max(row_max[:, :], scores, AX.X).then_inc(max_done, 1)
                dve.wait_ge(max_done, b + 1)
                nc.vector.tensor_scalar(neg_max[:, :], row_max[:, :], -SCALE, EXP_SHIFT, ALU.mult,
                                        ALU.add).then_inc(neg_done, 1)

            def low_keys(pair, r, m):
                dve.wait_ge(k_hi_done, KC * pair + m + 1)
                nc.vector.scalar_tensor_tensor(
                    out=kT_lo[r][:, m, :, 0:S], in0=k_bank(m), scalar=W_UNSCALE,
                    in1=kT_hi[r][:, m, :, 0:S], op0=ALU.mult, op1=ALU.subtract).then_inc(k_lo_done, 1)

            def low_values(b, u, t):
                dve.wait_ge(v_hi_done, ST * b + t + 1)
                nc.vector.scalar_tensor_tensor(
                    out=v_lo[u][:, t, :], in0=v_bank(t), scalar=W_UNSCALE, in1=v_hi[u][:, t, :],
                    op0=ALU.mult, op1=ALU.subtract).then_inc(v_lo_done, 1)

            def low_probs(b):
                for t in range(ST):
                    dve.wait_ge(pT_hi_done, ST * b + t + 1)
                    nc.vector.tensor_tensor(pT_lo[:, t, :], psum[:, t, :], pT_hi[:, t, :],
                                            ALU.subtract).then_inc(pT_lo_done, 1)

            def inverse(b):
                dve.wait_ge(e_done, KC * (b + 1))
                nc.vector.reciprocal(inv[:, :], sums[:, :]).then_inc(inv_done, 1)

            def gather_output(b):
                dve.wait_ge(pv_ps, b + 1)
                dve.wait_ge(last_done, b + 1)
                for h in range(HPG):
                    rows = slice(32 * h, 32 * h + 32)
                    nc.vector.tensor_tensor(o_sum[rows, :, :], out_bank[rows, :, 32 * h:32 * h + 32],
                                            last_part[rows, :, :], ALU.add).then_inc(o_sum_done, 1)

            def finish_output(b):
                dve.wait_ge(o_sum_done, HPG * (b + 1))
                dve.wait_ge(inv_done, b + 1)
                nc.vector.tensor_tensor(o_norm[:, :, :], o_sum[:, :, :],
                                        inv[:, :].unsqueeze(2).to_broadcast([P, KC, 32]),
                                        ALU.mult).then_inc(o_norm_done, 1)
                dve.wait_ge(o_norm_done, b + 1)
                past(dve, o_hi_done, b)
                past(dve, o_lo_done, b)
                nc.vector.transpose(o_T[:, :, :], o_norm[:, :, :]).then_inc(o_T_done, 1)

            def low_output(b):
                dve.wait_ge(o_hi_done, b + 1)
                nc.vector.tensor_tensor(heads_lo[:, :, bass.ds(b * L, L)], o_T[:, :, :],
                                        heads_hi[:, :, bass.ds(b * L, L)], ALU.subtract).then_inc(o_lo_done, 1)

            def low_late(n, c):
                dve.wait_ge(late_hi_done, KC * n + c + 1)
                cols = slice(c * D, (c + 1) * D)
                nc.vector.scalar_tensor_tensor(
                    out=late_lo_w[:, bass.ds(n, 1), cols], in0=late_raw[:, :, cols], scalar=W_SCALE,
                    in1=late_hi_w[:, bass.ds(n, 1), cols], op0=ALU.mult,
                    op1=ALU.subtract).then_inc(late_lo_done, 1)

            def step(i, u, more=True, keys=True):
                b = i * 4 + u
                maxima(b)
                if keys:
                    for m in (2 * (u % 2), 2 * (u % 2) + 1):
                        low_keys(i * 2 + u // 2 + 1, 1 - u // 2, m)
                elif more:
                    low_values(b + 1, (u + 1) % 2, 0)
                low_probs(b)
                inverse(b)
                if keys:
                    low_values(b + 1, (u + 1) % 2, 0)
                gather_output(b)
                finish_output(b)
                if more:
                    low_values(b + 1, (u + 1) % 2, 1)
                low_output(b)

            for m in range(KC):
                low_keys(0, 0, m)
            for t in range(ST):
                low_values(0, 0, t)
            with dve.Fori(0, LATE) as i:
                for u in range(4):
                    step(i, u)
                    low_late(i, u)
            with dve.Fori(LATE, QUADS - 1) as i:
                for u in range(4):
                    step(i, u)
            for u in range(4):
                step(QUADS - 1, u, more=u < 3, keys=u < 2)

        @block.tensor
        def _(pe):
            def run(bank, steps):
                for n, (a, b) in enumerate(steps):
                    mm = nc.tensor.matmul(bank, a, b, start=(n == 0), stop=(n == len(steps) - 1))
                return mm

            def keys(pair, r, m):
                pe.wait_ge(c_lo_done, 2 * pair + 2)
                past(pe, k_lo_done, KC * pair + m - 1)
                run(k_bank(m), [(w[:, k, m * P:(m + 1) * P], c[:, k, :, :]) for k in range(KC)
                                for w, c in passes(wk_hi, wk_lo, c_hi[r], c_lo[r])]).then_inc(k_ps, 1)

            def values(b, u, t):
                past(pe, v_lo_done, ST * (b - 1) + t + 1)
                rows = slice(t * P, (t + 1) * P)
                run(v_bank(t), [(c[:, k, u % 2, rows], w[:, k, :]) for k in range(KC)
                                for c, w in passes(c_hi[u // 2], c_lo[u // 2], wv_hi, wv_lo)]
                    ).then_inc(v_ps, 1)

            def score(i, u):
                b = i * 4 + u
                pe.wait_ge(bd_ready, 2 * HPG * (b + 1))
                pe.wait_ge(k_col, 2 * (i * 2 + u // 2 + 1))
                pe.wait_ge(k_lo_done, KC * (i * 2 + u // 2 + 1))
                past(pe, pT_lo_done, ST * b)
                past(pe, o_sum_done, HPG * b)
                for g in range(KC):
                    mm = run(psum[:, g, 0:S + 1],
                             [(q[:, g, :, :].rearrange("p h l -> p (h l)"), k[u // 2][:, g, u % 2, 0:S + 1])
                              for q, k in passes(bd_hi, bd_lo, kT_hi, kT_lo)])
                mm.then_inc(s_ps, 1)

            def probs(b):
                pe.wait_ge(e_done, KC * (b + 1))
                for t in range(ST):
                    for g in range(KC):
                        mm = nc.tensor.transpose(psum[:, t, g * P:(g + 1) * P], e[:, g, t * P:(t + 1) * P],
                                                 ident[:, :])
                    mm.then_inc(p_ps, 1)

            def outputs(b, u):
                pe.wait_ge(pT_lo_done, ST * (b + 1))
                pe.wait_ge(v_lo_done, ST * (b + 1))
                for g in range(KC):
                    cols = slice(g * P, (g + 1) * P)
                    mm = run(out_bank[:, g, :], [(p[:, t, cols], v[:, t, cols]) for t in range(ST)
                                                 for p, v in passes(pT_hi, pT_lo, v_hi[u % 2], v_lo[u % 2])])
                mm.then_inc(pv_ps, 1)

            def step(i, u, more=True, key=True):
                b = i * 4 + u
                score(i, u)
                if key:
                    for m in (2 * (u % 2), 2 * (u % 2) + 1):
                        keys(i * 2 + u // 2 + 1, 1 - u // 2, m)
                elif more:
                    values(b + 1, (u + 1) % 4, 0)
                probs(b)
                if key:
                    values(b + 1, (u + 1) % 4, 0)
                outputs(b, u)
                if more:
                    values(b + 1, (u + 1) % 4, 1)

            for m in range(KC):
                keys(0, 0, m)
            values(0, 0, 0)
            values(0, 0, 1)
            with pe.Fori(0, QUADS - 1) as i:
                for u in range(4):
                    step(i, u)
            for u in range(4):
                step(QUADS - 1, u, more=u < 3, key=u < 2)


def token_stages(nc, sem_in, sb_in, psum, x, bo, bq, bk, bv, b1, b2, w1_t, w2_t, late_hi, late_lo,
                 ident, ones, heads_hi, heads_lo, SCALE, out):
    TOKENS, D = x.shape
    HID = w1_t.shape[1]
    KC, NJ = D // P, HID // P
    T = 2
    GROUP = T * P
    NG = TOKENS // GROUP
    BT = 32
    BPT = P // BT
    LAG = 2
    AR = LAG + 1
    RING = 3
    PIECE = 2 * D
    x_rows = x.rearrange("(t p) d -> p t d", p=P)
    out_rows = out.rearrange("(t p) d -> p t d", p=P)

    with ExitStack() as ctx:
        sign1 = sb_in(ctx, "sign1", [P, KC, HID], F16)
        sign2 = sb_in(ctx, "sign2", [P, NJ, D], F16)
        alpha1 = sb_in(ctx, "alpha1", [P, NJ])
        alpha2_row = sb_in(ctx, "alpha2_row", [P, D])
        sum1 = sb_in(ctx, "sum1", [P, NJ])
        raw = [sb_in(ctx, f"ffn_raw{r}", [P, PIECE]) for r in range(RING - 1)]
        xb = sb_in(ctx, "xb", [P, T, D])
        res = [sb_in(ctx, f"res{u}", [P, T, D]) for u in range(2)]
        xn = sb_in(ctx, "xn", [P, T, D])
        at_hi = sb_in(ctx, "at_hi", [P, KC, GROUP], F16)
        at_lo = sb_in(ctx, "at_lo", [P, KC, GROUP], F16)
        x2T_hi = sb_in(ctx, "x2T_hi", [P, KC, GROUP], F16)
        x2T_lo = sb_in(ctx, "x2T_lo", [P, KC, GROUP], F16)
        x3T_hi = sb_in(ctx, "x3T_hi", [P, KC, GROUP], F16)
        x3T_lo = sb_in(ctx, "x3T_lo", [P, KC, GROUP], F16)
        qk = [sb_in(ctx, f"qk{r}", [P, 2, GROUP]) for r in range(2)]
        qk_hi = sb_in(ctx, "qk_hi", [P, 2 * KC, GROUP], F16)
        qk_lo = sb_in(ctx, "qk_lo", [P, 2 * KC, GROUP], F16)
        val = sb_in(ctx, "val", [P, D])
        val_hi = sb_in(ctx, "val_hi", [P, T, D], F16)
        val_lo = sb_in(ctx, "val_lo", [P, T, D], F16)
        act = [sb_in(ctx, f"gelu{r}", [P, GROUP]) for r in range(AR)]
        act_hi = [sb_in(ctx, f"gelu_hi{r}", [P, GROUP], F16) for r in range(AR)]
        act_lo = [sb_in(ctx, f"gelu_lo{r}", [P, GROUP], F16) for r in range(AR)]
        res_out = [sb_in(ctx, f"res_out{t}", [P, D]) for t in range(T)]
        raw.append(res[1][:, :, :].rearrange("p t d -> p (t d)"))
        mag = res_out + [alpha2_row]
        diagonal = act[0][:, :].rearrange("p (h n) -> p h n", n=P)
        bo_row = sb_in(ctx, "bo_row", [P, D])
        bv_row = sb_in(ctx, "bv_row", [P, D])
        b2_row = sb_in(ctx, "b2_row", [P, D])
        bqk_col = sb_in(ctx, "bqk_col", [P, 2 * KC])
        b1_col = sb_in(ctx, "b1_col", [P, NJ])
        zeros = sb_in(ctx, "zeros", [P, BT])
        mask = sb_in(ctx, "mask", [P, BT])
        half = sb_in(ctx, "neg_half", [P, T])
        stats = sb_in(ctx, "stats_c", [P, T, 6])
        both = sb_in(ctx, "both_c", [P, T, 2])
        diff = sb_in(ctx, "diff_c", [P, T])
        mean = sb_in(ctx, "mean_c", [P, T])
        var_eps = sb_in(ctx, "var_eps_c", [P, T])
        rstd = sb_in(ctx, "rstd_c", [P, T])
        sc = sb_in(ctx, "sc", [P, T, BT])
        row = sb_in(ctx, "row", [P, T])
        spread = sb_in(ctx, "spread", [P, T, BT])
        across = sb_in(ctx, "across", [P, T, BT])
        neg_max = sb_in(ctx, "neg_max_c", [P, T])
        ex = sb_in(ctx, "ex", [P, T, BT])
        ex_sum = sb_in(ctx, "ex_sum", [P, T])
        ex_T = sb_in(ctx, "ex_T", [P, T, BT])
        total = sb_in(ctx, "total", [P, T])
        inv_total = sb_in(ctx, "inv_total", [P, T])
        w_hi = sb_in(ctx, "w_hi", [P, T, P], F16)
        w_lo = sb_in(ctx, "w_lo", [P, T, P], F16)

        names = ["consts_landed", "x_landed", "pool_const", "mask_done", "xb_done", "at_done", "b2_added",
                 "rstd2_done", "rstd3_done", "wo_ps", "t2_ps", "t3_ps", "qk_ps", "val_ps", "sc_ps", "pv_ps",
                 "h_ps", "f_ps", "x2T_hi_done", "x2T_lo_done", "x3T_hi_done", "x3T_lo_done", "qk_done",
                 "qk_hi_done", "qk_lo_done", "val_done", "val_hi_done", "val_lo_done", "x1_done", "x2_done",
                 "stats2_done", "stats3_done", "merged2", "merged3", "eps2_done", "eps3_done",
                 "norm2_done", "norm3_done", "sc_done", "chain", "neg_done", "ex_done", "inv_done",
                 "ex_T_done", "w_hi_done", "w_done", "gelu_done", "gelu_hi_done", "gelu_lo_done",
                 "scaled_done", "out_done", "out_stored0", "out_stored1"]
        s = {n: sem_in(ctx, n + "_c") for n in names}
        stored = [s["out_stored0"], s["out_stored1"]]
        late = {name: (late_hi[:, w], late_lo[:, w]) for w, name in enumerate(("xWo", "sWq", "sWk", "sWv"))}
        landed = [sem_in(ctx, f"ffn_landed{r}") for r in range(RING)]
        sign_done = sem_in(ctx, "sign_done")
        mag_done = sem_in(ctx, "mag_done")
        added = sem_in(ctx, "added")
        diag_done = sem_in(ctx, "diag_done")
        sum1_done = sem_in(ctx, "sum1_done")
        alpha1_done = sem_in(ctx, "alpha1_done")
        alpha2_done = sem_in(ctx, "alpha2_done")
        NW = D * HID // (P * PIECE)
        SPLIT_SLOTS = {5: (0, 1, 2), 6: (3,), 7: (4,), 8: (5, 6), 9: (7,), 10: (8,), 11: (9,),
                       12: (10, 11), 13: (12, 13), 14: (14,), 15: (15,)}
        SUM_SLOTS = {6: (0,), 7: (1,), 8: (2, 3), 9: (4,), 10: (5,), 11: (6,), 12: (7, 8), 13: (9, 10),
                     14: (11,), 15: (12, 13, 14, 15)}
        WH = HID // NW
        pieces = ([w1_t.rearrange("(c p) n -> p c n", p=P)[:, :, j * WH:(j + 1) * WH] for j in range(NW)]
                  + [w2_t.rearrange("(j p) n -> p j n", p=P)[:, 2 * j:2 * j + 2, :] for j in range(NW)])

        def sign_of(j):
            return sign1[:, :, j * WH:(j + 1) * WH] if j < NW else sign2[:, 2 * (j - NW):2 * (j - NW) + 2, :]

        def piece(n):
            return raw[n % RING][:, 0:PIECE].rearrange("p (j n) -> p j n", j=KC if n < NW else 2)

        sum_bank = psum[:, 0, :]

        def sum1_bank(j):
            return psum[:, 1 + j % 2, 0:WH]

        CHAIN = 5

        def f_bank(t):
            return psum[:, t, :]

        def h_bank(j):
            return psum[:, 2 + j % 2, 0:GROUP]

        def g_bank(n):
            return psum[:, 4 + n, :]

        def chunks(bank, c):
            return bank.rearrange("p (c n) -> p c n", c=c)

        QK_BANK = (2, 3, 0, 1)
        sc_bank = g_bank(0)[:, 0:T * P].rearrange("p (t n) -> p t n", t=T)

        def has_tail(n):
            return not (isinstance(n, int) and n < 2)

        def rounds(engine, one):
            one(0, 0, front=True, ffn=False)
            for n in range(1, 4):
                one(n, n % 2, front=True, ffn=True)
            with engine.Fori(2, NG // 2 - 1) as i:
                one(i * 2, 0, front=True, ffn=True)
                one(i * 2 + 1, 1, front=True, ffn=True)
            one(NG - 2, 0, front=True, ffn=True)
            one(NG - 1, 1, front=True, ffn=True)
            one(NG, 0, front=False, ffn=True)

        block = ctx.enter_context(nc.Block())

        @block.sync
        def _(sp):
            def load(n):
                past(sp, s["x1_done"], T * n)
                sp.dma_start(xb[:, :, :], x_rows[:, bass.ds(n * T, T), :]).then_inc(s["x_landed"], 16)

            def store(g):
                for t in range(T):
                    sp.wait_ge(s["out_done"], g * T + t + 1)
                    sp.dma_start(out_rows[:, bass.ds(g * T + t, 1), :],
                                 res_out[t][:, :].unsqueeze(1)).then_inc(stored[t], 16)

            def one(n, u, front, ffn):
                if has_tail(n):
                    store(n - 2)
                if not (isinstance(n, int) and (n >= NG - 1 or n == 0)):
                    load(n + 1)
            load(0)
            sp.dma_start(bo_row[:, :], bo.to_broadcast([P, D])).then_inc(s["consts_landed"], 16)
            for dst, src in ((bqk_col[:, 0:KC], bq), (bqk_col[:, KC:], bk), (b1_col[:, :], b1)):
                sp.dma_start(dst, src).then_inc(s["consts_landed"], 16)
            for dst, src in ((bv_row, bv), (b2_row, b2)):
                sp.dma_start(dst[:, :], src.to_broadcast([P, D])).then_inc(s["consts_landed"], 16)
            def stage_pieces(first, last):
                for n in range(first, last):
                    past(sp, sign_done, n - RING + 1)
                    past(sp, mag_done, n - RING + 1)
                    sp.dma_start(piece(n), pieces[n]).then_inc(landed[n % RING], 16)
            stage_pieces(0, 4)
            load(1)
            stage_pieces(4, len(pieces))
            rounds(sp, one)
            store(NG - 1)
            for t in range(T):
                sp.wait_ge(stored[t], 16 * NG)

        @block.gpsimd
        def _(pool):
            def stage_heads(n):
                pool.wait_ge(s["wo_ps"], T * n)
                for src, dst in ((heads_hi, at_hi), (heads_lo, at_lo)):
                    nc.gpsimd.tensor_copy(dst[:, :, :], src[:, :, bass.ds(n * GROUP, GROUP)]
                                          ).then_inc(s["at_done"], 1)

            def stage_input(n):
                pool.wait_ge(s["x_landed"], 16 * (n + 1))
                nc.gpsimd.tensor_tensor(xb[:, :, :], xb[:, :, :],
                                        bo_row[:, :].unsqueeze(1).to_broadcast([P, T, D]),
                                        ALU.add).then_inc(s["xb_done"], 1)

            def power(n, eps_done, rstd_done):
                pool.wait_ge(eps_done, n + 1)
                nc.gpsimd.tensor_tensor(rstd[:, :], var_eps[:, :], half[:, :], ALU.pow).then_inc(rstd_done, 1)

            def one(n, u, front, ffn):
                if not front:
                    return
                power(n, s["eps2_done"], s["rstd2_done"])
                if not (isinstance(n, int) and n == NG - 1):
                    stage_heads(n + 1)
                    stage_input(n + 1)
                power(n, s["eps3_done"], s["rstd3_done"])
                pool.wait_ge(s["norm3_done"], T * (n + 1))
                nc.gpsimd.tensor_tensor(res[u][:, :, :], res[u][:, :, :],
                                        b2_row[:, :].unsqueeze(1).to_broadcast([P, T, D]),
                                        ALU.add).then_inc(s["b2_added"], 1)
            nc.gpsimd.memset(half[:, :], -0.5).then_inc(s["pool_const"], 1)
            pool.wait_ge(s["consts_landed"], 16 * 6)
            stage_input(0)
            nc.gpsimd.memset(zeros[:, :], 0.0).then_inc(s["pool_const"], 1)
            nc.gpsimd.memset(w_hi[:, :, :], 0.0).then_inc(s["pool_const"], 1)
            nc.gpsimd.memset(w_lo[:, :, :], 0.0).then_inc(s["pool_const"], 1)
            pool.wait_ge(s["pool_const"], 4)
            pool.wait_ge(s["xb_done"], 1)
            for b in range(BPT):
                rows = slice(BT * b, BT * b + BT)
                nc.gpsimd.affine_select(out=mask[rows, :], in_=zeros[rows, :], compare_op=ALU.is_ge,
                                        fill=MASKED, base=0, pattern=[[-1, BT]],
                                        channel_multiplier=1).then_inc(s["mask_done"], 1)
            pool.wait_ge(s["mask_done"], BPT)
            rounds(pool, one)

        @block.scalar
        def _(eng):
            def high_T(bank_ready, dst, done, n):
                for t in range(T):
                    eng.wait_ge(bank_ready, T * n + t + 1)
                    nc.scalar.copy(dst[:, :, t * P:(t + 1) * P], chunks(g_bank(t), KC)).then_inc(done, 1)

            def hidden(g, j):
                eng.wait_ge(s["h_ps"], NJ * g + j + 1)
                nc.scalar.activation(act[j % AR][:, :], h_bank(j), ACT.Gelu, bias=b1_col[:, j:j + 1],
                                     scale=alpha1[:, j:j + 1]).then_inc(s["gelu_done"], 1)
                eng.wait_ge(s["gelu_done"], NJ * g + j + 1)
                nc.scalar.copy(act_hi[j % AR][:, :], act[j % AR][:, :]).then_inc(s["gelu_hi_done"], 1)

            def prepare(j):
                eng.wait_ge(landed[j % RING], 16 * (j // RING + 1))
                nc.scalar.activation(sign_of(j), piece(j), ACT.Sign).then_inc(sign_done, 1)

            def one(n, u, front, ffn):
                g = n - 1

                def F(*js):
                    for j in js:
                        if ffn:
                            hidden(g, j)
                        else:
                            for piece_nr in SPLIT_SLOTS.get(j, ()):
                                prepare(piece_nr)
                F(0, 1, 2, 3, 4)
                if front:
                    high_T(s["t2_ps"], x2T_hi, s["x2T_hi_done"], n)
                F(5)
                if front:
                    if isinstance(n, int) and n == 0:
                        eng.wait_ge(s["consts_landed"], 16 * 6)
                    for r in range(4):
                        eng.wait_ge(s["qk_ps"], 4 * n + r + 1)
                        past(eng, s["qk_lo_done"], 4 * n + r - 1)
                        for c in range(2):
                            last = nc.scalar.activation(
                                qk[r % 2][:, c, :], chunks(g_bank(QK_BANK[r]), 2)[:, c, :], ACT.Identity,
                                bias=bqk_col[:, 2 * r + c:2 * r + c + 1], scale=W_UNSCALE)
                        last.then_inc(s["qk_done"], 1)
                F(6, 7)
                if front:
                    eng.wait_ge(s["neg_done"], n + 1)
                    for t in range(T):
                        nc.scalar.activation(ex[:, t, :], sc[:, t, :], ACT.Exp, bias=neg_max[:, t:t + 1],
                                             accum_out=ex_sum[:, t:t + 1]).then_inc(s["ex_done"], 1)
                F(*range(8, NJ))
                if front:
                    past(eng, s["h_ps"], NJ * n)
                    high_T(s["t3_ps"], x3T_hi, s["x3T_hi_done"], n)
                if not ffn:
                    eng.wait_ge(added, 2 * NW)
                    nc.scalar.mul(alpha2_row[:, :], sum_bank, 1.0 / HID).then_inc(alpha2_done, 1)
                    eng.wait_ge(alpha1_done, 1)
            nc.scalar.copy(at_hi[:, :, :], heads_hi[:, :, 0:GROUP]).then_inc(s["at_done"], 1)
            rounds(eng, one)

        @block.vector
        def _(dve):
            def low_T(hi_done, hi, lo, done, n):
                for t in range(T):
                    dve.wait_ge(hi_done, T * n + t + 1)
                    nc.vector.tensor_tensor(lo[:, :, t * P:(t + 1) * P], chunks(g_bank(t), KC),
                                            hi[:, :, t * P:(t + 1) * P], ALU.subtract).then_inc(done, 1)

            def hidden(g, j):
                dve.wait_ge(s["gelu_hi_done"], NJ * g + j + 1)
                nc.vector.tensor_tensor(act_lo[j % AR][:, :], act[j % AR][:, :], act_hi[j % AR][:, :],
                                        ALU.subtract).then_inc(s["gelu_lo_done"], 1)

            def statistics(n, u, k):
                for t in range(T):
                    dve.wait_ge(s["x1_done" if k == 2 else "x2_done"], T * n + t + 1)
                    nc.vector.bn_stats(stats[:, t, :], res[u][:, t, :]).then_inc(s[f"stats{k}_done"], 1)
                merge_statistics(nc, dve, n, stats, both[:, :, :], diff[:, :], mean[:, :], var_eps[:, :],
                                 s[f"stats{k}_done"], T * (n + 1), s[f"merged{k}"], s[f"eps{k}_done"])

            def normalise(n, u, k):
                dve.wait_ge(s[f"rstd{k}_done"], n + 1)
                if k == 2:
                    past(dve, s["t3_ps"], T * n)
                else:
                    dve.wait_ge(s["t2_ps"], T * (n + 1))
                for t in range(T):
                    nc.vector.tensor_scalar(xn[:, t, :], res[u][:, t, :], mean[:, t:t + 1],
                                            rstd[:, t:t + 1], ALU.subtract,
                                            ALU.mult).then_inc(s[f"norm{k}_done"], 1)

            def link(ins, value):
                ins.then_inc(s["chain"], 1)
                dve.wait_ge(s["chain"], value)

            def projections(n):
                for r in range(4):
                    cols = slice(2 * r, 2 * r + 2)
                    dve.wait_ge(s["qk_done"], 4 * n + r + 1)
                    nc.vector.tensor_copy(qk_hi[:, cols, :], qk[r % 2][:, :, :]).then_inc(s["qk_hi_done"], 1)
                    dve.wait_ge(s["qk_hi_done"], 4 * n + r + 1)
                    nc.vector.tensor_tensor(qk_lo[:, cols, :], qk[r % 2][:, :, :], qk_hi[:, cols, :],
                                            ALU.subtract).then_inc(s["qk_lo_done"], 1)

            def split_values(n, *tiles):
                for t in tiles:
                    dve.wait_ge(s["val_ps"], T * n + t + 1)
                    past(dve, s["val_lo_done"], T * n + t)
                    nc.vector.scalar_tensor_tensor(out=val[:, :], in0=g_bank(2 + t), scalar=W_UNSCALE,
                                                   in1=bv_row[:, :], op0=ALU.mult,
                                                   op1=ALU.add).then_inc(s["val_done"], 1)
                    dve.wait_ge(s["val_done"], T * n + t + 1)
                    nc.vector.tensor_copy(val_hi[:, t, :], val[:, :]).then_inc(s["val_hi_done"], 1)
                    dve.wait_ge(s["val_hi_done"], T * n + t + 1)
                    nc.vector.tensor_tensor(val_lo[:, t, :], val[:, :], val_hi[:, t, :],
                                            ALU.subtract).then_inc(s["val_lo_done"], 1)

            def maxima(n):
                dve.wait_ge(s["sc_ps"], n + 1)
                for b in range(BPT):
                    rows = slice(BT * b, BT * b + BT)
                    nc.vector.scalar_tensor_tensor(
                        out=sc[rows, :, :], in0=sc_bank[rows, :, BT * b:BT * b + BT], scalar=SCALE,
                        in1=mask[rows, :].unsqueeze(1).to_broadcast([BT, T, BT]), op0=ALU.mult,
                        op1=ALU.add).then_inc(s["sc_done"], 1)
                dve.wait_ge(s["sc_done"], BPT * (n + 1))
                link(nc.vector.reduce_max(row[:, :], sc[:, :, :], AX.X), CHAIN * n + 1)
                link(nc.vector.tensor_copy(spread[:, :, :], row[:, :].unsqueeze(2).to_broadcast([P, T, BT])),
                     CHAIN * n + 2)
                link(nc.vector.transpose(across[:, :, :], spread[:, :, :]), CHAIN * n + 3)
                link(nc.vector.reduce_max(row[:, :], across[:, :, :], AX.X), CHAIN * n + 4)
                nc.vector.tensor_scalar(neg_max[:, :], row[:, :], -1.0, EXP_SHIFT, ALU.mult,
                                        ALU.add).then_inc(s["neg_done"], 1)

            def weights(n):
                dve.wait_ge(s["ex_done"], T * (n + 1))
                nc.vector.transpose(ex_T[:, :, :], ex[:, :, :]).then_inc(s["ex_T_done"], 1)
                dve.wait_ge(s["ex_T_done"], n + 1)
                for b in range(BPT):
                    rows = slice(BT * b, BT * b + BT)
                    nc.vector.tensor_copy(w_hi[rows, :, rows], ex_T[rows, :, :]).then_inc(s["w_hi_done"], 1)
                for b in range(BPT):
                    rows = slice(BT * b, BT * b + BT)
                    dve.wait_ge(s["w_hi_done"], BPT * n + b + 1)
                    nc.vector.tensor_tensor(w_lo[rows, :, rows], ex_T[rows, :, :], w_hi[rows, :, rows],
                                            ALU.subtract).then_inc(s["w_done"], 1)

            def totals(n):
                link(nc.vector.tensor_copy(spread[:, :, :], ex_sum[:, :].unsqueeze(2).to_broadcast([P, T, BT])),
                     CHAIN * n + 5)
                nc.vector.transpose(across[:, :, :], spread[:, :, :]).then_inc(s["inv_done"], 1)
                dve.wait_ge(s["inv_done"], 3 * n + 1)
                nc.vector.reduce_sum(total[:, :], across[:, :, :], AX.X).then_inc(s["inv_done"], 1)
                dve.wait_ge(s["inv_done"], 3 * n + 2)
                nc.vector.reciprocal(inv_total[:, :], total[:, :]).then_inc(s["inv_done"], 1)

            def finish(g, u):
                dve.wait_ge(s["f_ps"], g + 1)
                for t in range(T):
                    past(dve, stored[t], 16 * g)
                    nc.vector.tensor_tensor(res_out[t][:, :], f_bank(t), alpha2_row[:, :],
                                            ALU.mult).then_inc(s["scaled_done"], 1)
                dve.wait_ge(s["b2_added"], g + 1)
                for t in range(T):
                    dve.wait_ge(s["scaled_done"], T * g + t + 1)
                    nc.vector.tensor_tensor(res_out[t][:, :], res_out[t][:, :], res[u][:, t, :],
                                            ALU.add).then_inc(s["out_done"], 1)

            def take_sums(j):
                dve.wait_ge(added, j + 1)
                past(dve, sum1_done, j)
                nc.vector.tensor_tensor(
                    diagonal[:, :, :], sum1_bank(j).rearrange("p (h n) -> p h n", n=P),
                    ident[:, :].unsqueeze(1).to_broadcast([P, WH // P, P]), ALU.mult).then_inc(diag_done, 1)
                dve.wait_ge(diag_done, j + 1)
                units = slice(j * (WH // P), (j + 1) * (WH // P))
                nc.vector.reduce_sum(sum1[:, units], diagonal[:, :, :], AX.X).then_inc(sum1_done, 1)

            def prepare(j):
                dve.wait_ge(landed[j % RING], 16 * (j // RING + 1))
                past(dve, added, j - 2)
                width = WH if j < NW else D
                nc.vector.tensor_reduce(mag[j % 3][:, 0:width], piece(j).rearrange("p j n -> p n j"), AX.X,
                                        ALU.add, apply_absolute_value=True).then_inc(mag_done, 1)
                if 3 <= j < NW + 3:
                    take_sums(j - 3)

            def one(n, u, front, ffn):
                g = n - 1

                def F(*js):
                    for j in js:
                        if ffn:
                            hidden(g, j)
                        else:
                            for piece_nr in SPLIT_SLOTS.get(j, ()):
                                prepare(piece_nr)
                if has_tail(n):
                    finish(n - 2, u)
                if front:
                    dve.wait_ge(s["xb_done"], n + 1)
                    past(dve, s["out_done"], T * (n - 1))
                    for t in range(T):
                        dve.wait_ge(s["wo_ps"], T * n + t + 1)
                        nc.vector.scalar_tensor_tensor(out=res[u][:, t, :], in0=g_bank(2 + t),
                                                       scalar=W_UNSCALE, in1=xb[:, t, :], op0=ALU.mult,
                                                       op1=ALU.add).then_inc(s["x1_done"], 1)
                F(0)
                if front:
                    statistics(n, u, 2)
                F(1)
                if front:
                    normalise(n, u, 2)
                F(2, 3, 4)
                if front:
                    low_T(s["x2T_hi_done"], x2T_hi, x2T_lo, s["x2T_lo_done"], n)
                F(5)
                if front:
                    projections(n)
                F(6, 7)
                if front:
                    if isinstance(n, int) and n == 0:
                        dve.wait_ge(s["mask_done"], BPT)
                        dve.wait_ge(s["consts_landed"], 16 * 6)
                    maxima(n)
                    weights(n)
                    split_values(n, 0)
                F(8)
                if front:
                    split_values(n, 1)
                F(9)
                if front:
                    totals(n)
                F(10, 11)
                if front:
                    dve.wait_ge(s["inv_done"], 3 * n + 3)
                    for t in range(T):
                        dve.wait_ge(s["pv_ps"], T * n + t + 1)
                        nc.vector.scalar_tensor_tensor(out=res[u][:, t, :], in0=g_bank(2 + t),
                                                       scalar=inv_total[:, t:t + 1], in1=res[u][:, t, :],
                                                       op0=ALU.mult, op1=ALU.add).then_inc(s["x2_done"], 1)
                F(12)
                if front:
                    statistics(n, u, 3)
                F(13)
                if front:
                    normalise(n, u, 3)
                F(14, 15)
                if front:
                    low_T(s["x3T_hi_done"], x3T_hi, x3T_lo, s["x3T_lo_done"], n)
                if not ffn:
                    dve.wait_ge(sum1_done, NW)
                    nc.vector.tensor_scalar(alpha1[:, :], sum1[:, :], 1.0 / D, None,
                                            ALU.mult).then_inc(alpha1_done, 1)
                    dve.wait_ge(alpha2_done, 1)
                    dve.wait_ge(sign_done, 2 * NW)
                    dve.wait_ge(mag_done, 2 * NW)
            nc.vector.tensor_copy(at_lo[:, :, :], heads_lo[:, :, 0:GROUP]).then_inc(s["at_done"], 1)
            rounds(dve, one)
            finish(NG - 1, (NG - 1) % 2)

        @block.tensor
        def _(pe):
            def run(bank, steps):
                for n, (a, b) in enumerate(steps):
                    mm = nc.tensor.matmul(bank, a, b, start=(n == 0), stop=(n == len(steps) - 1))
                return mm

            def transposes(n, norm_done, done):
                for t in range(T):
                    pe.wait_ge(norm_done, T * n + t + 1)
                    for c in range(KC):
                        mm = nc.tensor.transpose(chunks(g_bank(t), KC)[:, c, :], xn[:, t, c * P:(c + 1) * P],
                                                 ident[:, :])
                    mm.then_inc(done, 1)

            def layer1(g, j):
                past(pe, s["gelu_done"], NJ * g + j - 1)
                cols = slice(j * P, (j + 1) * P)
                run(h_bank(j), [(sign1[:, k, cols], x3[:, k, :]) for k in range(KC)
                                for x3 in (x3T_hi, x3T_lo)]).then_inc(s["h_ps"], 1)

            def layer2(g, j):
                pe.wait_ge(s["gelu_lo_done"], NJ * g + j + 1)
                if j == 0:
                    past(pe, s["scaled_done"], T * g)
                for t in range(T):
                    for n, a in enumerate((act_hi[j % AR], act_lo[j % AR])):
                        mm = nc.tensor.matmul(f_bank(t), a[:, t * P:(t + 1) * P], sign2[:, j, :],
                                              start=(j == 0 and n == 0), stop=(j == NJ - 1 and n == 1))
                if j == NJ - 1:
                    mm.then_inc(s["f_ps"], 1)

            def last_layer2(g):
                for j in range(NJ - LAG, NJ):
                    layer2(g, j)

            def prepare(j):
                pe.wait_ge(mag_done, j + 1)
                if j < NW:
                    past(pe, sum1_done, j - 1)
                    mm = nc.tensor.matmul(sum1_bank(j), ones[:, :], mag[j % 3][:, 0:WH], start=True, stop=True)
                else:
                    mm = nc.tensor.matmul(sum_bank, ones[:, :], mag[j % 3][:, :], start=(j == NW),
                                          stop=(j == 2 * NW - 1))
                mm.then_inc(added, 1)

            def one(n, u, front, ffn):
                g = n - 1

                def F(*js):
                    for j in js:
                        if not ffn:
                            for piece_nr in SUM_SLOTS.get(j, ()):
                                prepare(piece_nr)
                            continue
                        layer1(g, j)
                        if j >= LAG:
                            layer2(g, j - LAG)
                if front:
                    pe.wait_ge(s["at_done"], 2 * (n + 1))
                    for t in range(T):
                        rows = slice(t * P, (t + 1) * P)
                        run(g_bank(2 + t), [(a[:, k, rows], w[:, k, :]) for k in range(KC)
                                            for a, w in passes(at_hi, at_lo, *late["xWo"])]
                            ).then_inc(s["wo_ps"], 1)
                        if t == 0 and has_tail(n):
                            last_layer2(n - 2)
                elif has_tail(n):
                    last_layer2(n - 2)
                if ffn:
                    pe.wait_ge(s["x3T_lo_done"], T * (g + 1))
                F(0, 1, 2, 3, 4)
                if front:
                    transposes(n, s["norm2_done"], s["t2_ps"])
                F(5)
                if front:
                    pe.wait_ge(s["x2T_lo_done"], T * (n + 1))
                    for r in range(4):
                        hi, lo = late["sWq" if r < 2 else "sWk"]
                        for c in range(2):
                            m = 2 * (r % 2) + c
                            mm = run(chunks(g_bank(QK_BANK[r]), 2)[:, c, :],
                                     [(w[:, k, m * P:(m + 1) * P], xt[:, k, :]) for k in range(KC)
                                      for w, xt in passes(hi, lo, x2T_hi, x2T_lo)])
                        mm.then_inc(s["qk_ps"], 1)
                F(6, 7)
                if front:
                    pe.wait_ge(s["qk_lo_done"], 4 * (n + 1))
                    for t in range(T):
                        rows = slice(t * P, (t + 1) * P)
                        mm = run(sc_bank[:, t, :], [(q[:, m, rows], k[:, KC + m, rows]) for m in range(KC)
                                                    for q, k in passes(qk_hi, qk_lo, qk_hi, qk_lo)])
                    mm.then_inc(s["sc_ps"], 1)
                    for t in range(T):
                        rows = slice(t * P, (t + 1) * P)
                        run(g_bank(2 + t), [(xt[:, k, rows], w[:, k, :]) for k in range(KC)
                                            for xt, w in passes(x2T_hi, x2T_lo, *late["sWv"])]
                            ).then_inc(s["val_ps"], 1)
                F(8, 9, 10, 11)
                if front:
                    pe.wait_ge(s["w_done"], BPT * (n + 1))
                    pe.wait_ge(s["val_lo_done"], T * (n + 1))
                    for t in range(T):
                        run(g_bank(2 + t), [(w[:, t, :], v[:, t, :]) for w, v in
                                            passes(w_hi, w_lo, val_hi, val_lo)]).then_inc(s["pv_ps"], 1)
                F(12, 13, 14, 15)
                if front:
                    transposes(n, s["norm3_done"], s["t3_ps"])
                if not ffn:
                    pe.wait_ge(alpha1_done, 1)
                    pe.wait_ge(alpha2_done, 1)
            rounds(pe, one)
            last_layer2(NG - 1)


def kernel(x, ctx_1024, L0_xattn_Wq, L0_xattn_Wk, L0_xattn_Wv, L0_xattn_Wo, L0_xattn_bo, L0_attn_Wq,
           L0_attn_bq, L0_attn_Wk, L0_attn_bk, L0_attn_Wv, L0_attn_bv, L0_ffn_w1, L0_ffn_b1, L0_ffn_w2,
           L0_ffn_b2):
    import numpy as np
    import concourse.bacc as bacc
    from concourse.bass_utils import run_bass_kernel_spmd

    B, L, D = x.shape
    S = ctx_1024.shape[1] - 1
    ctx_t = np.asarray(ctx_1024).transpose(0, 2, 1).reshape(B, D // P, P, S + 1).transpose(0, 2, 1, 3)

    def columns(b):
        return np.asarray(b).reshape(-1, P).T

    def rows(w):
        return np.asarray(w).reshape(-1, P, D).transpose(1, 0, 2).reshape(P, -1)

    arrays = dict(
        x=np.asarray(x).reshape(B * L, D), ctx_main=ctx_t[..., :S],
        ctx_last=ctx_t[..., S].transpose(1, 2, 0), xWq=L0_xattn_Wq, xWk=L0_xattn_Wk, xWv=L0_xattn_Wv,
        late_w=np.stack([rows(L0_xattn_Wo), rows(L0_attn_Wq), rows(L0_attn_Wk), rows(L0_attn_Wv)]),
        bo=np.asarray(L0_xattn_bo)[None], bq=columns(L0_attn_bq), bk=columns(L0_attn_bk),
        bv=np.asarray(L0_attn_bv)[None], w1_t=np.asarray(L0_ffn_w1).T,
        b1=columns(L0_ffn_b1), w2_t=np.asarray(L0_ffn_w2).T, b2=np.asarray(L0_ffn_b2)[None])
    arrays = {name: np.ascontiguousarray(a) for name, a in arrays.items()}

    nc = bacc.Bacc("TRN2", target_bir_lowering=False, num_devices=1)
    args = {name: nc.dram_tensor(f"in_{name}", a.shape, mybir.dt.from_np(a.dtype), kind="ExternalInput").ap()
            for name, a in arrays.items()}
    v_last_rows = nc.dram_tensor("v_last_rows", (B, D), F32, kind="Internal").ap()
    out = nc.dram_tensor("out", (B * L, D), F32, kind="ExternalOutput").ap()
    perceiver_block(nc, v_last_rows=v_last_rows, out=out, **args)
    got = run_bass_kernel_spmd(nc, [{f"in_{name}": a for name, a in arrays.items()}], core_ids=[0])
    return got.results[0]["out"].reshape(B, L, D)
```
